# Optimizing a Trainium2 kernel written in Bass

```python
import numpy as np
import jax
import jax.numpy as jnp

def _softmax(x, axis=-1):
    return jax.nn.softmax(x, axis=axis)
def _gelu(x):
    return jax.nn.gelu(x, approximate=True)
def _silu(x):
    return jax.nn.silu(x)
def _sigmoid(x):
    return jax.nn.sigmoid(x)
def _layernorm(x, axis=-1, eps=1e-5):
    m = jnp.mean(x, axis=axis, keepdims=True)
    v = jnp.var(x, axis=axis, keepdims=True)
    return (x - m) / jnp.sqrt(v + eps)
def _scatter_add(tgt, idx, src, axis=0):
    return tgt.at[idx].add(src)
def _segment_sum(src, seg, n):
    return jax.ops.segment_sum(src, seg, n)

kernel_name = 'mk_conv_attn_hybrid_d2_conv_nchw256_fb07f7'

def setup_inputs(seed: int = 0):
    np.random.seed(seed)
    _w = jnp.asarray
    def _rec_inputs():
        import jax
        import jax.numpy as jnp
        _gk = jax.random.key(seed)
        x = -0.0009438 + 1 * jax.random.normal(jax.random.fold_in(_gk, 1), (2, 256, 48, 48), jnp.float32)
        return x
    x = _rec_inputs()
    def _L0_conv_setup():
        import math
        import jax, jax.numpy as jnp
        import numpy as np
        NUM_HEADS = 8
        DEPTH = 1
        LAMBDA_INIT = 0.8 - 0.6 * math.exp(-0.3 * DEPTH)
        EPS = 1e-05
        key = jax.random.key(seed)
        ks = jax.random.split(key, 10)
        B, C, H, W = (2, 256, 48, 48)
        hd = C // NUM_HEADS
        return {'x': jax.random.normal(ks[0], (B, C, H, W), jnp.float32), 'q_w': jax.random.normal(ks[1], (2 * C, C), jnp.float32) * C ** (-0.5), 'k_w': jax.random.normal(ks[2], (2 * C, C), jnp.float32) * C ** (-0.5), 'v_w': jax.random.normal(ks[3], (2 * C, C), jnp.float32) * C ** (-0.5), 'out_w': jax.random.normal(ks[4], (C, 2 * C), jnp.float32) * (2 * C) ** (-0.5), 'lambda_q1': 0.1 * jax.random.normal(ks[5], (NUM_HEADS, hd), jnp.float32), 'lambda_k1': 0.1 * jax.random.normal(ks[6], (NUM_HEADS, hd), jnp.float32), 'lambda_q2': 0.1 * jax.random.normal(ks[7], (NUM_HEADS, hd), jnp.float32), 'lambda_k2': 0.1 * jax.random.normal(ks[8], (NUM_HEADS, hd), jnp.float32), 'rms_scale': jnp.ones((1, 1, 2 * hd), jnp.float32)}
    _L0_conv_all = _L0_conv_setup()
    _L0_conv_in = {k: v for k, v in _L0_conv_all.items() if k in ('q_w', 'k_w', 'v_w', 'out_w', 'lambda_q1', 'lambda_k1', 'lambda_q2', 'lambda_k2', 'rms_scale', )}
    del _L0_conv_all

    def _L1_attn_setup():
        import jax, jax.numpy as jnp
        import numpy as np
        NUM_HEADS = 4
        D_MODEL = 256
        D_HEAD = D_MODEL // NUM_HEADS
        EPS_REC = 1e-06
        LN_EPS = 1e-05

        def layer_norm(x, g, b):
            m = jnp.mean(x, axis=-1, keepdims=True)
            v = jnp.mean(jnp.square(x - m), axis=-1, keepdims=True)
            return (x - m) * jax.lax.rsqrt(v + LN_EPS) * g + b

        def linear_recurrence(x, rq_w, rq_b, rk_w, rk_b, rv_w, rv_b, ro_w, ro_b):
            B, T, D = x.shape
            fmap = lambda z: jax.nn.elu(z) + 1.0
            Q = fmap((x @ rq_w + rq_b).reshape(B, T, NUM_HEADS, D_HEAD))
            K = fmap((x @ rk_w + rk_b).reshape(B, T, NUM_HEADS, D_HEAD))
            V = (x @ rv_w + rv_b).reshape(B, T, NUM_HEADS, D_HEAD)
            KV = jnp.einsum('bthd,bthm->bthdm', K, V)
            S = jnp.cumsum(KV, axis=1)
            Z = jnp.cumsum(K, axis=1)
            out = jnp.einsum('bthd,bthdm->bthm', Q, S)
            denom = jnp.einsum('bthd,bthd->bth', Q, Z)[..., None] + EPS_REC
            out = (out / denom).reshape(B, T, D)
            return out @ ro_w + ro_b
        key = jax.random.key(seed)
        ks = jax.random.split(key, 16)
        s = 0.02
        d, h = (D_MODEL, 4 * D_MODEL)
        inp = {'x': jax.random.normal(ks[0], (4, 2048, d), dtype=jnp.float32), 'qkv_w': jax.random.normal(ks[1], (d, 3 * d), dtype=jnp.float32) * s, 'qkv_b': jnp.zeros((3 * d,), jnp.float32), 'o_w': jax.random.normal(ks[2], (d, d), dtype=jnp.float32) * s, 'o_b': jnp.zeros((d,), jnp.float32), 'ffn_w1': jax.random.normal(ks[3], (d, h), dtype=jnp.float32) * s, 'ffn_b1': jnp.zeros((h,), jnp.float32), 'ffn_w2': jax.random.normal(ks[4], (h, d), dtype=jnp.float32) * s, 'ffn_b2': jnp.zeros((d,), jnp.float32), 'rq_w': jax.random.normal(ks[5], (d, d), dtype=jnp.float32) * s, 'rq_b': jnp.zeros((d,), jnp.float32), 'rk_w': jax.random.normal(ks[6], (d, d), dtype=jnp.float32) * s, 'rk_b': jnp.zeros((d,), jnp.float32), 'rv_w': jax.random.normal(ks[7], (d, d), dtype=jnp.float32) * s, 'rv_b': jnp.zeros((d,), jnp.float32), 'ro_w': jax.random.normal(ks[8], (d, d), dtype=jnp.float32) * s, 'ro_b': jnp.zeros((d,), jnp.float32), 'cg_w': jax.random.normal(ks[9], (2 * d, d), dtype=jnp.float32) * s, 'cg_b': jnp.zeros((d,), jnp.float32), 'ln1_g': jnp.ones((d,), jnp.float32), 'ln1_b': jnp.zeros((d,), jnp.float32), 'ln2_g': jnp.ones((d,), jnp.float32), 'ln2_b': jnp.zeros((d,), jnp.float32), 'ln3_g': jnp.ones((d,), jnp.float32), 'ln3_b': jnp.zeros((d,), jnp.float32)}
        return inp
    _L1_attn_all = _L1_attn_setup()
    _L1_attn_in = {k: v for k, v in _L1_attn_all.items() if k in ('qkv_w', 'qkv_b', 'o_w', 'o_b', 'ffn_w1', 'ffn_b1', 'ffn_w2', 'ffn_b2', 'rq_w', 'rq_b', 'rk_w', 'rk_b', 'rv_w', 'rv_b', 'ro_w', 'ro_b', 'cg_w', 'cg_b', 'ln1_g', 'ln1_b', 'ln2_g', 'ln2_b', 'ln3_g', 'ln3_b', )}
    del _L1_attn_all

    def _L1_ffn_setup():
        import jax, jax.numpy as jnp
        import numpy as np
        B, S, D = (8, 4096, 256)
        H = 4 * D
        CAPACITY = 0.5
        key = jax.random.key(seed)
        ks = jax.random.split(key, 6)
        x = jax.random.normal(ks[0], (B, S, D), dtype=jnp.float32)
        attention_mask = jnp.zeros((B, 1, 1, S), dtype=jnp.float32)
        wr = jax.random.normal(ks[1], (D, 1), dtype=jnp.float32) * 0.02
        br = jnp.zeros((1,), dtype=jnp.float32)
        w1 = jax.random.normal(ks[2], (D, H), dtype=jnp.float32) * 0.02
        b1 = jnp.zeros((H,), dtype=jnp.float32)
        w2 = jax.random.normal(ks[3], (H, D), dtype=jnp.float32) * 0.02
        b2 = jnp.zeros((D,), dtype=jnp.float32)
        return {'x': x, 'attention_mask': attention_mask, 'wr': wr, 'br': br, 'w1': w1, 'b1': b1, 'w2': w2, 'b2': b2}
    _L1_ffn_all = _L1_ffn_setup()
    _L1_ffn_in = {k: v for k, v in _L1_ffn_all.items() if k in ('attention_mask', 'wr', 'br', 'w1', 'b1', 'w2', 'b2', )}
    del _L1_ffn_all

    return {
        "x": x,
        "L0_conv_q_w": _L0_conv_in["q_w"],
        "L0_conv_k_w": _L0_conv_in["k_w"],
        "L0_conv_v_w": _L0_conv_in["v_w"],
        "L0_conv_out_w": _L0_conv_in["out_w"],
        "L0_conv_lambda_q1": _L0_conv_in["lambda_q1"],
        "L0_conv_lambda_k1": _L0_conv_in["lambda_k1"],
        "L0_conv_lambda_q2": _L0_conv_in["lambda_q2"],
        "L0_conv_lambda_k2": _L0_conv_in["lambda_k2"],
        "L0_conv_rms_scale": _L0_conv_in["rms_scale"],
        "L1_attn_qkv_w": _L1_attn_in["qkv_w"],
        "L1_attn_qkv_b": _L1_attn_in["qkv_b"],
        "L1_attn_o_w": _L1_attn_in["o_w"],
        "L1_attn_o_b": _L1_attn_in["o_b"],
        "L1_attn_ffn_w1": _L1_attn_in["ffn_w1"],
        "L1_attn_ffn_b1": _L1_attn_in["ffn_b1"],
        "L1_attn_ffn_w2": _L1_attn_in["ffn_w2"],
        "L1_attn_ffn_b2": _L1_attn_in["ffn_b2"],
        "L1_attn_rq_w": _L1_attn_in["rq_w"],
        "L1_attn_rq_b": _L1_attn_in["rq_b"],
        "L1_attn_rk_w": _L1_attn_in["rk_w"],
        "L1_attn_rk_b": _L1_attn_in["rk_b"],
        "L1_attn_rv_w": _L1_attn_in["rv_w"],
        "L1_attn_rv_b": _L1_attn_in["rv_b"],
        "L1_attn_ro_w": _L1_attn_in["ro_w"],
        "L1_attn_ro_b": _L1_attn_in["ro_b"],
        "L1_attn_cg_w": _L1_attn_in["cg_w"],
        "L1_attn_cg_b": _L1_attn_in["cg_b"],
        "L1_attn_ln1_g": _L1_attn_in["ln1_g"],
        "L1_attn_ln1_b": _L1_attn_in["ln1_b"],
        "L1_attn_ln2_g": _L1_attn_in["ln2_g"],
        "L1_attn_ln2_b": _L1_attn_in["ln2_b"],
        "L1_attn_ln3_g": _L1_attn_in["ln3_g"],
        "L1_attn_ln3_b": _L1_attn_in["ln3_b"],
        "L1_ffn_attention_mask": _L1_ffn_in["attention_mask"],
        "L1_ffn_wr": _L1_ffn_in["wr"],
        "L1_ffn_br": _L1_ffn_in["br"],
        "L1_ffn_w1": _L1_ffn_in["w1"],
        "L1_ffn_b1": _L1_ffn_in["b1"],
        "L1_ffn_w2": _L1_ffn_in["w2"],
        "L1_ffn_b2": _L1_ffn_in["b2"],
    }

def reference(x, L0_conv_q_w, L0_conv_k_w, L0_conv_v_w, L0_conv_out_w, L0_conv_lambda_q1, L0_conv_lambda_k1, L0_conv_lambda_q2, L0_conv_lambda_k2, L0_conv_rms_scale, L1_attn_qkv_w, L1_attn_qkv_b, L1_attn_o_w, L1_attn_o_b, L1_attn_ffn_w1, L1_attn_ffn_b1, L1_attn_ffn_w2, L1_attn_ffn_b2, L1_attn_rq_w, L1_attn_rq_b, L1_attn_rk_w, L1_attn_rk_b, L1_attn_rv_w, L1_attn_rv_b, L1_attn_ro_w, L1_attn_ro_b, L1_attn_cg_w, L1_attn_cg_b, L1_attn_ln1_g, L1_attn_ln1_b, L1_attn_ln2_g, L1_attn_ln2_b, L1_attn_ln3_g, L1_attn_ln3_b, L1_ffn_attention_mask, L1_ffn_wr, L1_ffn_br, L1_ffn_w1, L1_ffn_b1, L1_ffn_w2, L1_ffn_b2):
    import jax
    import jax.numpy as jnp
    def _L0_conv_ref(x, q_w, k_w, v_w, out_w, lambda_q1, lambda_k1, lambda_q2, lambda_k2, rms_scale):
        import math
        import jax, jax.numpy as jnp
        import numpy as np
        NUM_HEADS = 8
        DEPTH = 1
        LAMBDA_INIT = 0.8 - 0.6 * math.exp(-0.3 * DEPTH)
        EPS = 1e-05
        B, C, H, W = x.shape
        nh = NUM_HEADS
        hd = C // nh
        N = H * W
        xf = x.reshape(B, C, N)

        def proj(w):
            t = jnp.einsum('oc,bcn->bon', w, xf)
            return t.reshape(B, nh, 2 * hd, N).transpose(0, 1, 3, 2)
        Q = proj(q_w)
        K = proj(k_w)
        V = proj(v_w)
        Q1, Q2 = (Q[..., :hd], Q[..., hd:])
        K1, K2 = (K[..., :hd], K[..., hd:])
        scale = hd ** (-0.5)
        attn1 = jax.nn.softmax(jnp.einsum('bhnd,bhmd->bhnm', Q1, K1) * scale, axis=-1)
        attn2 = jax.nn.softmax(jnp.einsum('bhnd,bhmd->bhnm', Q2, K2) * scale, axis=-1)
        lam1 = jnp.exp(jnp.sum(lambda_q1 * lambda_k1, axis=-1))
        lam2 = jnp.exp(jnp.sum(lambda_q2 * lambda_k2, axis=-1))
        lam = (lam1 - lam2 + LAMBDA_INIT)[None, :, None, None]
        out = jnp.einsum('bhnm,bhmd->bhnd', attn1 - lam * attn2, V)
        rms = jnp.sqrt(jnp.mean(out * out, axis=-1, keepdims=True) + EPS)
        out = out / rms * rms_scale.reshape(1, 1, 1, 2 * hd)
        out = out * (1.0 - LAMBDA_INIT)
        out = out.transpose(0, 1, 3, 2).reshape(B, 2 * C, N)
        y = jnp.einsum('oc,bcn->bon', out_w, out)
        return y.reshape(B, C, H, W)

    def _L1_attn_ref(x, qkv_w, qkv_b, o_w, o_b, ffn_w1, ffn_b1, ffn_w2, ffn_b2, rq_w, rq_b, rk_w, rk_b, rv_w, rv_b, ro_w, ro_b, cg_w, cg_b, ln1_g, ln1_b, ln2_g, ln2_b, ln3_g, ln3_b):
        import jax, jax.numpy as jnp
        import numpy as np
        NUM_HEADS = 4
        D_MODEL = 256
        D_HEAD = D_MODEL // NUM_HEADS
        EPS_REC = 1e-06
        LN_EPS = 1e-05

        def layer_norm(x, g, b):
            m = jnp.mean(x, axis=-1, keepdims=True)
            v = jnp.mean(jnp.square(x - m), axis=-1, keepdims=True)
            return (x - m) * jax.lax.rsqrt(v + LN_EPS) * g + b

        def linear_recurrence(x, rq_w, rq_b, rk_w, rk_b, rv_w, rv_b, ro_w, ro_b):
            B, T, D = x.shape
            fmap = lambda z: jax.nn.elu(z) + 1.0
            Q = fmap((x @ rq_w + rq_b).reshape(B, T, NUM_HEADS, D_HEAD))
            K = fmap((x @ rk_w + rk_b).reshape(B, T, NUM_HEADS, D_HEAD))
            V = (x @ rv_w + rv_b).reshape(B, T, NUM_HEADS, D_HEAD)
            KV = jnp.einsum('bthd,bthm->bthdm', K, V)
            S = jnp.cumsum(KV, axis=1)
            Z = jnp.cumsum(K, axis=1)
            out = jnp.einsum('bthd,bthdm->bthm', Q, S)
            denom = jnp.einsum('bthd,bthd->bth', Q, Z)[..., None] + EPS_REC
            out = (out / denom).reshape(B, T, D)
            return out @ ro_w + ro_b
        B, T, D = x.shape
        qkv = x @ qkv_w + qkv_b
        q, k, v = jnp.split(qkv, 3, axis=-1)
        q = q.reshape(B, T, NUM_HEADS, D_HEAD)
        k = k.reshape(B, T, NUM_HEADS, D_HEAD)
        v = v.reshape(B, T, NUM_HEADS, D_HEAD)
        scale = 1.0 / np.sqrt(D_HEAD)
        logits = jnp.einsum('bqhd,bkhd->bhqk', q, k) * scale
        causal = jnp.tril(jnp.ones((T, T), dtype=bool))
        logits = jnp.where(causal, logits, jnp.finfo(logits.dtype).min)
        attn = jax.nn.softmax(logits, axis=-1)
        attn_out = jnp.einsum('bhqk,bkhd->bqhd', attn, v).reshape(B, T, D)
        attn_out = attn_out @ o_w + o_b
        parallel_repr = layer_norm(x + attn_out, ln1_g, ln1_b)
        seq = linear_recurrence(parallel_repr, rq_w, rq_b, rk_w, rk_b, rv_w, rv_b, ro_w, ro_b)
        seq_repr = layer_norm(parallel_repr + seq, ln2_g, ln2_b)
        combined = jnp.concatenate([parallel_repr, seq_repr], axis=-1)
        gate = jax.nn.sigmoid(combined @ cg_w + cg_b)
        merged = gate * parallel_repr + (1.0 - gate) * seq_repr
        ffn = jax.nn.gelu(merged @ ffn_w1 + ffn_b1, approximate=False) @ ffn_w2 + ffn_b2
        return layer_norm(merged + ffn, ln3_g, ln3_b)

    def _L1_ffn_ref(x, attention_mask, wr, br, w1, b1, w2, b2):
        import jax, jax.numpy as jnp
        import numpy as np
        B, S, D = (8, 4096, 256)
        H = 4 * D
        CAPACITY = 0.5
        b, s, d = x.shape
        weights = (jnp.einsum('bsd,do->bso', x, wr) + br)[..., 0]
        k = max(1, int(CAPACITY * s))
        kk = k - 1 if k > 1 else 1
        _, idx = jax.lax.top_k(weights, k)
        sel_idx = idx[:, :kk]
        sel = jnp.take_along_axis(x, sel_idx[:, :, None], axis=1)
        h = jax.nn.gelu(jnp.einsum('bkd,dh->bkh', sel, w1) + b1)
        y = jnp.einsum('bkh,hd->bkd', h, w2) + b2
        w_sel = jnp.take_along_axis(weights, sel_idx, axis=1)
        y = y * w_sel[..., None]
        batch_idx = jnp.arange(b)[:, None]
        processed = jnp.zeros_like(x).at[batch_idx, sel_idx].set(y)
        return processed + x

    def _gn(v, G=32, eps=1e-5):
        B_, C_, H_, W_ = v.shape
        g = v.reshape(B_, G, C_ // G, H_, W_)
        m = jnp.mean(g, axis=(2, 3, 4), keepdims=True)
        s = jnp.var(g, axis=(2, 3, 4), keepdims=True)
        return ((g - m) / jnp.sqrt(s + eps)).reshape(v.shape)

    def _ln_c(v, eps=1e-6):
        m = jnp.mean(v, axis=1, keepdims=True)
        s = jnp.var(v, axis=1, keepdims=True)
        return (v - m) / jnp.sqrt(s + eps)

    def _ln_t(v, eps=1e-5):
        m = jnp.mean(v, axis=-1, keepdims=True)
        s = jnp.var(v, axis=-1, keepdims=True)
        return (v - m) / jnp.sqrt(s + eps)

    def _to_tokens(v):
        B_, C_, H_, W_ = v.shape
        return v.reshape(B_, C_, H_ * W_).transpose(0, 2, 1)
    def _from_tokens(t, like):
        B_, C_, H_, W_ = like.shape
        return t.transpose(0, 2, 1).reshape(B_, C_, H_, W_)

    x = x + _L0_conv_ref(_gn(x), L0_conv_q_w, L0_conv_k_w, L0_conv_v_w, L0_conv_out_w, L0_conv_lambda_q1, L0_conv_lambda_k1, L0_conv_lambda_q2, L0_conv_lambda_k2, L0_conv_rms_scale)
    t = _to_tokens(x)
    t = t + _L1_attn_ref(_ln_t(t), L1_attn_qkv_w, L1_attn_qkv_b, L1_attn_o_w, L1_attn_o_b, L1_attn_ffn_w1, L1_attn_ffn_b1, L1_attn_ffn_w2, L1_attn_ffn_b2, L1_attn_rq_w, L1_attn_rq_b, L1_attn_rk_w, L1_attn_rk_b, L1_attn_rv_w, L1_attn_rv_b, L1_attn_ro_w, L1_attn_ro_b, L1_attn_cg_w, L1_attn_cg_b, L1_attn_ln1_g, L1_attn_ln1_b, L1_attn_ln2_g, L1_attn_ln2_b, L1_attn_ln3_g, L1_attn_ln3_b)
    t = t + _L1_ffn_ref(_ln_t(t), L1_ffn_attention_mask, L1_ffn_wr, L1_ffn_br, L1_ffn_w1, L1_ffn_b1, L1_ffn_w2, L1_ffn_b2)
    x = _from_tokens(t, x)
    return x


_drawn_inputs = setup_inputs


def setup_inputs(seed=0):
    import zlib

    import numpy as np

    out = dict(_drawn_inputs(seed))
    spreads = {'L0_conv_rms_scale': (1.0, 0.2),
     'L1_attn_qkv_b': (0.0, 0.449),
     'L1_attn_o_b': (0.0, 0.1),
     'L1_attn_ffn_b1': (0.0, 0.526),
     'L1_attn_ffn_b2': (0.0, 0.1),
     'L1_attn_rq_b': (0.0, 2.0),
     'L1_attn_rk_b': (0.0, 2.0),
     'L1_attn_rv_b': (0.0, 0.8),
     'L1_attn_ro_b': (0.0, 0.343),
     'L1_attn_cg_b': (0.0, 0.8),
     'L1_attn_ln1_g': (1.0, 0.2),
     'L1_attn_ln1_b': (0.0, 0.1),
     'L1_attn_ln2_g': (1.0, 0.2),
     'L1_attn_ln2_b': (0.0, 0.345),
     'L1_attn_ln3_g': (1.0, 0.2),
     'L1_attn_ln3_b': (0.0, 0.1),
     'L1_ffn_b1': (0.0, 0.8),
     'L1_ffn_b2': (0.0, 0.8)}
    factors = {'L1_attn_qkv_w': 8.0,
     'L1_attn_o_w': 3.014,
     'L1_attn_rq_w': 62.662,
     'L1_attn_rk_w': 8.0,
     'L1_attn_rv_w': 8.0,
     'L1_attn_ro_w': 6.788,
     'L1_attn_cg_w': 4.573,
     'L1_ffn_wr': 5.93,
     'L1_ffn_w1': 6.687,
     'L1_ffn_w2': 6.271}
    for name, (base, spread) in spreads.items():
        noise = np.random.default_rng([zlib.crc32(name.encode()), seed]).standard_normal(out[name].shape)
        drawn = base * np.exp(spread * noise) if base else spread * noise
        out[name] = jnp.asarray(drawn.astype(out[name].dtype))
    for name, factor in factors.items():
        out[name] = (out[name] * factor).astype(out[name].dtype)
    return out
```

```python
import math
from contextlib import ExitStack

import concourse.bass as bass
from concourse import mybir

F32 = mybir.dt.float32
F32R = mybir.dt.float32r
BF16 = mybir.dt.bfloat16
ALU = mybir.AluOpType
ACT = mybir.ActivationFunctionType
AX = mybir.AxisListType

P = 128
B = 2
C = 256
KC = C // P
N = 48 * 48
T = 384
NC = N // T
SUB = T // P
NT = N // P
H0 = 8
HD = 32
VD = 2 * HD
GN_EPS = 1e-5
LN_EPS = 1e-5
EPS_REC = 1e-6
GN_STEPS = 6
LAMBDA_INIT = 0.8 - 0.6 * math.exp(-0.3)


class Chain:

    def __init__(self, eng, sem, base=0):
        self.eng, self.sem, self.base, self.n = eng, sem, base, 0

    def link(self, ins, pad=None):
        self.n += 1
        ins.then_inc(self.sem, 1)
        self.eng.wait_ge(self.sem, self.base + self.n)
        if pad is not None:
            self.eng.memset(pad[:], 0.0)


def tools(nc, ctx, tag):
    def sb(name, shape, dt=F32):
        return ctx.enter_context(nc.sbuf_tensor(f"{tag}_{name}", shape, dt))

    def ps(name, shape):
        return ctx.enter_context(nc.psum_tensor(f"{tag}_{name}", shape, F32))

    used = []

    def sem(name):
        used.append(ctx.enter_context(nc.semaphore(f"{tag}_{name}")))
        return used[-1]

    def clear():
        with nc.Block() as block:
            @block.gpsimd
            def _(pool):
                for s in used:
                    pool.sem_clear(s)
    ctx.callback(clear)
    return sb, ps, sem


def norm_and_project(nc, x, wqk, wv, gmat, qk_hi, qk_lo, v_rows):
    MQK = 4 * C // P
    QB, VB = 4, 3
    with ExitStack() as ctx:
        sb, ps, sem = tools(nc, ctx, "proj")
        x_sb = sb("x", [P, KC, N])
        wqk_sb = sb("wqk", [P, KC, 4 * C])
        wv_sb = sb("wv", [P, KC, 2 * C])
        g_sb = sb("g", [P, P])
        stats = sb("stats", [P, KC, NC, 6])
        mv = sb("mv", [P, KC, 2])
        dev = sb("dev", [P, KC])
        dev2 = sb("dev2", [P, KC])
        spread = sb("spread", [P, KC])
        gmean = sb("gmean", [P, KC])
        std = sb("std", [P, KC])
        rstd = sb("rstd", [P, KC])
        shift = sb("shift", [P, KC])
        eps = sb("eps", [P, 1])
        pad = sb("pad", [P, 1])
        xn = [sb(f"xn{i}", [P, KC, T]) for i in range(2)]
        hi = [sb(f"hi{i}", [P, MQK, T], F32R) for i in range(2)]
        lo = [sb(f"lo{i}", [P, MQK, T], F32R) for i in range(2)]
        vst = [sb(f"vst{i}", [P, SUB, 2 * C]) for i in range(2)]
        qk_ps = [ps(f"qk{i}", [P, 512]) for i in range(QB)]
        v_ps = [ps(f"v{i}", [P, 512]) for i in range(VB)]
        gn_ps = ps("gn", [P, 512])
        s_w, s_x = sem("w"), sem("x_loaded")
        s_gn, s_mean, s_spread, s_gmean, s_gvar, s_std = (sem(n) for n in (
            "gn_step", "mean_ready", "spread_ready", "gmean_mm", "gvar_mm", "std_ready"))
        s_xn, s_qk, s_v = sem("xn_ready"), sem("qk_mm"), sem("v_mm")
        s_hi, s_lo, s_vst = sem("hi_done"), sem("lo_done"), sem("v_staged")
        s_out = [sem(f"stored{i}") for i in range(2)]
        s_eps = sem("eps")
        OUTS = 48

        with nc.Block() as block:
            @block.sync
            def _(sp):
                for i in range(2):
                    sp.sem_inc(s_out[i], 1)
                sp.dma_start(g_sb[:], gmat).then_inc(s_w, 16)
                sp.dma_start(wqk_sb[:], wqk).then_inc(s_w, 16)
                sp.dma_start(wv_sb[:], wv).then_inc(s_w, 16)
                with sp.Fori(0, B) as b:
                    sp.wait_ge(s_xn, b * NC * KC + 1)
                    sp.dma_start(x_sb[:], x.rearrange("b (k p) n -> p (b k) n", p=P)[
                        :, bass.ds(b * KC, KC), :]).then_inc(s_x, 16)
                    with sp.Fori(0, NC // 2) as i:
                        for par in range(2):
                            g = b * NC + i * 2 + par
                            cols = bass.ds((i * 2 + par) * T, T)
                            sp.wait_ge(s_lo, g * MQK + MQK + QB)
                            sp.dma_start(qk_hi.rearrange("b (m p) n -> p (b m) n", p=P)[
                                :, bass.ds(b * MQK, MQK), cols], hi[par][:].bitcast(F32)).then_inc(s_out[par], 16)
                            sp.dma_start(qk_lo.rearrange("b (m p) n -> p (b m) n", p=P)[
                                :, bass.ds(b * MQK, MQK), cols], lo[par][:].bitcast(F32)).then_inc(s_out[par], 16)
                            sp.wait_ge(s_vst, g * SUB + SUB + VB)
                            sp.dma_start(v_rows.rearrange("(t p) c -> p t c", p=P)[
                                :, bass.ds(g * SUB, SUB), :], vst[par][:]).then_inc(s_out[par], 16)
                for i in range(2):
                    sp.wait_ge(s_out[i], B * NC // 2 * OUTS + 1)

            @block.tensor
            def _(pe):
                pe.sem_inc(s_v, 2 * SUB)
                pe.wait_ge(s_w, 48)
                with pe.Fori(0, B) as b:
                    pe.wait_ge(s_mean, b + 1)
                    pe.matmul(gn_ps[:, 0:KC], g_sb[:], mv[:, :, 0], start=True, stop=True).then_inc(s_gmean, 1)
                    pe.wait_ge(s_spread, b + 1)
                    pe.matmul(gn_ps[:, KC:2 * KC], g_sb[:], spread[:], start=True, stop=True).then_inc(s_gvar, 1)
                    with pe.Fori(0, NC // 2) as i:
                        for par in range(2):
                            g = b * NC + i * 2 + par
                            pe.wait_ge(s_xn, (g + 1) * KC + 1)
                            for m in range(MQK):
                                pe.wait_ge(s_lo, g * MQK + m + 1)
                                for k in range(KC):
                                    mm = pe.matmul(qk_ps[m % QB][:, 0:T], wqk_sb[:, k, m * P:(m + 1) * P],
                                                   xn[par][:, k, :], start=k == 0, stop=k == KC - 1)
                                mm.then_inc(s_qk, 1)
                            for s in range(SUB):
                                pe.wait_ge(s_vst, g * SUB + s + 1)
                                for k in range(KC):
                                    mm = pe.matmul(v_ps[s][:, :], xn[par][:, k, s * P:(s + 1) * P],
                                                   wv_sb[:, k, :], start=k == 0, stop=k == KC - 1)
                                mm.then_inc(s_v, 1)

            @block.scalar
            def _(act):
                act.sem_inc(s_vst, VB)
                with act.Fori(0, B) as b:
                    act.wait_ge(s_gvar, b + 1)
                    act.wait_ge(s_eps, 1)
                    act.activation(std[:], gn_ps[:, KC:2 * KC], ACT.Sqrt, bias=eps[:, 0:1]).then_inc(s_std, 1)
                    with act.Fori(0, NC // 2) as i:
                        for par in range(2):
                            g = b * NC + i * 2 + par
                            act.wait_ge(s_out[par], (b * (NC // 2) + i) * OUTS + 1)
                            for m in range(MQK):
                                act.wait_ge(s_qk, g * MQK + m + 1)
                                act.activation(hi[par][:, m, :], qk_ps[m % QB][:, 0:T], ACT.Copy).then_inc(s_hi, 1)
                            for s in range(SUB):
                                act.wait_ge(s_v, g * SUB + s + 1 + 2 * SUB)
                                act.activation(vst[par][:, s, :], v_ps[s][:, :], ACT.Copy).then_inc(s_vst, 1)

            @block.vector
            def _(dve):
                dve.sem_inc(s_lo, QB)
                dve.sem_inc(s_xn, 1)
                dve.memset(eps[:], GN_EPS).then_inc(s_eps, 1)
                with dve.Fori(0, B) as b:
                    step = Chain(dve, s_gn, b * GN_STEPS)
                    dve.wait_ge(s_x, (b + 1) * 16)
                    for k in range(KC):
                        for c in range(NC):
                            ins = dve.bn_stats(stats[:, k, c, :], x_sb[:, k, c * T:(c + 1) * T])
                    step.link(ins, pad=pad)
                    for k in range(KC):
                        ins = dve.bn_aggr(mv[:, k, :], stats[:, k, :, :])
                    ins.then_inc(s_mean, 1)
                    dve.wait_ge(s_mean, b + 1)
                    dve.wait_ge(s_gmean, b + 1)
                    step.link(dve.tensor_copy(gmean[:], gn_ps[:, 0:KC]))
                    step.link(dve.tensor_tensor(dev[:], mv[:, :, 0], gmean[:], ALU.subtract))
                    step.link(dve.tensor_tensor(dev2[:], dev[:], dev[:], ALU.mult))
                    dve.tensor_tensor(spread[:], dev2[:], mv[:, :, 1], ALU.add).then_inc(s_spread, 1)
                    dve.wait_ge(s_std, b + 1)
                    step.link(dve.reciprocal(rstd[:], std[:]))
                    step.link(dve.scalar_tensor_tensor(out=shift[:], in0=gmean[:], scalar=-1.0, in1=rstd[:],
                                                       op0=ALU.mult, op1=ALU.mult), pad=pad)
                    assert step.n == GN_STEPS
                    with dve.Fori(0, NC // 2) as i:
                        for par in range(2):
                            c = i * 2 + par
                            g = b * NC + c
                            dve.wait_ge(s_v, g * SUB + SUB)
                            for k in range(KC):
                                dve.tensor_scalar(xn[par][:, k, :], x_sb[:, k, bass.ds(c * T, T)],
                                                  rstd[:, k:k + 1], shift[:, k:k + 1],
                                                  ALU.mult, ALU.add).then_inc(s_xn, 1)
                            for m in range(MQK):
                                dve.wait_ge(s_qk, g * MQK + m + 1)
                                dve.wait_ge(s_hi, g * MQK + m + 1)
                                dve.tensor_tensor(lo[par][:, m, :], qk_ps[m % QB][:, 0:T],
                                                  hi[par][:, m, :].bitcast(F32), ALU.subtract).then_inc(s_lo, 1)


def differential_attention(nc, qk_hi, qk_lo, v_rows, lambdas, ident, fold, o_rows):
    PARTS = 3
    ROWS = PARTS * HD
    HEADS = B * H0
    STEPS = NT
    BANKS = 3
    PBUF = 6
    LOADS = 2 * 2 * PARTS + 1
    UNITS = 2 * SUB * NC
    ROWS_STEP = STEPS - 2
    SUMS_STEP, COMBINE_STEP = 3, 9
    SCALE = HD ** -0.5
    on_dve = [g for g in range(STEPS) if g % 4 == 3]
    on_pool = [g for g in range(STEPS) if g not in on_dve]
    ND, NPOOL = len(on_dve) - 1, len(on_pool) - 1
    with ExitStack() as ctx:
        sb, ps, sem = tools(nc, ctx, "diff")
        ks = [[sb(f"ks{i}{j}", [ROWS + 1, N], F32R) for j in range(2)] for i in range(2)]
        qs = [[sb(f"qs{i}{j}", [ROWS + 1, N], F32R) for j in range(2)] for i in range(2)]
        vs = [sb(f"vs{i}", [P, NT, 2, VD]) for i in range(2)]
        q_now = sb("q_now", [ROWS, 2, T], F32R)
        probs = [sb(f"probs{i}", [P, 2 * T]) for i in range(PBUF)]
        run_pool = sb("run_pool", [P, 2 * T])
        sum_pool = sb("sum_pool", [P, 2 * T])
        run_dve = sb("run_dve", [P, 2 * T])
        sum_dve = sb("sum_dve", [P, 2 * T])
        maxes = sb("maxes", [P, 2 * SUB, NC])
        neg_max = sb("neg_max", [P, 2 * SUB])
        out_sb = sb("out", [P, T])
        recip = sb("recip", [P, T])
        normed = sb("normed", [P, T])
        combined = sb("combined", [VD, T])
        ones = sb("ones", [P, VD])
        ident_sb = sb("ident", [P, P])
        fold_sb = sb("fold", [P, VD])
        lam_in = sb("lam_in", [P, 4, C])
        lam_prod = sb("lam_prod", [P, 2, C])
        lam_sum = sb("lam_sum", [P, 2, H0])
        lam_exp = sb("lam_exp", [P, 2, H0])
        lam_diff = sb("lam_diff", [P, H0])
        neg_lam = sb("neg_lam", [P, HEADS])
        scores = [ps(f"scores{i}", [P, 512]) for i in range(BANKS)]
        max_ps = [ps(f"max{i}", [P, 512]) for i in range(BANKS)]
        out_ps = ps("out_ps", [P, 512])
        misc = ps("misc", [P, 512])
        s_const, s_ones, s_lam, s_lamexp, s_lamready = (sem(n) for n in (
            "const", "ones", "lam_step", "lam_exp", "lam_ready"))
        s_ld = [sem(f"loaded{i}") for i in range(2)]
        s_vs, s_qnow = sem("values_ready"), sem("q_now_ready")
        s_st, s_exp, s_pv, s_accp, s_accd = (sem(n) for n in (
            "scores_mm", "exp_done", "pv_mm", "sum_pool_done", "sum_dve_done"))
        s_mx, s_red, s_neg, s_rows, s_row = (sem(n) for n in (
            "max_mm", "max_taken", "neg_max_ready", "rows_mm", "rows_placed"))
        s_oev, s_l, s_rec, s_norm, s_comb, s_cout, s_st_o = (sem(n) for n in (
            "out_taken", "sums_mm", "recip_done", "normed_ready", "combined_mm", "combined_taken", "stored"))

        busy = [SUMS_STEP + 1 + s for s in range(SUB)] + [g + 1 for g in on_dve[1:]]
        per_step = [1 if g in busy else 3 for g in range(ROWS_STEP)]
        per_step[0] = per_step[COMBINE_STEP - 2] = 2
        assert sum(per_step) == UNITS

        def units_at(g):
            return list(range(sum(per_step[:g]), sum(per_step[:g + 1])))

        with nc.Block() as block:
            @block.sync
            def _(sp):
                sp.dma_start(ident_sb[:], ident).then_inc(s_const, 16)
                sp.dma_start(fold_sb[:], fold).then_inc(s_const, 16)
                for i, l in enumerate(lambdas):
                    sp.dma_start(lam_in[:, i, :], l.rearrange("h d -> (h d)").partition_broadcast(P)).then_inc(s_const, 16)

                qh = qk_hi.rearrange("b (h j d) n -> (b h) j d n", j=2, d=HD)
                ql = qk_lo.rearrange("b (h j d) n -> (b h) j d n", j=2, d=HD)

                def load(par, b, h):
                    for j in range(2):
                        for dst, kind, parts in ((qs, 0, (qh, qh, ql)), (ks, 1, (qh, ql, qh))):
                            for r, src in enumerate(parts):
                                sp.dma_start(dst[par][j][r * HD:(r + 1) * HD, :].bitcast(F32),
                                             src[bass.ds(b * 2 * H0 + kind * H0 + h, 1), j, :, :].rearrange(
                                                 "a d n -> (a d) n")).then_inc(s_ld[par], 16)
                    sp.dma_start(vs[par][:, :, 0, :], v_rows.rearrange("(t p) c -> p t c", p=P)[
                        :, bass.ds(b * NT, NT), bass.ds(h * VD, VD)]).then_inc(s_ld[par], 16)

                with sp.Fori(0, B) as b:
                    with sp.Fori(0, H0 // 2) as i:
                        for par in range(2):
                            sp.wait_ge(s_comb, (b * H0 + i * 2 + par) * NC + NC + 1)
                            load(par, b, i * 2 + par)
                sp.wait_ge(s_comb, HEADS * NC + NC + 1)
                load(0, 0, 0)
                sp.wait_ge(s_ld[0], (HEADS // 2 + 1) * LOADS * 16)
                sp.wait_ge(s_ld[1], HEADS // 2 * LOADS * 16)

            @block.tensor
            def _(pe):
                pe.sem_inc(s_comb, 2 * NC)
                pe.sem_inc(s_mx, 2 * UNITS)
                pe.sem_inc(s_st, 2 * STEPS)
                pe.sem_inc(s_pv, PBUF + STEPS)
                pe.sem_inc(s_rows, 1)
                pe.wait_ge(s_const, 16 * 6)
                pe.wait_ge(s_ones, 5)

                def score_step(par, q, c, g):
                    if g == 0:
                        pe.wait_ge(s_row, q * 2 + 2)
                    for j in range(2):
                        pe.wait_ge(s_exp, (q * STEPS + g) * 2 + j + 1)
                        pe.matmul(scores[(2 * g + j) % BANKS][:, 0:T], ks[par][j][:, g * P:(g + 1) * P],
                                  qs[par][j][:, bass.ds(c * T, T)], start=True, stop=True).then_inc(s_st, 1)

                def max_unit(par, q1, u):
                    j, s, k = u // (SUB * NC), u // NC % SUB, u % NC
                    if u % (SUB * NC) == 0:
                        pe.wait_ge(s_qnow, q1 * 2 + j + 1)
                    pe.wait_ge(s_red, q1 * UNITS + u + 1)
                    pe.matmul(max_ps[u % BANKS][:, 0:T], q_now[:, j, s * P:(s + 1) * P],
                              ks[par][j][0:ROWS, k * T:(k + 1) * T], start=True, stop=True).then_inc(s_mx, 1)

                def pv_step(par, q, g, n=None):
                    if g == 0 and n is not None:
                        pe.wait_ge(s_vs, n + 1)
                    if g == 0:
                        pe.wait_ge(s_oev, q)
                    pe.wait_ge(s_exp, (q * STEPS + g) * 2 + 2 + BANKS)
                    for j in range(2):
                        mm = pe.matmul(out_ps[64 * j:64 * j + VD, 0:T], vs[par][:, g, j, :],
                                       probs[g % PBUF][:, j * T:(j + 1) * T], start=g == 0, stop=g == STEPS - 1,
                                       tile_position=(0, 64 * j))
                    mm.then_inc(s_pv, 1)

                def rows(q1, first=False):
                    if not first:
                        pe.wait_ge(s_cout, q1 - 1)
                    pe.wait_ge(s_neg, q1 + 1)
                    for j in range(2):
                        for s in range(SUB):
                            mm = pe.matmul(misc[32 * j:32 * j + 1, s * P:(s + 1) * P],
                                           neg_max[:, j * SUB + s:j * SUB + s + 1], ident_sb[:],
                                           start=True, stop=True, tile_position=(0, 32 * j))
                    mm.then_inc(s_rows, 1)

                def sums(q):
                    pe.wait_ge(s_row, q * 2 + 4)
                    pe.wait_ge(s_accp, (q + 2) * NPOOL)
                    pe.wait_ge(s_accd, (q + 2) * ND)
                    for j in range(2):
                        for k, part in enumerate((sum_pool, sum_dve)):
                            mm = pe.matmul(misc[64 * j:64 * j + VD, 0:T], ones[:],
                                           part[:, j * T:(j + 1) * T], start=k == 0, stop=k == 1,
                                           tile_position=(0, 64 * j))
                    mm.then_inc(s_l, 1)

                def combine(q):
                    pe.wait_ge(s_norm, q + 2)
                    pe.matmul(misc[0:VD, 0:T], fold_sb[:], normed[:], start=True, stop=True).then_inc(s_comb, 1)

                def slot(par, q, c, next_par, n=None):
                    for g in range(STEPS):
                        units = units_at(g)
                        before, between = (units[:1], units[1:2]) if len(units) == 3 else ([], units[:1])
                        for u in before:
                            max_unit(next_par, q + 1, u)
                        score_step(par, q, c, g)
                        for u in between:
                            max_unit(next_par, q + 1, u)
                        if g > 0:
                            pv_step(par, q, g - 1, n)
                        for u in units[len(before + between):]:
                            max_unit(next_par, q + 1, u)
                        if g == SUMS_STEP:
                            sums(q - 1)
                        if g == COMBINE_STEP:
                            combine(q - 1)
                        if g == ROWS_STEP:
                            rows(q + 1)
                    pv_step(par, q, STEPS - 1)

                pe.wait_ge(s_ld[0], LOADS * 16)
                for u in range(UNITS):
                    max_unit(0, 1, u)
                rows(1, first=True)
                with pe.Fori(0, HEADS // 2) as i:
                    for par in range(2):
                        n = i * 2 + par
                        slot(par, n * NC + 1, 0, par, n)
                        with pe.Fori(1, NC - 1) as c:
                            slot(par, n * NC + c + 1, c, par)
                        pe.wait_ge(s_ld[1 - par], (i + 1 + par) * LOADS * 16)
                        slot(par, n * NC + NC, NC - 1, 1 - par)
                sums(HEADS * NC)
                combine(HEADS * NC)

            @block.scalar
            def _(act):
                act.sem_inc(s_exp, BANKS + 2 * STEPS)
                act.sem_inc(s_row, 2)
                act.sem_inc(s_qnow, 2)
                act.sem_inc(s_st_o, 1)

                def stage_queries(par, q1, c1, j):
                    act.wait_ge(s_mx, q1 * UNITS + (j + 1) * (UNITS // 2))
                    act.activation(q_now[:, j, :], qs[par][j][0:ROWS, bass.ds(c1 * T, T)].bitcast(F32),
                                   ACT.Copy).then_inc(s_qnow, 1)

                def place_rows(par, q1, c1):
                    act.wait_ge(s_rows, q1 + 1)
                    act.activation(qs[par][0][ROWS:ROWS + 1, bass.ds(c1 * T, T)], misc[0:1, 0:T],
                                   ACT.Copy).then_inc(s_row, 1)

                def take_out(q):
                    act.wait_ge(s_norm, q + 1)
                    act.wait_ge(s_pv, (q + 1) * STEPS + PBUF)
                    act.activation(out_sb[:], out_ps[:, 0:T], ACT.Copy).then_inc(s_oev, 1)

                def take_combined(q):
                    act.wait_ge(s_comb, q + 1 + 2 * NC)
                    act.wait_ge(s_st_o, q * 16 + 1)
                    act.activation(combined[:], misc[0:VD, 0:T], ACT.Copy).then_inc(s_cout, 1)

                def store_combined(q, n, c):
                    act.wait_ge(s_cout, q + 1)
                    act.dma_start(o_rows[:, bass.ds(n + 1, 1), bass.ds(c * T, T)], combined[:]).then_inc(s_st_o, 16)

                def slot(par, q, next_par, c1, n_prev, c_prev):
                    for g in range(STEPS):
                        if g == 0:
                            stage_queries(next_par, q + 1, c1, 0)
                        if UNITS // 2 - 1 in units_at(g):
                            stage_queries(next_par, q + 1, c1, 1)
                        act.wait_ge(s_pv, q * STEPS + g + 1)
                        back = (g - PBUF) % STEPS
                        lap = 1 if g >= PBUF else 0
                        if back in on_pool:
                            act.wait_ge(s_accp, (q + lap) * NPOOL + max(on_pool.index(back), 1))
                        else:
                            act.wait_ge(s_accd, (q + lap) * ND + max(on_dve.index(back), 1))
                        for j in range(2):
                            act.wait_ge(s_st, (q * STEPS + g) * 2 + j + 1)
                            act.activation(probs[g % PBUF][:, j * T:(j + 1) * T],
                                           scores[(2 * g + j) % BANKS][:, 0:T], ACT.Exp, scale=SCALE
                                           ).then_inc(s_exp, 1)
                        if g == 0:
                            take_out(q - 1)
                        if g == COMBINE_STEP + 1:
                            take_combined(q - 1)
                        if g == COMBINE_STEP + 2:
                            store_combined(q - 1, n_prev, c_prev)
                        if g == ROWS_STEP:
                            place_rows(next_par, q + 1, c1)

                act.wait_ge(s_lam, 2)
                act.activation(lam_exp[:], lam_sum[:], ACT.Exp).then_inc(s_lamexp, 1)
                act.wait_ge(s_ld[0], LOADS * 16)
                for j in range(2):
                    act.activation(q_now[:, j, :], qs[0][j][0:ROWS, 0:T].bitcast(F32), ACT.Copy).then_inc(s_qnow, 1)
                place_rows(0, 1, 0)
                with act.Fori(0, HEADS // 2) as i:
                    for par in range(2):
                        n = i * 2 + par
                        slot(par, n * NC + 1, par, 1, n - 1, NC - 1)
                        with act.Fori(1, NC - 1) as c:
                            slot(par, n * NC + c + 1, par, c + 1, n, c - 1)
                        act.wait_ge(s_ld[1 - par], (i + 1 + par) * LOADS * 16)
                        slot(par, n * NC + NC, 1 - par, 0, n, NC - 2)
                take_out(HEADS * NC)
                take_combined(HEADS * NC)
                store_combined(HEADS * NC, HEADS - 1, NC - 1)
                act.wait_ge(s_st_o, (HEADS * NC + 1) * 16 + 1)

            @block.vector
            def _(dve):
                dve.sem_inc(s_red, BANKS + UNITS)
                dve.sem_inc(s_neg, 1)
                dve.sem_inc(s_accd, 2 * ND)
                dve.sem_inc(s_norm, 1)
                for par in range(2):
                    for j in range(2):
                        ins = dve.memset(ks[par][j][ROWS:ROWS + 1, :].bitcast(F32), 1.0)
                ins.then_inc(s_ones, 1)
                dve.memset(ones[:], 1.0).then_inc(s_ones, 1)
                dve.memset(sum_dve[:], 1.0).then_inc(s_ones, 1)
                dve.memset(out_ps[:, 0:T], 0.0).then_inc(s_ones, 1)
                dve.wait_ge(s_const, 16 * 6)
                step = Chain(dve, s_lam)
                for i in range(2):
                    ins = dve.tensor_tensor(lam_prod[:, i, :], lam_in[:, 2 * i, :], lam_in[:, 2 * i + 1, :], ALU.mult)
                step.link(ins)
                step.link(dve.tensor_reduce(lam_sum[:], lam_prod[:].rearrange("p i (h d) -> p i h d", d=HD),
                                            AX.X, ALU.add))
                dve.wait_ge(s_lamexp, 1)
                step.link(dve.tensor_tensor(lam_diff[:], lam_exp[:, 1, :], lam_exp[:, 0, :], ALU.subtract))
                for b in range(B):
                    ins = dve.tensor_scalar(neg_lam[:, b * H0:(b + 1) * H0], lam_diff[:], -LAMBDA_INIT, None, ALU.add)
                step.link(ins)

                def max_unit(q1, u):
                    dve.wait_ge(s_mx, (q1 + 1) * UNITS + u + 1)
                    dve.tensor_reduce(maxes[:, u // NC:u // NC + 1, u % NC], max_ps[u % BANKS][:, 0:T], AX.X,
                                      ALU.max).then_inc(s_red, 1)

                def negate(q1):
                    dve.wait_ge(s_rows, q1)
                    dve.wait_ge(s_red, q1 * UNITS + UNITS + BANKS)
                    dve.tensor_reduce(neg_max[:], maxes[:], AX.X, ALU.max, negate=True).then_inc(s_neg, 1)

                def add_up(q, g):
                    i = on_dve.index(g)
                    if i == 0:
                        return
                    dve.wait_ge(s_exp, (q * STEPS + g) * 2 + 2 + BANKS)
                    dve.wait_ge(s_accd, (q + 1) * ND + i - 1)
                    acc = probs[on_dve[0] % PBUF] if i == 1 else run_dve
                    to = sum_dve if i == ND else run_dve
                    dve.tensor_tensor(to[:], acc[:], probs[g % PBUF][:], ALU.add).then_inc(s_accd, 1)

                def invert(q, s):
                    if s == 0:
                        dve.wait_ge(s_l, q + 1)
                        dve.wait_ge(s_norm, q + 1)
                    dve.reciprocal(recip[:, s * P:(s + 1) * P], misc[:, s * P:(s + 1) * P]).then_inc(s_rec, 1)

                def normalise(q):
                    dve.wait_ge(s_oev, q + 1)
                    dve.wait_ge(s_rec, (q + 1) * SUB)
                    dve.tensor_tensor(normed[:], out_sb[:], recip[:], ALU.mult).then_inc(s_norm, 1)

                def place_rows(par, q1, c1):
                    dve.wait_ge(s_rows, q1 + 1)
                    dve.tensor_copy(qs[par][1][ROWS:ROWS + 1, bass.ds(c1 * T, T)], misc[32:33, 0:T]
                                    ).then_inc(s_row, 1)

                def slot(q, next_par, c1):
                    for g in range(STEPS):
                        for u in units_at(g):
                            max_unit(q + 1, u)
                        if g - 1 in on_dve:
                            add_up(q, g - 1)
                        if 0 < g - SUMS_STEP <= SUB:
                            invert(q - 1, g - SUMS_STEP - 1)
                        if g == COMBINE_STEP - 2:
                            normalise(q - 1)
                        if g == ROWS_STEP - 1:
                            negate(q + 1)
                        if g == ROWS_STEP:
                            place_rows(next_par, q + 1, c1)

                for u in range(UNITS):
                    max_unit(1, u)
                negate(1)
                place_rows(0, 1, 0)
                with dve.Fori(0, HEADS // 2) as i:
                    for par in range(2):
                        n = i * 2 + par
                        dve.wait_ge(s_lam, 4)
                        dve.wait_ge(s_ld[par], (i + 1) * LOADS * 16)
                        dve.tensor_scalar(vs[par][:, :, 1, :], vs[par][:, :, 0, :], neg_lam[:, bass.ds(n, 1)],
                                          None, ALU.mult).then_inc(s_vs, 1)
                        with dve.Fori(1, NC) as c:
                            slot(n * NC + c, par, c)
                        slot(n * NC + NC, 1 - par, 0)
                for s in range(SUB):
                    invert(HEADS * NC, s)
                normalise(HEADS * NC)

            @block.gpsimd
            def _(pool):
                pool.sem_inc(s_accp, 2 * NPOOL)
                pool.memset(sum_pool[:], 1.0).then_inc(s_ones, 1)

                def slot(q):
                    for i, g in enumerate(on_pool):
                        if i == 0:
                            continue
                        pool.wait_ge(s_exp, (q * STEPS + g) * 2 + 2 + BANKS)
                        pool.wait_ge(s_accp, (q + 1) * NPOOL + i - 1)
                        acc = probs[on_pool[0] % PBUF] if i == 1 else run_pool
                        to = sum_pool if i == NPOOL else run_pool
                        pool.tensor_tensor(to[:], acc[:], probs[g % PBUF][:], ALU.add).then_inc(s_accp, 1)

                with pool.Fori(1, HEADS * NC + 1) as q:
                    slot(q)


def nth(c, lane):
    return c * B + lane + 1


def head_norm_and_layer1_inputs(nc, a, o_rows, t_rows, a_t, qk_hi, qk_lo, v_rows):
    MO = 2 * C // P
    MQK = 2 * C // P
    with ExitStack() as ctx:
        sb, ps, sem = tools(nc, ctx, "mid")
        L = range(B)
        wo = sb("wo", [P, MO, C])
        wqk = sb("wqk", [P, KC, 2 * C])
        wv = sb("wv", [P, KC, C])
        qk_bias = sb("qk_bias", [P, MQK])
        v_bias = sb("v_bias", [P, C])
        to_heads = sb("to_heads", [P, MO, H0])
        from_heads = sb("from_heads", [H0, MO, P])
        mean_mat = sb("mean_mat", [P, P])
        gain = sb("gain", [P, 1])
        eps = sb("eps", [P, 1])
        o_in = [sb(f"o_in{i}", [P, MO, T]) for i in L]
        x_in = [sb(f"x_in{i}", [P, KC, T]) for i in L]
        o_sq = [sb(f"o_sq{i}", [P, MO, T]) for i in L]
        h_std = [sb(f"h_std{i}", [H0, T]) for i in L]
        h_rstd = [sb(f"h_rstd{i}", [H0, T]) for i in L]
        o_norm = [sb(f"o_norm{i}", [P, MO, T]) for i in L]
        t = [sb(f"t{i}", [P, KC, T]) for i in L]
        dev = [sb(f"dev{i}", [P, KC, T]) for i in L]
        dev_sq = [sb(f"dev_sq{i}", [P, KC, T]) for i in L]
        std = [sb(f"std{i}", [P, T]) for i in L]
        rstd = [sb(f"rstd{i}", [P, T]) for i in L]
        ln = [sb(f"ln{i}", [P, KC, T]) for i in L]
        hi = [sb(f"hi{i}", [P, MQK, T], F32R) for i in L]
        lo = [sb(f"lo{i}", [P, MQK, T], F32R) for i in L]
        v_out = [sb(f"v_out{i}", [P, SUB, C]) for i in L]
        bank = [[ps(f"bank{i}{k}", [P, 512]) for k in range(4)] for i in L]
        s_w, s_eps, s_gain = sem("weights"), sem("eps"), sem("gain")
        s_ld = [sem(f"loaded{i}") for i in L]
        s_st_t = [sem(f"t_stored{i}") for i in L]
        s_st_q = [sem(f"qk_stored{i}") for i in L]
        s_st_v = [sem(f"v_stored{i}") for i in L]
        (s_osq, s_ms, s_hstd, s_hrstd, s_bc, s_onorm, s_y, s_t, s_mean, s_dev, s_dsq, s_var, s_std, s_rstd,
         s_ln, s_qk, s_hi, s_lo, s_v, s_vout) = (sem(n) for n in (
             "o_squared", "head_ms_mm", "head_std", "head_rstd", "head_rstd_mm", "o_normed", "y_mm", "t_ready",
             "mean_mm", "dev_ready", "dev_squared", "var_mm", "std_ready", "rstd_ready", "ln_ready", "qk_mm",
             "hi_done", "lo_done", "v_mm", "v_done"))

        with nc.Block() as block:
            @block.sync
            def _(sp):
                for i in L:
                    sp.sem_inc(s_st_t[i], 1)
                    sp.sem_inc(s_st_q[i], 1)
                    sp.sem_inc(s_st_v[i], 1)
                for dst, src in ((wo, a["out_w"]), (wqk, a["wqk1"]), (wv, a["wv1"]), (qk_bias, a["qk_bias1"]),
                                 (to_heads, a["to_heads"]), (from_heads, a["from_heads"]),
                                 (mean_mat, a["mean_mat"]), (gain, a["rms_scale"])):
                    sp.dma_start(dst[:], src).then_inc(s_w, 16)
                sp.dma_start(v_bias[:], a["v_bias1"].partition_broadcast(P)).then_inc(s_w, 16)
                with sp.Fori(0, NC) as c:
                    cols = bass.ds(c * T, T)
                    for i in L:
                        sp.wait_ge(s_t, nth(c, i))
                        for h in range(2):
                            sp.dma_start(o_in[i][h * VD:(h + 1) * VD, :, :],
                                         o_rows[:, bass.ds(1 + i * H0 + h, MO, step=2), cols]
                                         ).then_inc(s_ld[i], 16)
                        sp.dma_start(x_in[i][:], a["x"][i].rearrange("(k p) n -> p k n", p=P)[:, :, cols]
                                     ).then_inc(s_ld[i], 16)
                    for i in L:
                        sp.wait_ge(s_ln, nth(c, i))
                        sp.dma_start(t_rows[i].rearrange("(k p) n -> p k n", p=P)[:, :, cols], t[i][:]
                                     ).then_inc(s_st_t[i], 16)
                        sp.dma_start(a_t[i].rearrange("(k p) n -> p k n", p=P)[:, :, cols], ln[i][:]
                                     ).then_inc(s_st_t[i], 16)
                    for i in L:
                        sp.wait_ge(s_lo, nth(c, i) * MQK)
                        sp.dma_start(qk_hi[i].rearrange("(m p) n -> p m n", p=P)[:, :, cols],
                                     hi[i][:].bitcast(F32)).then_inc(s_st_q[i], 16)
                        sp.dma_start(qk_lo[i].rearrange("(m p) n -> p m n", p=P)[:, :, cols],
                                     lo[i][:].bitcast(F32)).then_inc(s_st_q[i], 16)
                    for i in L:
                        sp.wait_ge(s_vout, nth(c + 1, i))
                        sp.dma_start(v_rows[i].rearrange("(t p) c -> p t c", p=P)[:, bass.ds(c * SUB, SUB), :],
                                     v_out[i][:]).then_inc(s_st_v[i], 16)
                for i in L:
                    sp.wait_ge(s_st_t[i], NC * 32 + 1)
                    sp.wait_ge(s_st_q[i], NC * 32 + 1)
                    sp.wait_ge(s_st_v[i], NC * 16 + 1)

            @block.tensor
            def _(pe):
                pe.wait_ge(s_w, 16 * 9)
                with pe.Fori(0, NC) as c:
                    for i in L:
                        pe.wait_ge(s_osq, nth(c, i))
                        pe.wait_ge(s_vout, nth(c, i))
                        for m in range(MO):
                            mm = pe.matmul(bank[i][0][0:H0, 0:T], to_heads[:, m, :], o_sq[i][:, m, :],
                                           start=m == 0, stop=m == MO - 1)
                        mm.then_inc(s_ms, 1)
                    for i in L:
                        pe.wait_ge(s_hrstd, nth(c, i))
                        for m in range(MO):
                            mm = pe.matmul(bank[i][m][:, 0:T], from_heads[:, m, :], h_rstd[i][:],
                                           start=True, stop=True)
                        mm.then_inc(s_bc, 1)
                    for i in L:
                        pe.wait_ge(s_onorm, nth(c, i))
                        for h in range(KC):
                            for m in range(MO):
                                mm = pe.matmul(bank[i][h][:, 0:T], wo[:, m, h * P:(h + 1) * P],
                                               o_norm[i][:, m, :], start=m == 0, stop=m == MO - 1)
                        mm.then_inc(s_y, 1)
                    for i in L:
                        pe.wait_ge(s_t, nth(c + 1, i))
                        for k in range(KC):
                            mm = pe.matmul(bank[i][2][:, 0:T], mean_mat[:], t[i][:, k, :],
                                           start=k == 0, stop=k == KC - 1)
                        mm.then_inc(s_mean, 1)
                    for i in L:
                        pe.wait_ge(s_dsq, nth(c, i))
                        for k in range(KC):
                            mm = pe.matmul(bank[i][3][:, 0:T], mean_mat[:], dev_sq[i][:, k, :],
                                           start=k == 0, stop=k == KC - 1)
                        mm.then_inc(s_var, 1)
                    for i in L:
                        pe.wait_ge(s_ln, nth(c, i))
                        for m in range(MQK):
                            for k in range(KC):
                                mm = pe.matmul(bank[i][m][:, 0:T], wqk[:, k, m * P:(m + 1) * P], ln[i][:, k, :],
                                               start=k == 0, stop=k == KC - 1)
                            mm.then_inc(s_qk, 1)
                    for i in L:
                        pe.wait_ge(s_lo, nth(c, i) * MQK)
                        for s in range(SUB):
                            for k in range(KC):
                                mm = pe.matmul(bank[i][s][:, 0:C], ln[i][:, k, s * P:(s + 1) * P], wv[:, k, :],
                                               start=k == 0, stop=k == KC - 1)
                        mm.then_inc(s_v, 1)

            @block.scalar
            def _(act):
                act.wait_ge(s_eps, 1)
                act.wait_ge(s_w, 16 * 9)
                with act.Fori(0, NC) as c:
                    for i in L:
                        act.wait_ge(s_ld[i], (c + 1) * 48)
                        act.activation(o_sq[i][:], o_in[i][:], ACT.Square).then_inc(s_osq, 1)
                    for i in L:
                        act.wait_ge(s_ms, nth(c, i))
                        act.activation(h_std[i][:], bank[i][0][0:H0, 0:T], ACT.Sqrt,
                                       bias=eps[0:H0, 0:1]).then_inc(s_hstd, 1)
                    for i in L:
                        act.wait_ge(s_dev, nth(c, i))
                        act.activation(dev_sq[i][:], dev[i][:], ACT.Square).then_inc(s_dsq, 1)
                    for i in L:
                        act.wait_ge(s_var, nth(c, i))
                        act.activation(std[i][:], bank[i][3][:, 0:T], ACT.Sqrt, bias=eps[:, 0:1]).then_inc(s_std, 1)
                    for i in L:
                        act.wait_ge(s_st_q[i], c * 32 + 1)
                        for m in range(MQK):
                            act.wait_ge(s_qk, nth(c, i) * MQK - (MQK - 1) + m)
                            act.activation(hi[i][:, m, :], bank[i][m][:, 0:T], ACT.Identity,
                                           bias=qk_bias[:, m:m + 1]).then_inc(s_hi, 1)

            @block.vector
            def _(dve):
                dve.sem_inc(s_t, B)
                dve.sem_inc(s_vout, B)
                dve.memset(eps[:], LN_EPS).then_inc(s_eps, 1)
                dve.wait_ge(s_w, 16 * 9)
                dve.tensor_scalar(gain[:], gain[:], 1.0 - LAMBDA_INIT, None, ALU.mult).then_inc(s_gain, 1)
                dve.wait_ge(s_gain, 1)
                with dve.Fori(0, NC) as c:
                    for i in L:
                        dve.wait_ge(s_hstd, nth(c, i))
                        dve.reciprocal(h_rstd[i][:], h_std[i][:]).then_inc(s_hrstd, 1)
                    for i in L:
                        dve.wait_ge(s_bc, nth(c, i))
                        for m in range(MO):
                            ins = dve.scalar_tensor_tensor(out=o_norm[i][:, m, :], in0=o_in[i][:, m, :],
                                                           scalar=gain[:, 0:1], in1=bank[i][m][:, 0:T],
                                                           op0=ALU.mult, op1=ALU.mult)
                        ins.then_inc(s_onorm, 1)
                    for i in L:
                        dve.wait_ge(s_y, nth(c, i))
                        dve.wait_ge(s_st_t[i], c * 32 + 1)
                        for k in range(KC):
                            ins = dve.tensor_tensor(t[i][:, k, :], x_in[i][:, k, :], bank[i][k][:, 0:T], ALU.add)
                        ins.then_inc(s_t, 1)
                    for i in L:
                        dve.wait_ge(s_mean, nth(c, i))
                        for k in range(KC):
                            ins = dve.tensor_tensor(dev[i][:, k, :], t[i][:, k, :], bank[i][2][:, 0:T], ALU.subtract)
                        ins.then_inc(s_dev, 1)
                    for i in L:
                        dve.wait_ge(s_std, nth(c, i))
                        dve.reciprocal(rstd[i][:], std[i][:]).then_inc(s_rstd, 1)
                        dve.wait_ge(s_rstd, nth(c, i))
                        for k in range(KC):
                            ins = dve.tensor_tensor(ln[i][:, k, :], dev[i][:, k, :], rstd[i][:], ALU.mult)
                        ins.then_inc(s_ln, 1)
                    for i in L:
                        for m in range(MQK):
                            dve.wait_ge(s_hi, nth(c, i) * MQK - (MQK - 1) + m)
                            dve.scalar_tensor_tensor(out=lo[i][:, m, :], in0=bank[i][m][:, 0:T],
                                                     scalar=qk_bias[:, m:m + 1], in1=hi[i][:, m, :].bitcast(F32),
                                                     op0=ALU.add, op1=ALU.subtract).then_inc(s_lo, 1)
                    for i in L:
                        dve.wait_ge(s_v, nth(c, i))
                        dve.wait_ge(s_st_v[i], c * 16 + 1)
                        for s in range(SUB):
                            ins = dve.tensor_tensor(v_out[i][:, s, :], bank[i][s][:, 0:C], v_bias[:], ALU.add)
                        ins.then_inc(s_vout, 1)


def causal_attention(nc, qk_hi, qk_lo, v_rows, ident, o_t):
    HN, DH = 4, C // 4
    PAIRS = HN // 2
    PBUF = 6
    LOADS = 2 * 6 + 1
    SCALE = DH ** -0.5
    MASKED = -3e38
    steps = [SUB * (c + 1) for c in range(NC)]
    first = [sum(steps[:c]) for c in range(NC + 1)]
    units = [[(j, s, list(range(k, min(k + 2, c + 1)))) for j in range(2) for s in range(SUB)
              for k in range(0, c + 1, 2)] for c in range(NC)]
    ufirst = [sum(len(u) for u in units[:c]) for c in range(NC + 1)]
    adds = [n - 1 for n in steps]
    afirst = [sum(adds[:c]) for c in range(NC + 1)]
    at_step = [(c, g) for c in range(NC) for g in range(steps[c])]

    def units_at(c, g):
        n = len(units[c + 1])
        return [u for u in range(n) if u * steps[c] // n == g]

    with ExitStack() as ctx:
        sb, ps, sem = tools(nc, ctx, "causal")
        ka = [sb(f"ka{j}", [P, N], F32R) for j in range(2)]
        kb = [sb(f"kb{j}", [DH + 1, N], F32R) for j in range(2)]
        qa = [sb(f"qa{j}", [P, N], F32R) for j in range(2)]
        qb = [sb(f"qb{j}", [DH + 1, N], F32R) for j in range(2)]
        vs = sb("vs", [P, NT, 2, DH])
        probs = [sb(f"probs{i}", [P, 2 * T]) for i in range(PBUF)]
        run_sum = sb("run_sum", [P, 2 * T])
        row_sum = sb("row_sum", [P, 2 * T])
        maxes = sb("maxes", [P, 2 * SUB, 3])
        neg_max = sb("neg_max", [P, 2 * SUB])
        out_sb = sb("out", [P, T])
        recip = sb("recip", [P, T])
        normed = [sb(f"normed{i}", [P, T]) for i in range(2)]
        ones = sb("ones", [P, DH])
        ident_sb = sb("ident", [P, P])
        ident_bf = sb("ident_bf", [P, P], BF16)
        mask_q = sb("mask_q", [P, SUB, T], BF16)
        mask_k = sb("mask_k", [P, SUB, T], BF16)
        scores = [ps(f"scores{i}", [P, 2, 512]) for i in range(2)]
        max_ps = ps("max", [P, 2, 512])
        out_ps = ps("out_ps", [P, 512])
        misc = ps("misc", [P, 512])
        s_const, s_ones, s_zero, s_mask = sem("const"), sem("ones"), sem("mask_zeroed"), sem("masks_ready")
        s_ld = [sem(f"loaded{c}") for c in range(NC)]
        s_st, s_exp, s_pv, s_acc = (sem(n) for n in ("scores_mm", "exp_done", "pv_mm", "row_sum_done"))
        s_mx, s_red, s_neg, s_rows, s_row = (sem(n) for n in (
            "max_mm", "max_taken", "neg_max_ready", "rows_mm", "rows_placed"))
        s_oev, s_l, s_rec, s_norm = (sem(n) for n in ("out_taken", "sums_mm", "recip_done", "normed_ready"))
        s_store = [sem(f"stored{i}") for i in range(2)]

        with nc.Block() as block:
            @block.sync
            def _(sp):
                for i in range(2):
                    sp.sem_inc(s_store[i], 1)
                sp.dma_start(ident_sb[:], ident).then_inc(s_const, 16)
                parts = qk_hi, qk_lo
                hi, lo = (x.rearrange("b (x h j d) n -> (b x h) j d n", x=2, h=PAIRS, j=2) for x in parts)
                with sp.Fori(0, B) as b:
                    with sp.Fori(0, PAIRS) as h:
                        it = b * PAIRS + h
                        sp.wait_ge(s_pv, it * first[NC] + PBUF)
                        for c in range(NC):
                            cols = slice(c * T, (c + 1) * T)
                            for j in range(2):
                                q = [x[bass.ds(b * 2 * PAIRS + h, 1), j, :, cols].rearrange("a d n -> (a d) n")
                                     for x in (hi, lo)]
                                k = [x[bass.ds(b * 2 * PAIRS + PAIRS + h, 1), j, :, cols].rearrange("a d n -> (a d) n")
                                     for x in (hi, lo)]
                                for dst, row, src in ((ka, 0, k[0]), (ka, DH, k[1]), (kb, 0, k[0]),
                                                      (qa, 0, q[0]), (qa, DH, q[0]), (qb, 0, q[1])):
                                    sp.dma_start(dst[j][row:row + DH, cols].bitcast(F32), src).then_inc(s_ld[c], 16)
                            sp.dma_start(vs[:, c * SUB:(c + 1) * SUB, :, :].rearrange("p t j d -> p t (j d)"),
                                         v_rows.rearrange("b (t p) c -> p (b t) c", p=P)[
                                             :, bass.ds(b * NT + c * SUB, SUB), bass.ds(h * 2 * DH, 2 * DH)]
                                         ).then_inc(s_ld[c], 16)
                        for c in range(NC):
                            sp.wait_ge(s_norm, it * NC + c + 2)
                            sp.dma_start(o_t.rearrange("b (h p) n -> p (b h) n", p=P)[
                                :, bass.ds(it, 1), c * T:(c + 1) * T].rearrange("p a n -> p (a n)"),
                                normed[c % 2][:]).then_inc(s_store[c % 2], 16)
                for i in range(2):
                    sp.wait_ge(s_store[i], B * PAIRS * NC // 2 * 16 + 1)

            @block.tensor
            def _(pe):
                pe.sem_inc(s_pv, PBUF)
                pe.sem_inc(s_rows, 1)
                pe.wait_ge(s_const, 16)
                pe.wait_ge(s_ones, 2)
                pe.wait_ge(s_mask, 3)

                def score_step(it, c, g):
                    if g == 0:
                        pe.wait_ge(s_row, (it * NC + c + 1) * 2)
                    pe.wait_ge(s_exp, it * first[NC] + max(first[c] + g + 1, 2))
                    cols, keys = slice(c * T, (c + 1) * T), slice(g * P, (g + 1) * P)
                    diagonal = g - SUB * c
                    for j in range(2):
                        to = scores[(first[c] + g) % 2][:, j, 0:T]
                        pe.matmul(to, ka[j][:, keys], qa[j][:, cols], start=True, stop=False)
                        mm = pe.matmul(to, kb[j][:, keys], qb[j][:, cols], start=False, stop=diagonal < 0)
                        if diagonal >= 0:
                            mm = pe.matmul(to, ident_bf[:], mask_k[:, diagonal, :], start=False, stop=True)
                    mm.then_inc(s_st, 1)

                def max_unit(it, c, u):
                    if u == 0:
                        pe.wait_ge(s_ld[c], (it + 1) * LOADS * 16)
                    pe.wait_ge(s_red, it * ufirst[NC] + ufirst[c] + u + 1)
                    j, s, chunks = units[c][u]
                    queries = slice(c * T + s * P, c * T + (s + 1) * P)
                    for k, at in enumerate(chunks):
                        to, keys = max_ps[:, k, 0:T], slice(at * T, (at + 1) * T)
                        pe.matmul(to, qa[j][:, queries], ka[j][:, keys], start=True, stop=False)
                        mm = pe.matmul(to, qb[j][0:DH, queries], kb[j][0:DH, keys], start=False, stop=at < c)
                        if at == c:
                            mm = pe.matmul(to, ident_bf[:], mask_q[:, s, :], start=False, stop=True)
                    mm.then_inc(s_mx, 1)

                def pv_step(it, c, g):
                    if g == 0:
                        pe.wait_ge(s_oev, it * NC + c + 1)
                    pe.wait_ge(s_exp, it * first[NC] + first[c] + g + 3)
                    for j in range(2):
                        mm = pe.matmul(out_ps[DH * j:DH * (j + 1), 0:T], vs[:, g, j, :],
                                       probs[(first[c] + g) % PBUF][:, j * T:(j + 1) * T],
                                       start=g == 0, stop=g == steps[c] - 1, tile_position=(0, DH * j))
                    mm.then_inc(s_pv, 1)

                def rows(it, c):
                    pe.wait_ge(s_rec, it * NC + max(c - 1, 0) + 1)
                    pe.wait_ge(s_neg, it * NC + c + 1)
                    for j in range(2):
                        for s in range(SUB):
                            mm = pe.matmul(misc[32 * j:32 * j + 1, s * P:(s + 1) * P],
                                           neg_max[:, j * SUB + s:j * SUB + s + 1], ident_sb[:],
                                           start=True, stop=True, tile_position=(0, 32 * j))
                    mm.then_inc(s_rows, 1)

                def sums(it, c):
                    if c < NC - 1:
                        pe.wait_ge(s_row, (it * NC + c + 2) * 2)
                    else:
                        pe.wait_ge(s_rec, it * NC + c + 1)
                    pe.wait_ge(s_acc, it * afirst[NC] + afirst[c + 1] + 1)
                    for j in range(2):
                        mm = pe.matmul(misc[DH * j:DH * (j + 1), 0:T], ones[:], row_sum[:, j * T:(j + 1) * T],
                                       start=True, stop=True, tile_position=(0, DH * j))
                    mm.then_inc(s_l, 1)

                with pe.Fori(0, B * PAIRS) as it:
                    for u in range(len(units[0])):
                        max_unit(it, 0, u)
                    rows(it, 0)
                    for c in range(NC):
                        for g in range(steps[c]):
                            score_step(it, c, g)
                            if c + 1 < NC:
                                for u in units_at(c, g):
                                    max_unit(it, c + 1, u)
                            if g > 0:
                                pv_step(it, c, g - 1)
                            if c > 0 and g == 2:
                                sums(it, c - 1)
                        pv_step(it, c, steps[c] - 1)
                        if c + 1 < NC:
                            rows(it, c + 1)
                    sums(it, NC - 1)

            @block.scalar
            def _(act):
                act.sem_inc(s_exp, 2)
                act.sem_inc(s_oev, 1)

                def place_row(it, c):
                    act.wait_ge(s_rows, it * NC + c + 2)
                    act.activation(qb[1][DH:DH + 1, c * T:(c + 1) * T], misc[32:33, 0:T], ACT.Copy).then_inc(s_row, 1)

                with act.Fori(0, B * PAIRS) as it:
                    place_row(it, 0)
                    for c in range(NC):
                        for g in range(steps[c]):
                            at = first[c] + g
                            act.wait_ge(s_st, it * first[NC] + at + 1)
                            act.wait_ge(s_pv, it * first[NC] + max(at + 1, PBUF))
                            if at >= PBUF:
                                bc, bg = at_step[at - PBUF]
                                act.wait_ge(s_acc, it * afirst[NC] + afirst[bc] + max(bg, 1) + 1)
                            elif at == 0:
                                act.wait_ge(s_acc, it * afirst[NC] + 1)
                            act.activation(probs[at % PBUF][:].rearrange("p (j n) -> p j n", j=2),
                                           scores[at % 2][:, :, 0:T], ACT.Exp, scale=SCALE).then_inc(s_exp, 1)
                        act.wait_ge(s_norm, it * NC + c + 1)
                        act.wait_ge(s_pv, it * first[NC] + first[c + 1] + PBUF)
                        act.activation(out_sb[:], out_ps[:, 0:T], ACT.Copy).then_inc(s_oev, 1)
                        if c + 1 < NC:
                            place_row(it, c + 1)

            @block.vector
            def _(dve):
                dve.sem_inc(s_red, 1)
                dve.sem_inc(s_rec, 1)
                dve.sem_inc(s_norm, 1)
                for j in range(2):
                    ins = dve.memset(kb[j][DH:DH + 1, :].bitcast(F32), 1.0)
                ins.then_inc(s_ones, 1)
                dve.memset(ones[:], 1.0).then_inc(s_ones, 1)
                dve.wait_ge(s_const, 16)
                dve.tensor_copy(ident_bf[:], ident_sb[:]).then_inc(s_mask, 1)

                def max_unit(it, c, u):
                    j, s, chunks = units[c][u]
                    dve.wait_ge(s_mx, it * ufirst[NC] + ufirst[c] + u + 1)
                    k = chunks[0] // 2
                    dve.tensor_reduce(maxes[:, j * SUB + s:j * SUB + s + 1, k], max_ps[:, 0:len(chunks), 0:T],
                                      AX.XY, ALU.max).then_inc(s_red, 1)

                def negate(it, c):
                    dve.wait_ge(s_rows, it * NC + c + 1)
                    dve.wait_ge(s_red, it * ufirst[NC] + ufirst[c + 1] + 1)
                    dve.tensor_reduce(neg_max[:], maxes[:, :, 0:c // 2 + 1], AX.X, ALU.max,
                                      negate=True).then_inc(s_neg, 1)

                def place_row(it, c):
                    dve.wait_ge(s_rows, it * NC + c + 2)
                    dve.tensor_copy(qb[0][DH:DH + 1, c * T:(c + 1) * T], misc[0:1, 0:T]).then_inc(s_row, 1)

                def normalise(it, c):
                    dve.wait_ge(s_l, it * NC + c + 1)
                    dve.wait_ge(s_norm, it * NC + c + 1)
                    dve.reciprocal(recip[:], misc[:, 0:T]).then_inc(s_rec, 1)
                    dve.wait_ge(s_oev, it * NC + c + 2)
                    dve.wait_ge(s_store[c % 2], (it * (NC // 2) + c // 2) * 16 + 1)
                    dve.wait_ge(s_rec, it * NC + c + 2)
                    dve.tensor_tensor(normed[c % 2][:], out_sb[:], recip[:], ALU.mult).then_inc(s_norm, 1)

                with dve.Fori(0, B * PAIRS) as it:
                    for u in range(len(units[0])):
                        max_unit(it, 0, u)
                    negate(it, 0)
                    place_row(it, 0)
                    for c in range(NC):
                        for g in range(steps[c]):
                            if c + 1 < NC:
                                for u in units_at(c, g):
                                    max_unit(it, c + 1, u)
                            if c > 0 and g == 2:
                                normalise(it, c - 1)
                        if c + 1 < NC:
                            negate(it, c + 1)
                            place_row(it, c + 1)
                    normalise(it, NC - 1)

            @block.gpsimd
            def _(pool):
                pool.sem_inc(s_acc, 1)
                pool.memset(mask_q[:], 0.0).then_inc(s_zero, 1)
                pool.memset(mask_k[:], 0.0).then_inc(s_zero, 1)
                pool.wait_ge(s_zero, 2)
                for s in range(SUB):
                    ins = pool.affine_select(out=mask_q[:, s, :], in_=mask_q[:, s, :], compare_op=ALU.is_ge,
                                             fill=MASKED, base=s * P, pattern=[[-1, T]], channel_multiplier=1)
                ins.then_inc(s_mask, 1)
                for s in range(SUB):
                    ins = pool.affine_select(out=mask_k[:, s, :], in_=mask_k[:, s, :], compare_op=ALU.is_ge,
                                             fill=MASKED, base=-s * P, pattern=[[1, T]], channel_multiplier=-1)
                ins.then_inc(s_mask, 1)
                with pool.Fori(0, B * PAIRS) as it:
                    for c in range(NC):
                        for g in range(1, steps[c]):
                            at = first[c] + g
                            pool.wait_ge(s_exp, it * first[NC] + at + 3)
                            pool.wait_ge(s_acc, it * afirst[NC] + afirst[c] + g)
                            acc = probs[(at - 1) % PBUF] if g == 1 else run_sum
                            to = row_sum if g == steps[c] - 1 else run_sum
                            pool.tensor_tensor(to[:], acc[:], probs[at % PBUF][:], ALU.add).then_inc(s_acc, 1)


def recurrence_gate_and_ffn(nc, a, o_t, a_t, t_t, t2_t):
    HN, DH = 4, C // 4
    FF = 4 * C // P
    LNS = 3
    WEIGHTS = 24
    with ExitStack() as ctx:
        sb, ps, sem = tools(nc, ctx, "rec")
        L = range(B)
        w = {n: sb(n, [P, KC, C]) for n in ("o_w", "rq_w", "rk_w", "rv_w", "ro_w")}
        w["cg_w"] = sb("cg_w", [P, 2 * KC, C])
        w["ffn_w1"] = sb("ffn_w1", [P, KC, 4 * C])
        w["ffn_w2"] = sb("ffn_w2", [P, FF, C])
        cols = {n: sb(n, [P, KC]) for n in ("o_b", "rq_b", "rk_b", "ro_b", "cg_b", "ffn_b2", "ln1_g", "ln1_b",
                                            "ln2_g", "ln2_b", "ln3_g", "ln3_b")}
        cols["ffn_b1"] = sb("ffn_b1", [P, FF])
        rv_bias = sb("rv_bias", [P, C])
        mean_mat = sb("mean_mat", [P, P])
        ident = sb("ident", [P, P])
        half_cg_b = sb("half_cg_b", [P, KC])
        eps = sb("eps", [P, 1])
        tri = sb("tri", [P, 2 * T])
        gain = [cols["ln1_g"], cols["ln2_g"], cols["ln3_g"]]
        bias = [cols["ln1_b"], cols["ln2_b"], cols["ln3_b"]]

        def per_lane(name, shape, dt=F32):
            return [sb(f"{name}{i}", shape, dt) for i in L]
        t, x, o = (per_lane(n, [P, KC, T]) for n in ("t", "x", "o"))
        res, par, dev, sq, nm, dn, seq, mrg, t2 = (per_lane(n, [P, KC, T]) for n in (
            "res", "par", "dev", "sq", "nm", "dn", "seq", "mrg", "t2"))
        std, rstd = per_lane("std", [P, T]), per_lane("rstd", [P, T])
        hid = per_lane("hid", [P, FF, T])
        fm = per_lane("fm", [P, 2 * KC, T])
        vx = per_lane("vx", [P, SUB, HN, P])
        kt = per_lane("kt", [P, SUB, C])
        at = [[sb(f"at{i}{k}", [P, 2 * T]) for k in range(2)] for i in L]
        state = per_lane("state", [P, KC, P])
        bank = [[ps(f"bank{i}{k}", [P, 512]) for k in range(4)] for i in L]
        s_w, s_set = sem("weights"), sem("set_up")
        s_ld = [sem(f"loaded{i}") for i in L]
        s_st = [sem(f"stored{i}") for i in L]
        (s_att, s_res, s_mean, s_dev, s_sq, s_var, s_std, s_rstd, s_scaled, s_ln, s_z, s_zmin, s_zout, s_zexp,
         s_fm, s_v, s_vx, s_kt, s_ktout) = (sem(n) for n in (
             "att_mm", "res_ready", "mean_mm", "dev_ready", "dev_squared", "var_mm", "std_ready", "rstd_ready",
             "scaled", "ln_ready", "features_mm", "z_min", "z_taken", "z_exp", "features_ready", "v_mm",
             "values_ready", "keys_turned", "keys_ready"))
        (s_a, s_at, s_oe, s_upd, s_num, s_den, s_state, s_rden, s_rec, s_ro, s_gate, s_th, s_diff, s_gated, s_mrg,
         s_h, s_gelu, s_f, s_t2, s_cgb) = (sem(n) for n in (
             "a_mm", "a_masked", "out_mm", "update_mm", "num_taken", "den_taken", "state_ready", "den_inverted",
             "rec_ready", "ro_mm", "gate_mm", "gate_tanh", "par_less_seq", "gated", "merged_ready", "hidden_mm",
             "hidden_ready", "ffn_mm", "t2_ready", "cgb_halved"))
        s_tri = sem("tri_set")

        def ln(c, r, i):
            return (c * LNS + r) * B + i + 1

        def head(c, h, i):
            return (c * HN + h) * B + i + 1

        def project(pe, to, weight, src, tiles, m):
            for k in range(tiles):
                mm = pe.matmul(to[:, 0:T], weight[:, k, m * P:(m + 1) * P], src(k), start=k == 0, stop=k == tiles - 1)
            return mm

        with nc.Block() as block:
            @block.sync
            def _(sp):
                for i in L:
                    sp.sem_inc(s_st[i], 1)
                loads = [(w[n], a[n]) for n in w] + [(cols[n], a[n]) for n in cols] + [
                    (mean_mat, a["mean_mat"]), (ident, a["ident"])]
                assert len(loads) + 1 == WEIGHTS
                for dst, src in loads:
                    sp.dma_start(dst[:], src).then_inc(s_w, 16)
                sp.dma_start(rv_bias[:], a["rv_b"].partition_broadcast(P)).then_inc(s_w, 16)
                with sp.Fori(0, NC) as c:
                    at_c = bass.ds(c * T, T)
                    for i in L:
                        sp.wait_ge(s_t2, nth(c, i))
                        for dst, src in ((o, o_t), (x, a_t), (t, t_t)):
                            sp.dma_start(dst[i][:], src[i].rearrange("(k p) n -> p k n", p=P)[:, :, at_c]
                                         ).then_inc(s_ld[i], 16)
                    for i in L:
                        sp.wait_ge(s_t2, nth(c + 1, i))
                        sp.dma_start(t2_t[i].rearrange("(k p) n -> p k n", p=P)[:, :, at_c], t2[i][:]
                                     ).then_inc(s_st[i], 16)
                for i in L:
                    sp.wait_ge(s_st[i], NC * 16 + 1)

            @block.tensor
            def _(pe):
                pe.wait_ge(s_w, 16 * WEIGHTS)
                pe.wait_ge(s_set, 6)

                def mean(c, r):
                    for i in L:
                        pe.wait_ge(s_res, ln(c, r, i))
                        for k in range(KC):
                            mm = pe.matmul(bank[i][2][:, 0:T], mean_mat[:], res[i][:, k, :],
                                           start=k == 0, stop=k == KC - 1)
                        mm.then_inc(s_mean, 1)

                def var(c, r):
                    for i in L:
                        pe.wait_ge(s_sq, ln(c, r, i))
                        for k in range(KC):
                            mm = pe.matmul(bank[i][3][:, 0:T], mean_mat[:], sq[i][:, k, :],
                                           start=k == 0, stop=k == KC - 1)
                        mm.then_inc(s_var, 1)

                with pe.Fori(0, NC) as c:
                    for i in L:
                        pe.wait_ge(s_ld[i], (c + 1) * 48)
                        pe.wait_ge(s_t2, nth(c, i))
                        for m in range(KC):
                            mm = project(pe, bank[i][m], w["o_w"], lambda k: o[i][:, k, :], KC, m)
                        mm.then_inc(s_att, 1)
                    mean(c, 0)
                    var(c, 0)
                    for i in L:
                        pe.wait_ge(s_ln, ln(c, 0, i))
                        for m in range(2 * KC):
                            mm = project(pe, bank[i][m], w["rq_w" if m < KC else "rk_w"],
                                         lambda k: par[i][:, k, :], KC, m % KC)
                        mm.then_inc(s_z, 1)
                    for i in L:
                        pe.wait_ge(s_zout, nth(c, i))
                        for s in range(SUB):
                            for k in range(KC):
                                mm = pe.matmul(bank[i][s][:, 0:C], par[i][:, k, s * P:(s + 1) * P],
                                               w["rv_w"][:, k, :], start=k == 0, stop=k == KC - 1)
                        mm.then_inc(s_v, 1)
                    for i in L:
                        pe.wait_ge(s_fm, nth(c, i))
                        pe.wait_ge(s_vx, nth(c, i))
                        for k in range(KC):
                            for s in range(SUB):
                                mm = pe.transpose(bank[i][3 if k == 0 else 0][:, s * P:(s + 1) * P],
                                                  fm[i][:, KC + k, s * P:(s + 1) * P], ident[:])
                        mm.then_inc(s_kt, 1)
                    for h in range(HN):
                        half, base = h // 2, DH * (h % 2)
                        rows = slice(base, base + DH)
                        for i in L:
                            if h == 0:
                                pe.wait_ge(s_ktout, nth(c, i))
                            else:
                                pe.wait_ge(s_at, head(c, h - 1, i))
                            for s, (b, col) in enumerate(((0, 0), (1, 0), (0, T))):
                                mm = pe.matmul(bank[i][b][:, col:col + T - s * P],
                                               fm[i][rows, KC + half, s * P:(s + 1) * P],
                                               fm[i][rows, half, s * P:T], start=True, stop=True)
                            mm.then_inc(s_a, 1)
                        for i in L:
                            pe.wait_ge(s_at, head(c, h, i))
                            pe.wait_ge(s_num, head(c, h, i))
                            pe.wait_ge(s_den, head(c, h, i))
                            if h == 0:
                                pe.wait_ge(s_state, nth(c, i))
                            pe.matmul(bank[i][2][:, 0:T], state[i][rows, half, :], fm[i][rows, half, :],
                                      start=True, stop=False)
                            for s, col in enumerate((0, T + P, T)):
                                mm = pe.matmul(bank[i][2][:, s * P:T], vx[i][:, s, h, :],
                                               at[i][h % 2][:, col:col + T - s * P], start=False, stop=s == SUB - 1)
                            mm.then_inc(s_oe, 1)
                            for s in range(SUB):
                                mm = pe.matmul(bank[i][3][rows, half * P:(half + 1) * P],
                                               kt[i][:, s, h * DH:(h + 1) * DH], vx[i][:, s, h, :],
                                               start=s == 0, stop=s == SUB - 1, tile_position=(0, base))
                            if h == HN - 1:
                                mm.then_inc(s_upd, 1)
                    for i in L:
                        pe.wait_ge(s_rec, nth(c, i))
                        for m in range(KC):
                            mm = project(pe, bank[i][m], w["ro_w"], lambda k: nm[i][:, k, :], KC, m)
                        mm.then_inc(s_ro, 1)
                    mean(c, 1)
                    var(c, 1)
                    for i in L:
                        pe.wait_ge(s_ln, ln(c, 1, i))
                        for m in range(KC):
                            mm = project(pe, bank[i][m], w["cg_w"],
                                         lambda k: (par if k < KC else seq)[i][:, k % KC, :], 2 * KC, m)
                        mm.then_inc(s_gate, 1)
                    for i in L:
                        pe.wait_ge(s_mrg, nth(c, i))
                        for m in range(FF):
                            if m >= 4:
                                pe.wait_ge(s_gelu, nth(c, i) * FF - (FF - 1) + m - 4)
                            project(pe, bank[i][m % 4], w["ffn_w1"], lambda k: mrg[i][:, k, :], KC, m
                                    ).then_inc(s_h, 1)
                    for i in L:
                        pe.wait_ge(s_gelu, nth(c, i) * FF)
                        for m in range(KC):
                            mm = project(pe, bank[i][m], w["ffn_w2"], lambda k: hid[i][:, k, :], FF, m)
                        mm.then_inc(s_f, 1)
                    mean(c, 2)
                    var(c, 2)

            @block.scalar
            def _(act):
                act.wait_ge(s_w, 16 * WEIGHTS)
                act.wait_ge(s_set, 6)
                act.sem_inc(s_num, B)
                act.activation(half_cg_b[:], cols["cg_b"][:], ACT.Copy, scale=0.5).then_inc(s_cgb, 1)
                act.wait_ge(s_cgb, 1)

                def layer_norm(c, r, out):
                    for i in L:
                        act.wait_ge(s_dev, ln(c, r, i))
                        act.activation(sq[i][:], dev[i][:], ACT.Square).then_inc(s_sq, 1)
                    for i in L:
                        act.wait_ge(s_var, ln(c, r, i))
                        act.activation(std[i][:], bank[i][3][:, 0:T], ACT.Sqrt, bias=eps[:, 0:1]).then_inc(s_std, 1)
                    for i in L:
                        act.wait_ge(s_scaled, ln(c, r, i))
                        for k in range(KC):
                            ins = act.activation(out[i][:, k, :], dev[i][:, k, :], ACT.Identity,
                                                 bias=bias[r][:, k:k + 1])
                        ins.then_inc(s_ln, 1)

                with act.Fori(0, NC) as c:
                    layer_norm(c, 0, par)
                    for i in L:
                        act.wait_ge(s_z, nth(c, i))
                        for m in range(2 * KC):
                            ins = act.activation(hid[i][:, m, :], bank[i][m][:, 0:T], ACT.Identity,
                                                 bias=cols["rq_b" if m < KC else "rk_b"][:, m % KC:m % KC + 1])
                        ins.then_inc(s_zout, 1)
                    for i in L:
                        act.wait_ge(s_zmin, nth(c, i))
                        act.activation(fm[i][:], hid[i][:, 4:8, :], ACT.Exp).then_inc(s_zexp, 1)
                    for i in L:
                        act.wait_ge(s_kt, nth(c, i))
                        for k in range(KC):
                            ins = act.activation(kt[i][:, :, k * P:(k + 1) * P],
                                                 bank[i][3 if k == 0 else 0][:, 0:T].rearrange(
                                                     "p (s c) -> p s c", s=SUB), ACT.Copy)
                        ins.then_inc(s_ktout, 1)
                    for h in range(HN):
                        half, base = h // 2, DH * (h % 2)
                        for i in L:
                            act.wait_ge(s_oe, head(c, h, i))
                            act.activation(nm[i][base:base + DH, half, :], bank[i][2][0:DH, 0:T], ACT.Copy
                                           ).then_inc(s_num, 1)
                    layer_norm(c, 1, seq)
                    for i in L:
                        act.wait_ge(s_gate, nth(c, i))
                        for m in range(KC):
                            ins = act.activation(nm[i][:, m, :], bank[i][m][:, 0:T], ACT.Tanh, scale=0.5,
                                                 bias=half_cg_b[:, m:m + 1])
                        ins.then_inc(s_th, 1)
                    for i in L:
                        for m in range(FF):
                            act.wait_ge(s_h, nth(c, i) * FF - (FF - 1) + m)
                            act.activation(hid[i][:, m, :], bank[i][m % 4][:, 0:T], ACT.Gelu,
                                           bias=cols["ffn_b1"][:, m:m + 1]).then_inc(s_gelu, 1)
                    layer_norm(c, 2, seq)

            @block.vector
            def _(dve):
                dve.sem_inc(s_den, B)
                dve.sem_inc(s_t2, B)
                dve.memset(eps[:], LN_EPS).then_inc(s_set, 1)
                for i in L:
                    dve.memset(vx[i][:], 1.0).then_inc(s_set, 1)
                    dve.memset(state[i][:], 0.0).then_inc(s_state, 1)
                dve.wait_ge(s_w, 16 * WEIGHTS)
                dve.wait_ge(s_set, 6)

                def residual(c, r, counter, bias_cols, other):
                    for i in L:
                        dve.wait_ge(counter, nth(c, i))
                        for m in range(KC):
                            ins = dve.scalar_tensor_tensor(out=res[i][:, m, :], in0=bank[i][m][:, 0:T],
                                                           scalar=bias_cols[:, m:m + 1], in1=other[i][:, m, :],
                                                           op0=ALU.add, op1=ALU.add)
                        ins.then_inc(s_res, 1)

                def layer_norm(c, r):
                    for i in L:
                        dve.wait_ge(s_mean, ln(c, r, i))
                        for k in range(KC):
                            ins = dve.tensor_tensor(dev[i][:, k, :], res[i][:, k, :], bank[i][2][:, 0:T], ALU.subtract)
                        ins.then_inc(s_dev, 1)
                    for i in L:
                        dve.wait_ge(s_std, ln(c, r, i))
                        dve.reciprocal(rstd[i][:], std[i][:]).then_inc(s_rstd, 1)
                    for i in L:
                        dve.wait_ge(s_rstd, ln(c, r, i))
                        for k in range(KC):
                            ins = dve.scalar_tensor_tensor(out=dev[i][:, k, :], in0=dev[i][:, k, :],
                                                           scalar=gain[r][:, k:k + 1], in1=rstd[i][:],
                                                           op0=ALU.mult, op1=ALU.mult)
                        ins.then_inc(s_scaled, 1)

                with dve.Fori(0, NC) as c:
                    residual(c, 0, s_att, cols["o_b"], x)
                    layer_norm(c, 0)
                    for i in L:
                        dve.wait_ge(s_zout, nth(c, i))
                        dve.tensor_scalar(hid[i][:, 4:8, :], hid[i][:, 0:4, :], 0.0, None, ALU.min
                                          ).then_inc(s_zmin, 1)
                    for i in L:
                        dve.wait_ge(s_zexp, nth(c, i))
                        dve.scalar_tensor_tensor(out=fm[i][:], in0=hid[i][:, 0:4, :], scalar=0.0, in1=fm[i][:],
                                                 op0=ALU.max, op1=ALU.add).then_inc(s_fm, 1)
                    for i in L:
                        dve.wait_ge(s_v, nth(c, i))
                        for s in range(SUB):
                            ins = dve.tensor_tensor(vx[i][:, s, :, 0:DH],
                                                    bank[i][s][:, 0:C].rearrange("p (h d) -> p h d", h=HN),
                                                    rv_bias[:].rearrange("p (h d) -> p h d", h=HN), ALU.add)
                        ins.then_inc(s_vx, 1)
                    for h in range(HN):
                        half, base = h // 2, DH * (h % 2)
                        for i in L:
                            dve.wait_ge(s_a, head(c, h, i))
                            if h >= 2:
                                dve.wait_ge(s_oe, head(c, h - 2, i))
                            dve.tensor_tensor(at[i][h % 2][:, 0:512], bank[i][0][:, 0:512], tri[:, 0:512], ALU.mult)
                            dve.tensor_tensor(at[i][h % 2][:, 512:768], bank[i][1][:, 0:256], tri[:, 512:768],
                                              ALU.mult).then_inc(s_at, 1)
                        for i in L:
                            dve.wait_ge(s_oe, head(c, h, i))
                            dve.tensor_scalar(dn[i][base:base + DH, half, :], bank[i][2][DH:P, 0:T], EPS_REC, None,
                                              ALU.add).then_inc(s_den, 1)
                    for i in L:
                        dve.wait_ge(s_upd, nth(c, i))
                        dve.tensor_tensor(state[i][:].rearrange("p k m -> p (k m)"),
                                          state[i][:].rearrange("p k m -> p (k m)"), bank[i][3][:, 0:2 * P],
                                          ALU.add).then_inc(s_state, 1)
                    for i in L:
                        dve.wait_ge(s_den, head(c + 1, 0, i))
                        dve.reciprocal(dn[i][:], dn[i][:]).then_inc(s_rden, 1)
                        dve.wait_ge(s_rden, nth(c, i))
                        dve.wait_ge(s_num, head(c + 1, 0, i))
                        dve.tensor_tensor(nm[i][:], nm[i][:], dn[i][:], ALU.mult).then_inc(s_rec, 1)
                    residual(c, 1, s_ro, cols["ro_b"], par)
                    layer_norm(c, 1)
                    for i in L:
                        dve.wait_ge(s_ln, ln(c, 1, i))
                        dve.tensor_tensor(dn[i][:], par[i][:], seq[i][:], ALU.subtract).then_inc(s_diff, 1)
                    for i in L:
                        dve.wait_ge(s_th, nth(c, i))
                        dve.wait_ge(s_diff, nth(c, i))
                        dve.scalar_tensor_tensor(out=mrg[i][:], in0=nm[i][:], scalar=1.0, in1=dn[i][:],
                                                 op0=ALU.add, op1=ALU.mult).then_inc(s_gated, 1)
                        dve.wait_ge(s_gated, nth(c, i))
                        dve.scalar_tensor_tensor(out=mrg[i][:], in0=mrg[i][:], scalar=0.5, in1=seq[i][:],
                                                 op0=ALU.mult, op1=ALU.add).then_inc(s_mrg, 1)
                    residual(c, 2, s_f, cols["ffn_b2"], mrg)
                    layer_norm(c, 2)
                    for i in L:
                        dve.wait_ge(s_ln, ln(c, 2, i))
                        dve.wait_ge(s_st[i], c * 16 + 1)
                        dve.tensor_tensor(t2[i][:], t[i][:], seq[i][:], ALU.add).then_inc(s_t2, 1)

            @block.gpsimd
            def _(pool):
                pool.memset(tri[:], 1.0).then_inc(s_tri, 1)
                pool.wait_ge(s_tri, 1)
                for col in (0, T, T + P):
                    pool.affine_select(out=tri[:, col:col + P], in_=tri[:, col:col + P], compare_op=ALU.is_ge,
                                       fill=0.0, base=0, pattern=[[1, P]], channel_multiplier=-1).then_inc(s_set, 1)


def routed_ffn(nc, a, t_t, logits, base_t, delta_t):
    FF = 4 * C // P
    WEIGHTS = 7
    with ExitStack() as ctx:
        sb, ps, sem = tools(nc, ctx, "ffn")
        L = range(B)
        w1 = sb("w1", [P, KC, 4 * C])
        w2 = sb("w2", [P, FF, C])
        wr = sb("wr", [P, KC])
        br = sb("br", [1, 1])
        b1 = sb("b1", [P, FF])
        b2 = sb("b2", [P, KC])
        mean_mat = sb("mean_mat", [P, P])
        eps = sb("eps", [P, 1])
        t, dev, sq, x, base, delta = ([sb(f"{n}{i}", [P, KC, T]) for i in L] for n in (
            "t", "dev", "sq", "x", "base", "delta"))
        std, rstd = ([sb(f"{n}{i}", [P, T]) for i in L] for n in ("std", "rstd"))
        hid = [sb(f"hid{i}", [P, FF, T]) for i in L]
        row = [sb(f"row{i}", [1, T]) for i in L]
        bank = [[ps(f"bank{i}{k}", [P, 512]) for k in range(4)] for i in L]
        s_w, s_set = sem("weights"), sem("set_up")
        s_ld = [sem(f"loaded{i}") for i in L]
        s_st = [sem(f"stored{i}") for i in L]
        (s_mean, s_dev, s_sq, s_var, s_std, s_rstd, s_x, s_logit, s_row, s_base, s_h, s_gelu, s_f, s_delta) = (
            sem(n) for n in ("mean_mm", "dev_ready", "dev_squared", "var_mm", "std_ready", "rstd_ready", "x_ready",
                             "logit_mm", "row_ready", "base_ready", "hidden_mm", "hidden_ready", "ffn_mm",
                             "delta_ready"))

        with nc.Block() as block:
            @block.sync
            def _(sp):
                for i in L:
                    sp.sem_inc(s_st[i], 1)
                for dst, src in ((w1, a["w1"]), (w2, a["w2"]), (wr, a["wr"]), (br, a["br"]), (b1, a["b1"]),
                                 (b2, a["b2"]), (mean_mat, a["mean_mat"])):
                    sp.dma_start(dst[:], src).then_inc(s_w, 16)
                with sp.Fori(0, NC) as c:
                    at_c = bass.ds(c * T, T)
                    for i in L:
                        sp.wait_ge(s_base, nth(c, i))
                        sp.dma_start(t[i][:], t_t[i].rearrange("(k p) n -> p k n", p=P)[:, :, at_c]
                                     ).then_inc(s_ld[i], 16)
                    for i in L:
                        sp.wait_ge(s_row, nth(c, i))
                        sp.dma_start(logits[i:i + 1, at_c], row[i][:]).then_inc(s_st[i], 16)
                        sp.wait_ge(s_base, nth(c + 1, i))
                        sp.dma_start(base_t[i].rearrange("(k p) n -> p k n", p=P)[:, :, at_c], base[i][:]
                                     ).then_inc(s_st[i], 16)
                    for i in L:
                        sp.wait_ge(s_delta, nth(c + 1, i))
                        sp.dma_start(delta_t[i].rearrange("(k p) n -> p k n", p=P)[:, :, at_c], delta[i][:]
                                     ).then_inc(s_st[i], 16)
                for i in L:
                    sp.wait_ge(s_st[i], NC * 48 + 1)

            @block.tensor
            def _(pe):
                pe.wait_ge(s_w, 16 * WEIGHTS)
                with pe.Fori(0, NC) as c:
                    for i in L:
                        pe.wait_ge(s_ld[i], (c + 1) * 16)
                        pe.wait_ge(s_delta, nth(c, i))
                        for k in range(KC):
                            mm = pe.matmul(bank[i][2][:, 0:T], mean_mat[:], t[i][:, k, :],
                                           start=k == 0, stop=k == KC - 1)
                        mm.then_inc(s_mean, 1)
                    for i in L:
                        pe.wait_ge(s_sq, nth(c, i))
                        for k in range(KC):
                            mm = pe.matmul(bank[i][3][:, 0:T], mean_mat[:], sq[i][:, k, :],
                                           start=k == 0, stop=k == KC - 1)
                        mm.then_inc(s_var, 1)
                    for i in L:
                        pe.wait_ge(s_x, nth(c, i))
                        for k in range(KC):
                            mm = pe.matmul(bank[i][2][0:1, 0:T], wr[:, k:k + 1], x[i][:, k, :],
                                           start=k == 0, stop=k == KC - 1)
                        mm.then_inc(s_logit, 1)
                    for i in L:
                        for m in range(FF):
                            if m == 2:
                                pe.wait_ge(s_row, nth(c, i))
                            if m >= 4:
                                pe.wait_ge(s_gelu, nth(c, i) * FF - (FF - 1) + m - 4)
                            for k in range(KC):
                                mm = pe.matmul(bank[i][m % 4][:, 0:T], w1[:, k, m * P:(m + 1) * P], x[i][:, k, :],
                                               start=k == 0, stop=k == KC - 1)
                            mm.then_inc(s_h, 1)
                    for i in L:
                        pe.wait_ge(s_gelu, nth(c, i) * FF)
                        for m in range(KC):
                            for k in range(FF):
                                mm = pe.matmul(bank[i][m][:, 0:T], w2[:, k, m * P:(m + 1) * P], hid[i][:, k, :],
                                               start=k == 0, stop=k == FF - 1)
                        mm.then_inc(s_f, 1)

            @block.scalar
            def _(act):
                act.wait_ge(s_w, 16 * WEIGHTS)
                act.wait_ge(s_set, 1)
                act.sem_inc(s_delta, B)
                with act.Fori(0, NC) as c:
                    for i in L:
                        act.wait_ge(s_dev, nth(c, i))
                        act.activation(sq[i][:], dev[i][:], ACT.Square).then_inc(s_sq, 1)
                    for i in L:
                        act.wait_ge(s_var, nth(c, i))
                        act.activation(std[i][:], bank[i][3][:, 0:T], ACT.Sqrt, bias=eps[:, 0:1]).then_inc(s_std, 1)
                    for i in L:
                        act.wait_ge(s_logit, nth(c, i))
                        act.wait_ge(s_st[i], c * 48 + 1)
                        act.activation(row[i][:], bank[i][2][0:1, 0:T], ACT.Identity, bias=br[:, 0:1]
                                       ).then_inc(s_row, 1)
                    for i in L:
                        for m in range(FF):
                            act.wait_ge(s_h, nth(c, i) * FF - (FF - 1) + m)
                            act.activation(hid[i][:, m, :], bank[i][m % 4][:, 0:T], ACT.Gelu_apprx_tanh,
                                           bias=b1[:, m:m + 1]).then_inc(s_gelu, 1)
                    for i in L:
                        act.wait_ge(s_f, nth(c, i))
                        for m in range(KC):
                            ins = act.activation(delta[i][:, m, :], bank[i][m][:, 0:T], ACT.Identity,
                                                 bias=b2[:, m:m + 1])
                        ins.then_inc(s_delta, 1)

            @block.vector
            def _(dve):
                dve.sem_inc(s_base, B)
                dve.memset(eps[:], LN_EPS).then_inc(s_set, 1)
                dve.wait_ge(s_set, 1)
                with dve.Fori(0, NC) as c:
                    for i in L:
                        dve.wait_ge(s_mean, nth(c, i))
                        for k in range(KC):
                            ins = dve.tensor_tensor(dev[i][:, k, :], t[i][:, k, :], bank[i][2][:, 0:T], ALU.subtract)
                        ins.then_inc(s_dev, 1)
                    for i in L:
                        dve.wait_ge(s_std, nth(c, i))
                        dve.reciprocal(rstd[i][:], std[i][:]).then_inc(s_rstd, 1)
                    for i in L:
                        dve.wait_ge(s_rstd, nth(c, i))
                        for k in range(KC):
                            ins = dve.tensor_tensor(x[i][:, k, :], dev[i][:, k, :], rstd[i][:], ALU.mult)
                        ins.then_inc(s_x, 1)
                    for i in L:
                        dve.wait_ge(s_x, nth(c, i))
                        dve.wait_ge(s_st[i], c * 48 + 1)
                        dve.tensor_tensor(base[i][:], t[i][:], x[i][:], ALU.add).then_inc(s_base, 1)


def select_and_merge(nc, logits, factors, ident, base_t, delta_t, out):
    KEPT = N // 2 - 1
    with ExitStack() as ctx:
        sb, ps, sem = tools(nc, ctx, "pick")
        L = range(B)
        row = [sb(f"row{i}", [P, N]) for i in L]
        by_tile = [sb(f"by_tile{i}", [NT, P]) for i in L]
        factor_row = [sb(f"factor_row{i}", [NT, P]) for i in L]
        ident_sb = sb("ident", [P, P])
        turn = [ps(f"turn{i}", [P, 512]) for i in L]
        s_const, s_turned, s_col, s_back, s_frow = (sem(n) for n in (
            "const", "logits_turned", "column_ready", "factors_turned", "factor_row_ready"))
        col = [sb(f"col{i}", [P, NT]) for i in L]
        before = sb("before", [P, P])
        scratch = sb("scratch", [P, N])
        tie = sb("tie", [P, P])
        counts = [sb(f"counts{i}", [P, NT, 3]) for i in L]
        rank = [sb(f"rank{i}", [P, NT]) for i in L]
        factor = [sb(f"factor{i}", [P, NT]) for i in L]
        spread = [sb(f"spread{i}", [P, N]) for i in L]
        base = [[sb(f"base{i}{k}", [P, N]) for k in range(KC)] for i in L]
        delta = [[sb(f"delta{i}{k}", [P, N]) for k in range(KC)] for i in L]
        s_tri, s_before, s_zero, s_step = sem("tri"), sem("before_ready"), sem("counts_zeroed"), sem("step")
        s_ld, s_in = [sem(f"loaded{i}") for i in L], [sem(f"tokens_loaded{i}") for i in L]
        s_rank, s_factor = sem("rank_ready"), sem("factor_ready")
        s_kept = [sem(f"factor_stored{i}") for i in L]
        s_spread = [sem(f"factor_spread{i}") for i in L]
        s_scaled, s_done, s_out = sem("scaled"), sem("merged"), sem("stored")

        with nc.Block() as block:
            @block.sync
            def _(sp):
                sp.dma_start(ident_sb[:], ident).then_inc(s_const, 16)
                for i in L:
                    sp.dma_start(row[i][:], logits[i].partition_broadcast(P)).then_inc(s_ld[i], 16)
                    sp.dma_start(by_tile[i][:], logits[i].rearrange("(t p) -> t p", p=P)).then_inc(s_ld[i], 16)
                for i in L:
                    for k in range(KC):
                        sp.dma_start(base[i][k][:], base_t[i, k * P:(k + 1) * P, :]).then_inc(s_in[i], 16)
                        sp.dma_start(delta[i][k][:], delta_t[i, k * P:(k + 1) * P, :]).then_inc(s_in[i], 16)
                for i in L:
                    sp.wait_ge(s_frow, i + 1)
                    sp.dma_start(factors[i].rearrange("(t p) -> t p", p=P), factor_row[i][:]).then_inc(s_kept[i], 16)
                    sp.wait_ge(s_kept[i], 16)
                    sp.dma_start(spread[i][:], factors[i].partition_broadcast(P)).then_inc(s_spread[i], 16)
                for i in L:
                    for k in range(KC):
                        sp.wait_ge(s_done, i * KC + k + 1)
                        sp.dma_start(out[i, k * P:(k + 1) * P, :], base[i][k][:]).then_inc(s_out, 16)
                sp.wait_ge(s_out, B * KC * 16)

            @block.tensor
            def _(pe):
                pe.wait_ge(s_const, 16)
                for i in L:
                    pe.wait_ge(s_ld[i], 32)
                    pe.transpose(turn[i][:, 0:NT], by_tile[i][:], ident_sb[0:NT, 0:NT]).then_inc(s_turned, 1)
                for i in L:
                    pe.wait_ge(s_factor, i + 1)
                    pe.transpose(turn[i][0:NT, 128:128 + P], factor[i][:], ident_sb[:]).then_inc(s_back, 1)

            @block.scalar
            def _(act):
                for i in L:
                    act.wait_ge(s_turned, i + 1)
                    act.activation(col[i][:], turn[i][:, 0:NT], ACT.Copy).then_inc(s_col, 1)
                for i in L:
                    act.wait_ge(s_back, i + 1)
                    act.activation(factor_row[i][:], turn[i][0:NT, 128:128 + P], ACT.Copy).then_inc(s_frow, 1)

            @block.gpsimd
            def _(pool):
                pool.memset(before[:], 1.0).then_inc(s_tri, 1)
                pool.wait_ge(s_tri, 1)
                pool.affine_select(out=before[:], in_=before[:], compare_op=ALU.is_gt, fill=0.0, base=0,
                                   pattern=[[-1, P]], channel_multiplier=1).then_inc(s_before, 1)

            @block.vector
            def _(dve):
                for i in L:
                    dve.memset(counts[i][:], 0.0).then_inc(s_zero, 1)
                dve.wait_ge(s_zero, B)
                dve.wait_ge(s_before, 1)
                step = Chain(dve, s_step)
                for i in L:
                    dve.wait_ge(s_ld[i], 32)
                    dve.wait_ge(s_col, i + 1)
                    for t in range(NT):
                        me = col[i][:, t:t + 1]
                        here = slice(t * P, (t + 1) * P)
                        if t > 0:
                            step.link(dve.tensor_scalar(scratch[:, 0:t * P], row[i][:, 0:t * P], me, 0.0,
                                                        ALU.is_ge, ALU.add, accum_out=counts[i][:, t, 0:1]))
                        if t < NT - 1:
                            step.link(dve.tensor_scalar(scratch[:, (t + 1) * P:N], row[i][:, (t + 1) * P:N], me, 0.0,
                                                        ALU.is_gt, ALU.add, accum_out=counts[i][:, t, 1:2]))
                        step.link(dve.scalar_tensor_tensor(out=tie[:], in0=row[i][:, here], scalar=me,
                                                           in1=before[:], op0=ALU.is_equal, op1=ALU.mult))
                        step.link(dve.scalar_tensor_tensor(out=scratch[:, here], in0=row[i][:, here], scalar=me,
                                                           in1=tie[:], op0=ALU.is_gt, op1=ALU.add,
                                                           accum_out=counts[i][:, t, 2:3]))
                    dve.tensor_reduce(rank[i][:], counts[i][:], AX.X, ALU.add).then_inc(s_rank, 1)
                    dve.wait_ge(s_rank, i + 1)
                    dve.scalar_tensor_tensor(out=factor[i][:], in0=rank[i][:], scalar=float(KEPT), in1=col[i][:],
                                             op0=ALU.is_lt, op1=ALU.mult).then_inc(s_factor, 1)
                for i in L:
                    dve.wait_ge(s_in[i], 2 * KC * 16)
                    dve.wait_ge(s_spread[i], 16)
                    for k in range(KC):
                        dve.tensor_tensor(delta[i][k][:], delta[i][k][:], spread[i][:], ALU.mult).then_inc(s_scaled, 1)
                        dve.wait_ge(s_scaled, i * KC + k + 1)
                        dve.tensor_tensor(base[i][k][:], base[i][k][:], delta[i][k][:], ALU.add).then_inc(s_done, 1)


def build(nc, a, out):
    qk_hi = nc.dram_tensor("qk_hi", (B, 4 * C, N), F32).ap()
    qk_lo = nc.dram_tensor("qk_lo", (B, 4 * C, N), F32).ap()
    v_rows = nc.dram_tensor("v_rows", (B * N, 2 * C), F32).ap()
    norm_and_project(nc, a["x"], a["wqk"], a["wv"], a["gmat"], qk_hi, qk_lo, v_rows)
    o_rows = nc.dram_tensor("o_rows", (VD, 1 + B * H0, N), F32).ap()
    differential_attention(nc, qk_hi, qk_lo, v_rows, [a[f"lambda_{n}"] for n in ("q1", "k1", "q2", "k2")],
                           a["ident"], a["fold"], o_rows)
    t_t = nc.dram_tensor("t_t", (B, C, N), F32).ap()
    a_t = nc.dram_tensor("a_t", (B, C, N), F32).ap()
    qk1_hi = nc.dram_tensor("qk1_hi", (B, 2 * C, N), F32).ap()
    qk1_lo = nc.dram_tensor("qk1_lo", (B, 2 * C, N), F32).ap()
    v1_rows = nc.dram_tensor("v1_rows", (B, N, C), F32).ap()
    head_norm_and_layer1_inputs(nc, a, o_rows, t_t, a_t, qk1_hi, qk1_lo, v1_rows)
    o1_t = nc.dram_tensor("o1_t", (B, C, N), F32).ap()
    causal_attention(nc, qk1_hi, qk1_lo, v1_rows, a["ident"], o1_t)
    t2_t = nc.dram_tensor("t2_t", (B, C, N), F32).ap()
    recurrence_gate_and_ffn(nc, a, o1_t, a_t, t_t, t2_t)
    logits = nc.dram_tensor("logits", (B, N), F32).ap()
    factors = nc.dram_tensor("factors", (B, N), F32).ap()
    base_t = nc.dram_tensor("base_t", (B, C, N), F32).ap()
    delta_t = nc.dram_tensor("delta_t", (B, C, N), F32).ap()
    routed_ffn(nc, a, t2_t, logits, base_t, delta_t)
    select_and_merge(nc, logits, factors, a["ident"], base_t, delta_t, out)


def layout(inputs):
    import numpy as np

    def tiles(w):
        w = np.asarray(w)
        return np.ascontiguousarray(w.reshape(-1, P, w.shape[1]).transpose(1, 0, 2))

    def columns(v):
        return np.ascontiguousarray(np.asarray(v).reshape(-1, P).T)

    a = {}
    a["x"] = np.ascontiguousarray(np.asarray(inputs["x"]).reshape(B, C, N))
    q_w, k_w, v_w = (np.asarray(inputs[f"L0_conv_{n}_w"]) for n in "qkv")
    a["wqk"] = tiles(np.concatenate([q_w, k_w]).T)
    a["wv"] = tiles(v_w.T)
    for n in ("q1", "k1", "q2", "k2"):
        a[f"lambda_{n}"] = np.ascontiguousarray(inputs[f"L0_conv_lambda_{n}"])
    a["ident"] = np.eye(P, dtype=np.float32)
    a["fold"] = np.concatenate([np.eye(VD, dtype=np.float32)] * 2)
    f = {k: np.asarray(v) for k, v in inputs.items()}
    a["out_w"] = tiles(f["L0_conv_out_w"].T)
    a["rms_scale"] = np.tile(f["L0_conv_rms_scale"].reshape(VD, 1), (2, 1))
    a["wqk1"] = tiles(f["L1_attn_qkv_w"][:, 0:2 * C])
    a["wv1"] = tiles(f["L1_attn_qkv_w"][:, 2 * C:])
    a["qk_bias1"] = np.ascontiguousarray(f["L1_attn_qkv_b"][0:2 * C].reshape(-1, P).T)
    a["v_bias1"] = np.ascontiguousarray(f["L1_attn_qkv_b"][2 * C:])
    of_head = (np.arange(2 * C)[:, None] // VD == np.arange(H0)[None, :]).astype(np.float32)
    a["to_heads"] = tiles(of_head / np.float32(VD))
    a["from_heads"] = np.ascontiguousarray(of_head.reshape(-1, P, H0).transpose(2, 0, 1))
    a["mean_mat"] = np.full((P, P), 1.0 / C, np.float32)
    for n in ("o_w", "rq_w", "rk_w", "rv_w", "ro_w", "cg_w", "ffn_w1", "ffn_w2"):
        a[n] = tiles(f[f"L1_attn_{n}"])
    for n in ("o_b", "rq_b", "rk_b", "ro_b", "cg_b", "ffn_b1", "ffn_b2", "ln1_g", "ln1_b", "ln2_g", "ln2_b",
              "ln3_g", "ln3_b"):
        a[n] = columns(f[f"L1_attn_{n}"])
    a["rv_b"] = f["L1_attn_rv_b"]
    for n in ("w1", "w2", "wr"):
        a[n] = tiles(f[f"L1_ffn_{n}"])
    a["wr"] = a["wr"].reshape(P, KC)
    a["br"] = f["L1_ffn_br"].reshape(1, 1)
    a["b1"], a["b2"] = columns(f["L1_ffn_b1"]), columns(f["L1_ffn_b2"])
    group = np.arange(P) // 8
    a["gmat"] = (group[:, None] == group[None, :]).astype(np.float32) / np.float32(8)
    return a


def kernel(**inputs):
    import numpy as np
    import concourse.bacc as bacc
    from concourse import mybir as mb
    from concourse.bass_utils import run_bass_kernel_spmd as run

    nc = bacc.Bacc("TRN2", target_bir_lowering=False, num_devices=1)
    arrays, a = {}, {}
    for name, value in layout(inputs).items():
        arrays[f"in_{name}"] = value
        a[name] = nc.dram_tensor(f"in_{name}", value.shape, mb.dt.from_np(value.dtype), kind="ExternalInput").ap()
    out = nc.dram_tensor("out", (B, C, N), F32, kind="ExternalOutput").ap()
    build(nc, a, out)
    r = run(nc, [arrays], core_ids=[0])
    return r.results[0]["out"].reshape(B, C, 48, 48)
```

```python
import math
from contextlib import ExitStack

import concourse.bass as bass
from concourse import mybir

F32 = mybir.dt.float32
F32R = mybir.dt.float32r
BF16 = mybir.dt.bfloat16
ALU = mybir.AluOpType
ACT = mybir.ActivationFunctionType
AX = mybir.AxisListType

P = 128
B = 2
C = 256
KC = C // P
N = 48 * 48
T = 384
NC = N // T
SUB = T // P
NT = N // P
H0 = 8
HD = 32
VD = 2 * HD
GN_EPS = 1e-5
LN_EPS = 1e-5
EPS_REC = 1e-6
GN_STEPS = 6
LAMBDA_INIT = 0.8 - 0.6 * math.exp(-0.3)


class Chain:

    def __init__(self, eng, sem, base=0):
        self.eng, self.sem, self.base, self.n = eng, sem, base, 0

    def link(self, ins, pad=None):
        self.n += 1
        ins.then_inc(self.sem, 1)
        self.eng.wait_ge(self.sem, self.base + self.n)
        if pad is not None:
            self.eng.memset(pad[:], 0.0)


def tools(nc, ctx, tag):
    def sb(name, shape, dt=F32):
        return ctx.enter_context(nc.sbuf_tensor(f"{tag}_{name}", shape, dt))

    def ps(name, shape):
        return ctx.enter_context(nc.psum_tensor(f"{tag}_{name}", shape, F32))

    used = []

    def sem(name):
        used.append(ctx.enter_context(nc.semaphore(f"{tag}_{name}")))
        return used[-1]

    def clear():
        with nc.Block() as block:
            @block.gpsimd
            def _(pool):
                for s in used:
                    pool.sem_clear(s)
    ctx.callback(clear)
    return sb, ps, sem


def norm_and_project(nc, x, wqk, wv, gmat, qk_hi, qk_lo, v_rows):
    MQK = 4 * C // P
    QB, VB = 4, 3
    with ExitStack() as ctx:
        sb, ps, sem = tools(nc, ctx, "proj")
        x_sb = sb("x", [P, KC, N])
        wqk_sb = sb("wqk", [P, KC, 4 * C])
        wv_sb = sb("wv", [P, KC, 2 * C])
        g_sb = sb("g", [P, P])
        stats = sb("stats", [P, KC, NC, 6])
        mv = sb("mv", [P, KC, 2])
        dev = sb("dev", [P, KC])
        dev2 = sb("dev2", [P, KC])
        spread = sb("spread", [P, KC])
        gmean = sb("gmean", [P, KC])
        std = sb("std", [P, KC])
        rstd = sb("rstd", [P, KC])
        shift = sb("shift", [P, KC])
        eps = sb("eps", [P, 1])
        pad = sb("pad", [P, 1])
        xn = [sb(f"xn{i}", [P, KC, T]) for i in range(2)]
        hi = [sb(f"hi{i}", [P, MQK, T], F32R) for i in range(2)]
        lo = [sb(f"lo{i}", [P, MQK, T], F32R) for i in range(2)]
        vst = [sb(f"vst{i}", [P, SUB, 2 * C]) for i in range(2)]
        qk_ps = [ps(f"qk{i}", [P, 512]) for i in range(QB)]
        v_ps = [ps(f"v{i}", [P, 512]) for i in range(VB)]
        gn_ps = ps("gn", [P, 512])
        s_w, s_x = sem("w"), sem("x_loaded")
        s_gn, s_mean, s_spread, s_gmean, s_gvar, s_std = (sem(n) for n in (
            "gn_step", "mean_ready", "spread_ready", "gmean_mm", "gvar_mm", "std_ready"))
        s_xn, s_qk, s_v = sem("xn_ready"), sem("qk_mm"), sem("v_mm")
        s_hi, s_lo, s_vst = sem("hi_done"), sem("lo_done"), sem("v_staged")
        s_out = [sem(f"stored{i}") for i in range(2)]
        s_eps = sem("eps")
        OUTS = 48

        with nc.Block() as block:
            @block.sync
            def _(sp):
                for i in range(2):
                    sp.sem_inc(s_out[i], 1)
                sp.dma_start(g_sb[:], gmat).then_inc(s_w, 16)
                sp.dma_start(wqk_sb[:], wqk).then_inc(s_w, 16)
                sp.dma_start(wv_sb[:], wv).then_inc(s_w, 16)
                with sp.Fori(0, B) as b:
                    sp.wait_ge(s_xn, b * NC * KC + 1)
                    sp.dma_start(x_sb[:], x.rearrange("b (k p) n -> p (b k) n", p=P)[
                        :, bass.ds(b * KC, KC), :]).then_inc(s_x, 16)
                    with sp.Fori(0, NC // 2) as i:
                        for par in range(2):
                            g = b * NC + i * 2 + par
                            cols = bass.ds((i * 2 + par) * T, T)
                            sp.wait_ge(s_lo, g * MQK + MQK + QB)
                            sp.dma_start(qk_hi.rearrange("b (m p) n -> p (b m) n", p=P)[
                                :, bass.ds(b * MQK, MQK), cols], hi[par][:].bitcast(F32)).then_inc(s_out[par], 16)
                            sp.dma_start(qk_lo.rearrange("b (m p) n -> p (b m) n", p=P)[
                                :, bass.ds(b * MQK, MQK), cols], lo[par][:].bitcast(F32)).then_inc(s_out[par], 16)
                            sp.wait_ge(s_vst, g * SUB + SUB + VB)
                            sp.dma_start(v_rows.rearrange("(t p) c -> p t c", p=P)[
                                :, bass.ds(g * SUB, SUB), :], vst[par][:]).then_inc(s_out[par], 16)
                for i in range(2):
                    sp.wait_ge(s_out[i], B * NC // 2 * OUTS + 1)

            @block.tensor
            def _(pe):
                pe.sem_inc(s_v, 2 * SUB)
                pe.wait_ge(s_w, 48)
                with pe.Fori(0, B) as b:
                    pe.wait_ge(s_mean, b + 1)
                    pe.matmul(gn_ps[:, 0:KC], g_sb[:], mv[:, :, 0], start=True, stop=True).then_inc(s_gmean, 1)
                    pe.wait_ge(s_spread, b + 1)
                    pe.matmul(gn_ps[:, KC:2 * KC], g_sb[:], spread[:], start=True, stop=True).then_inc(s_gvar, 1)
                    with pe.Fori(0, NC // 2) as i:
                        for par in range(2):
                            g = b * NC + i * 2 + par
                            pe.wait_ge(s_xn, (g + 1) * KC + 1)
                            for m in range(MQK):
                                pe.wait_ge(s_lo, g * MQK + m + 1)
                                for k in range(KC):
                                    mm = pe.matmul(qk_ps[m % QB][:, 0:T], wqk_sb[:, k, m * P:(m + 1) * P],
                                                   xn[par][:, k, :], start=k == 0, stop=k == KC - 1)
                                mm.then_inc(s_qk, 1)
                            for s in range(SUB):
                                pe.wait_ge(s_vst, g * SUB + s + 1)
                                for k in range(KC):
                                    mm = pe.matmul(v_ps[s][:, :], xn[par][:, k, s * P:(s + 1) * P],
                                                   wv_sb[:, k, :], start=k == 0, stop=k == KC - 1)
                                mm.then_inc(s_v, 1)

            @block.scalar
            def _(act):
                act.sem_inc(s_vst, VB)
                with act.Fori(0, B) as b:
                    act.wait_ge(s_gvar, b + 1)
                    act.wait_ge(s_eps, 1)
                    act.activation(std[:], gn_ps[:, KC:2 * KC], ACT.Sqrt, bias=eps[:, 0:1]).then_inc(s_std, 1)
                    with act.Fori(0, NC // 2) as i:
                        for par in range(2):
                            g = b * NC + i * 2 + par
                            act.wait_ge(s_out[par], (b * (NC // 2) + i) * OUTS + 1)
                            for m in range(MQK):
                                act.wait_ge(s_qk, g * MQK + m + 1)
                                act.activation(hi[par][:, m, :], qk_ps[m % QB][:, 0:T], ACT.Copy).then_inc(s_hi, 1)
                            for s in range(SUB):
                                act.wait_ge(s_v, g * SUB + s + 1 + 2 * SUB)
                                act.activation(vst[par][:, s, :], v_ps[s][:, :], ACT.Copy).then_inc(s_vst, 1)

            @block.vector
            def _(dve):
                dve.sem_inc(s_lo, QB)
                dve.sem_inc(s_xn, 1)
                dve.memset(eps[:], GN_EPS).then_inc(s_eps, 1)
                with dve.Fori(0, B) as b:
                    step = Chain(dve, s_gn, b * GN_STEPS)
                    dve.wait_ge(s_x, (b + 1) * 16)
                    for k in range(KC):
                        for c in range(NC):
                            ins = dve.bn_stats(stats[:, k, c, :], x_sb[:, k, c * T:(c + 1) * T])
                    step.link(ins, pad=pad)
                    for k in range(KC):
                        ins = dve.bn_aggr(mv[:, k, :], stats[:, k, :, :])
                    ins.then_inc(s_mean, 1)
                    dve.wait_ge(s_mean, b + 1)
                    dve.wait_ge(s_gmean, b + 1)
                    step.link(dve.tensor_copy(gmean[:], gn_ps[:, 0:KC]))
                    step.link(dve.tensor_tensor(dev[:], mv[:, :, 0], gmean[:], ALU.subtract))
                    step.link(dve.tensor_tensor(dev2[:], dev[:], dev[:], ALU.mult))
                    dve.tensor_tensor(spread[:], dev2[:], mv[:, :, 1], ALU.add).then_inc(s_spread, 1)
                    dve.wait_ge(s_std, b + 1)
                    step.link(dve.reciprocal(rstd[:], std[:]))
                    step.link(dve.scalar_tensor_tensor(out=shift[:], in0=gmean[:], scalar=-1.0, in1=rstd[:],
                                                       op0=ALU.mult, op1=ALU.mult), pad=pad)
                    assert step.n == GN_STEPS
                    with dve.Fori(0, NC // 2) as i:
                        for par in range(2):
                            c = i * 2 + par
                            g = b * NC + c
                            dve.wait_ge(s_v, g * SUB + SUB)
                            for k in range(KC):
                                dve.tensor_scalar(xn[par][:, k, :], x_sb[:, k, bass.ds(c * T, T)],
                                                  rstd[:, k:k + 1], shift[:, k:k + 1],
                                                  ALU.mult, ALU.add).then_inc(s_xn, 1)
                            for m in range(MQK):
                                dve.wait_ge(s_qk, g * MQK + m + 1)
                                dve.wait_ge(s_hi, g * MQK + m + 1)
                                dve.tensor_tensor(lo[par][:, m, :], qk_ps[m % QB][:, 0:T],
                                                  hi[par][:, m, :].bitcast(F32), ALU.subtract).then_inc(s_lo, 1)


def differential_attention(nc, qk_hi, qk_lo, v_rows, lambdas, ident, fold, o_rows):
    PARTS = 3
    ROWS = PARTS * HD
    HEADS = B * H0
    STEPS = NT
    BANKS = 3
    PBUF = 6
    LOADS = 2 * 2 * PARTS + 1
    UNITS = 2 * SUB * NC
    ROWS_STEP = STEPS - 2
    SUMS_STEP, COMBINE_STEP = 3, 9
    SCALE = HD ** -0.5
    on_dve = [g for g in range(STEPS) if g % 4 == 3]
    on_pool = [g for g in range(STEPS) if g not in on_dve]
    ND, NPOOL = len(on_dve) - 1, len(on_pool) - 1
    with ExitStack() as ctx:
        sb, ps, sem = tools(nc, ctx, "diff")
        ks = [[sb(f"ks{i}{j}", [ROWS + 1, N], F32R) for j in range(2)] for i in range(2)]
        qs = [[sb(f"qs{i}{j}", [ROWS + 1, N], F32R) for j in range(2)] for i in range(2)]
        vs = [sb(f"vs{i}", [P, NT, 2, VD]) for i in range(2)]
        q_now = sb("q_now", [ROWS, 2, T], F32R)
        probs = [sb(f"probs{i}", [P, 2 * T]) for i in range(PBUF)]
        run_pool = sb("run_pool", [P, 2 * T])
        sum_pool = sb("sum_pool", [P, 2 * T])
        run_dve = sb("run_dve", [P, 2 * T])
        sum_dve = sb("sum_dve", [P, 2 * T])
        maxes = sb("maxes", [P, 2 * SUB, NC])
        neg_max = sb("neg_max", [P, 2 * SUB])
        out_sb = sb("out", [P, T])
        recip = sb("recip", [P, T])
        normed = sb("normed", [P, T])
        combined = sb("combined", [VD, T])
        ones = sb("ones", [P, VD])
        ident_sb = sb("ident", [P, P])
        fold_sb = sb("fold", [P, VD])
        lam_in = sb("lam_in", [P, 4, C])
        lam_prod = sb("lam_prod", [P, 2, C])
        lam_sum = sb("lam_sum", [P, 2, H0])
        lam_exp = sb("lam_exp", [P, 2, H0])
        lam_diff = sb("lam_diff", [P, H0])
        neg_lam = sb("neg_lam", [P, HEADS])
        scores = [ps(f"scores{i}", [P, 512]) for i in range(BANKS)]
        max_ps = [ps(f"max{i}", [P, 512]) for i in range(BANKS)]
        out_ps = ps("out_ps", [P, 512])
        misc = ps("misc", [P, 512])
        s_const, s_ones, s_lam, s_lamexp, s_lamready = (sem(n) for n in (
            "const", "ones", "lam_step", "lam_exp", "lam_ready"))
        s_ld = [sem(f"loaded{i}") for i in range(2)]
        s_vs, s_qnow = sem("values_ready"), sem("q_now_ready")
        s_st, s_exp, s_pv, s_accp, s_accd = (sem(n) for n in (
            "scores_mm", "exp_done", "pv_mm", "sum_pool_done", "sum_dve_done"))
        s_mx, s_red, s_neg, s_rows, s_row = (sem(n) for n in (
            "max_mm", "max_taken", "neg_max_ready", "rows_mm", "rows_placed"))
        s_oev, s_l, s_rec, s_norm, s_comb, s_cout, s_st_o = (sem(n) for n in (
            "out_taken", "sums_mm", "recip_done", "normed_ready", "combined_mm", "combined_taken", "stored"))

        busy = [SUMS_STEP + 1 + s for s in range(SUB)] + [g + 1 for g in on_dve[1:]]
        per_step = [1 if g in busy else 3 for g in range(ROWS_STEP)]
        per_step[0] = per_step[COMBINE_STEP - 2] = 2
        assert sum(per_step) == UNITS

        def units_at(g):
            return list(range(sum(per_step[:g]), sum(per_step[:g + 1])))

        with nc.Block() as block:
            @block.sync
            def _(sp):
                sp.dma_start(ident_sb[:], ident).then_inc(s_const, 16)
                sp.dma_start(fold_sb[:], fold).then_inc(s_const, 16)
                for i, l in enumerate(lambdas):
                    sp.dma_start(lam_in[:, i, :], l.rearrange("h d -> (h d)").partition_broadcast(P)).then_inc(s_const, 16)

                qh = qk_hi.rearrange("b (h j d) n -> (b h) j d n", j=2, d=HD)
                ql = qk_lo.rearrange("b (h j d) n -> (b h) j d n", j=2, d=HD)

                def load(par, b, h):
                    for j in range(2):
                        for dst, kind, parts in ((qs, 0, (qh, qh, ql)), (ks, 1, (qh, ql, qh))):
                            for r, src in enumerate(parts):
                                sp.dma_start(dst[par][j][r * HD:(r + 1) * HD, :].bitcast(F32),
                                             src[bass.ds(b * 2 * H0 + kind * H0 + h, 1), j, :, :].rearrange(
                                                 "a d n -> (a d) n")).then_inc(s_ld[par], 16)
                    sp.dma_start(vs[par][:, :, 0, :], v_rows.rearrange("(t p) c -> p t c", p=P)[
                        :, bass.ds(b * NT, NT), bass.ds(h * VD, VD)]).then_inc(s_ld[par], 16)

                with sp.Fori(0, B) as b:
                    with sp.Fori(0, H0 // 2) as i:
                        for par in range(2):
                            sp.wait_ge(s_comb, (b * H0 + i * 2 + par) * NC + NC + 1)
                            load(par, b, i * 2 + par)
                sp.wait_ge(s_comb, HEADS * NC + NC + 1)
                load(0, 0, 0)
                sp.wait_ge(s_ld[0], (HEADS // 2 + 1) * LOADS * 16)
                sp.wait_ge(s_ld[1], HEADS // 2 * LOADS * 16)

            @block.tensor
            def _(pe):
                pe.sem_inc(s_comb, 2 * NC)
                pe.sem_inc(s_mx, 2 * UNITS)
                pe.sem_inc(s_st, 2 * STEPS)
                pe.sem_inc(s_pv, PBUF + STEPS)
                pe.sem_inc(s_rows, 1)
                pe.wait_ge(s_const, 16 * 6)
                pe.wait_ge(s_ones, 5)

                def score_step(par, q, c, g):
                    if g == 0:
                        pe.wait_ge(s_row, q * 2 + 2)
                    for j in range(2):
                        pe.wait_ge(s_exp, (q * STEPS + g) * 2 + j + 1)
                        pe.matmul(scores[(2 * g + j) % BANKS][:, 0:T], ks[par][j][:, g * P:(g + 1) * P],
                                  qs[par][j][:, bass.ds(c * T, T)], start=True, stop=True).then_inc(s_st, 1)

                def max_unit(par, q1, u):
                    j, s, k = u // (SUB * NC), u // NC % SUB, u % NC
                    if u % (SUB * NC) == 0:
                        pe.wait_ge(s_qnow, q1 * 2 + j + 1)
                    pe.wait_ge(s_red, q1 * UNITS + u + 1)
                    pe.matmul(max_ps[u % BANKS][:, 0:T], q_now[:, j, s * P:(s + 1) * P],
                              ks[par][j][0:ROWS, k * T:(k + 1) * T], start=True, stop=True).then_inc(s_mx, 1)

                def pv_step(par, q, g, n=None):
                    if g == 0 and n is not None:
                        pe.wait_ge(s_vs, n + 1)
                    if g == 0:
                        pe.wait_ge(s_oev, q)
                    pe.wait_ge(s_exp, (q * STEPS + g) * 2 + 2 + BANKS)
                    for j in range(2):
                        mm = pe.matmul(out_ps[64 * j:64 * j + VD, 0:T], vs[par][:, g, j, :],
                                       probs[g % PBUF][:, j * T:(j + 1) * T], start=g == 0, stop=g == STEPS - 1,
                                       tile_position=(0, 64 * j))
                    mm.then_inc(s_pv, 1)

                def rows(q1, first=False):
                    if not first:
                        pe.wait_ge(s_cout, q1 - 1)
                    pe.wait_ge(s_neg, q1 + 1)
                    for j in range(2):
                        for s in range(SUB):
                            mm = pe.matmul(misc[32 * j:32 * j + 1, s * P:(s + 1) * P],
                                           neg_max[:, j * SUB + s:j * SUB + s + 1], ident_sb[:],
                                           start=True, stop=True, tile_position=(0, 32 * j))
                    mm.then_inc(s_rows, 1)

                def sums(q):
                    pe.wait_ge(s_row, q * 2 + 4)
                    pe.wait_ge(s_accp, (q + 2) * NPOOL)
                    pe.wait_ge(s_accd, (q + 2) * ND)
                    for j in range(2):
                        for k, part in enumerate((sum_pool, sum_dve)):
                            mm = pe.matmul(misc[64 * j:64 * j + VD, 0:T], ones[:],
                                           part[:, j * T:(j + 1) * T], start=k == 0, stop=k == 1,
                                           tile_position=(0, 64 * j))
                    mm.then_inc(s_l, 1)

                def combine(q):
                    pe.wait_ge(s_norm, q + 2)
                    pe.matmul(misc[0:VD, 0:T], fold_sb[:], normed[:], start=True, stop=True).then_inc(s_comb, 1)

                def slot(par, q, c, next_par, n=None):
                    for g in range(STEPS):
                        units = units_at(g)
                        before, between = (units[:1], units[1:2]) if len(units) == 3 else ([], units[:1])
                        for u in before:
                            max_unit(next_par, q + 1, u)
                        score_step(par, q, c, g)
                        for u in between:
                            max_unit(next_par, q + 1, u)
                        if g > 0:
                            pv_step(par, q, g - 1, n)
                        for u in units[len(before + between):]:
                            max_unit(next_par, q + 1, u)
                        if g == SUMS_STEP:
                            sums(q - 1)
                        if g == COMBINE_STEP:
                            combine(q - 1)
                        if g == ROWS_STEP:
                            rows(q + 1)
                    pv_step(par, q, STEPS - 1)

                pe.wait_ge(s_ld[0], LOADS * 16)
                for u in range(UNITS):
                    max_unit(0, 1, u)
                rows(1, first=True)
                with pe.Fori(0, HEADS // 2) as i:
                    for par in range(2):
                        n = i * 2 + par
                        slot(par, n * NC + 1, 0, par, n)
                        with pe.Fori(1, NC - 1) as c:
                            slot(par, n * NC + c + 1, c, par)
                        pe.wait_ge(s_ld[1 - par], (i + 1 + par) * LOADS * 16)
                        slot(par, n * NC + NC, NC - 1, 1 - par)
                sums(HEADS * NC)
                combine(HEADS * NC)

            @block.scalar
            def _(act):
                act.sem_inc(s_exp, BANKS + 2 * STEPS)
                act.sem_inc(s_row, 2)
                act.sem_inc(s_qnow, 2)
                act.sem_inc(s_st_o, 1)

                def stage_queries(par, q1, c1, j):
                    act.wait_ge(s_mx, q1 * UNITS + (j + 1) * (UNITS // 2))
                    act.activation(q_now[:, j, :], qs[par][j][0:ROWS, bass.ds(c1 * T, T)].bitcast(F32),
                                   ACT.Copy).then_inc(s_qnow, 1)

                def place_rows(par, q1, c1):
                    act.wait_ge(s_rows, q1 + 1)
                    act.activation(qs[par][0][ROWS:ROWS + 1, bass.ds(c1 * T, T)], misc[0:1, 0:T],
                                   ACT.Copy).then_inc(s_row, 1)

                def take_out(q):
                    act.wait_ge(s_norm, q + 1)
                    act.wait_ge(s_pv, (q + 1) * STEPS + PBUF)
                    act.activation(out_sb[:], out_ps[:, 0:T], ACT.Copy).then_inc(s_oev, 1)

                def take_combined(q):
                    act.wait_ge(s_comb, q + 1 + 2 * NC)
                    act.wait_ge(s_st_o, q * 16 + 1)
                    act.activation(combined[:], misc[0:VD, 0:T], ACT.Copy).then_inc(s_cout, 1)

                def store_combined(q, n, c):
                    act.wait_ge(s_cout, q + 1)
                    act.dma_start(o_rows[:, bass.ds(n + 1, 1), bass.ds(c * T, T)], combined[:]).then_inc(s_st_o, 16)

                def slot(par, q, next_par, c1, n_prev, c_prev):
                    for g in range(STEPS):
                        if g == 0:
                            stage_queries(next_par, q + 1, c1, 0)
                        if UNITS // 2 - 1 in units_at(g):
                            stage_queries(next_par, q + 1, c1, 1)
                        act.wait_ge(s_pv, q * STEPS + g + 1)
                        back = (g - PBUF) % STEPS
                        lap = 1 if g >= PBUF else 0
                        if back in on_pool:
                            act.wait_ge(s_accp, (q + lap) * NPOOL + max(on_pool.index(back), 1))
                        else:
                            act.wait_ge(s_accd, (q + lap) * ND + max(on_dve.index(back), 1))
                        for j in range(2):
                            act.wait_ge(s_st, (q * STEPS + g) * 2 + j + 1)
                            act.activation(probs[g % PBUF][:, j * T:(j + 1) * T],
                                           scores[(2 * g + j) % BANKS][:, 0:T], ACT.Exp, scale=SCALE
                                           ).then_inc(s_exp, 1)
                        if g == 0:
                            take_out(q - 1)
                        if g == COMBINE_STEP + 1:
                            take_combined(q - 1)
                        if g == COMBINE_STEP + 2:
                            store_combined(q - 1, n_prev, c_prev)
                        if g == ROWS_STEP:
                            place_rows(next_par, q + 1, c1)

                act.wait_ge(s_lam, 2)
                act.activation(lam_exp[:], lam_sum[:], ACT.Exp).then_inc(s_lamexp, 1)
                act.wait_ge(s_ld[0], LOADS * 16)
                for j in range(2):
                    act.activation(q_now[:, j, :], qs[0][j][0:ROWS, 0:T].bitcast(F32), ACT.Copy).then_inc(s_qnow, 1)
                place_rows(0, 1, 0)
                with act.Fori(0, HEADS // 2) as i:
                    for par in range(2):
                        n = i * 2 + par
                        slot(par, n * NC + 1, par, 1, n - 1, NC - 1)
                        with act.Fori(1, NC - 1) as c:
                            slot(par, n * NC + c + 1, par, c + 1, n, c - 1)
                        act.wait_ge(s_ld[1 - par], (i + 1 + par) * LOADS * 16)
                        slot(par, n * NC + NC, 1 - par, 0, n, NC - 2)
                take_out(HEADS * NC)
                take_combined(HEADS * NC)
                store_combined(HEADS * NC, HEADS - 1, NC - 1)
                act.wait_ge(s_st_o, (HEADS * NC + 1) * 16 + 1)

            @block.vector
            def _(dve):
                dve.sem_inc(s_red, BANKS + UNITS)
                dve.sem_inc(s_neg, 1)
                dve.sem_inc(s_accd, 2 * ND)
                dve.sem_inc(s_norm, 1)
                for par in range(2):
                    for j in range(2):
                        ins = dve.memset(ks[par][j][ROWS:ROWS + 1, :].bitcast(F32), 1.0)
                ins.then_inc(s_ones, 1)
                dve.memset(ones[:], 1.0).then_inc(s_ones, 1)
                dve.memset(sum_dve[:], 1.0).then_inc(s_ones, 1)
                dve.memset(out_ps[:, 0:T], 0.0).then_inc(s_ones, 1)
                dve.wait_ge(s_const, 16 * 6)
                step = Chain(dve, s_lam)
                for i in range(2):
                    ins = dve.tensor_tensor(lam_prod[:, i, :], lam_in[:, 2 * i, :], lam_in[:, 2 * i + 1, :], ALU.mult)
                step.link(ins)
                step.link(dve.tensor_reduce(lam_sum[:], lam_prod[:].rearrange("p i (h d) -> p i h d", d=HD),
                                            AX.X, ALU.add))
                dve.wait_ge(s_lamexp, 1)
                step.link(dve.tensor_tensor(lam_diff[:], lam_exp[:, 1, :], lam_exp[:, 0, :], ALU.subtract))
                for b in range(B):
                    ins = dve.tensor_scalar(neg_lam[:, b * H0:(b + 1) * H0], lam_diff[:], -LAMBDA_INIT, None, ALU.add)
                step.link(ins)

                def max_unit(q1, u):
                    dve.wait_ge(s_mx, (q1 + 1) * UNITS + u + 1)
                    dve.tensor_reduce(maxes[:, u // NC:u // NC + 1, u % NC], max_ps[u % BANKS][:, 0:T], AX.X,
                                      ALU.max).then_inc(s_red, 1)

                def negate(q1):
                    dve.wait_ge(s_rows, q1)
                    dve.wait_ge(s_red, q1 * UNITS + UNITS + BANKS)
                    dve.tensor_reduce(neg_max[:], maxes[:], AX.X, ALU.max, negate=True).then_inc(s_neg, 1)

                def add_up(q, g):
                    i = on_dve.index(g)
                    if i == 0:
                        return
                    dve.wait_ge(s_exp, (q * STEPS + g) * 2 + 2 + BANKS)
                    dve.wait_ge(s_accd, (q + 1) * ND + i - 1)
                    acc = probs[on_dve[0] % PBUF] if i == 1 else run_dve
                    to = sum_dve if i == ND else run_dve
                    dve.tensor_tensor(to[:], acc[:], probs[g % PBUF][:], ALU.add).then_inc(s_accd, 1)

                def invert(q, s):
                    if s == 0:
                        dve.wait_ge(s_l, q + 1)
                        dve.wait_ge(s_norm, q + 1)
                    dve.reciprocal(recip[:, s * P:(s + 1) * P], misc[:, s * P:(s + 1) * P]).then_inc(s_rec, 1)

                def normalise(q):
                    dve.wait_ge(s_oev, q + 1)
                    dve.wait_ge(s_rec, (q + 1) * SUB)
                    dve.tensor_tensor(normed[:], out_sb[:], recip[:], ALU.mult).then_inc(s_norm, 1)

                def place_rows(par, q1, c1):
                    dve.wait_ge(s_rows, q1 + 1)
                    dve.tensor_copy(qs[par][1][ROWS:ROWS + 1, bass.ds(c1 * T, T)], misc[32:33, 0:T]
                                    ).then_inc(s_row, 1)

                def slot(q, next_par, c1):
                    for g in range(STEPS):
                        for u in units_at(g):
                            max_unit(q + 1, u)
                        if g - 1 in on_dve:
                            add_up(q, g - 1)
                        if 0 < g - SUMS_STEP <= SUB:
                            invert(q - 1, g - SUMS_STEP - 1)
                        if g == COMBINE_STEP - 2:
                            normalise(q - 1)
                        if g == ROWS_STEP - 1:
                            negate(q + 1)
                        if g == ROWS_STEP:
                            place_rows(next_par, q + 1, c1)

                for u in range(UNITS):
                    max_unit(1, u)
                negate(1)
                place_rows(0, 1, 0)
                with dve.Fori(0, HEADS // 2) as i:
                    for par in range(2):
                        n = i * 2 + par
                        dve.wait_ge(s_lam, 4)
                        dve.wait_ge(s_ld[par], (i + 1) * LOADS * 16)
                        dve.tensor_scalar(vs[par][:, :, 1, :], vs[par][:, :, 0, :], neg_lam[:, bass.ds(n, 1)],
                                          None, ALU.mult).then_inc(s_vs, 1)
                        with dve.Fori(1, NC) as c:
                            slot(n * NC + c, par, c)
                        slot(n * NC + NC, 1 - par, 0)
                for s in range(SUB):
                    invert(HEADS * NC, s)
                normalise(HEADS * NC)

            @block.gpsimd
            def _(pool):
                pool.sem_inc(s_accp, 2 * NPOOL)
                pool.memset(sum_pool[:], 1.0).then_inc(s_ones, 1)

                def slot(q):
                    for i, g in enumerate(on_pool):
                        if i == 0:
                            continue
                        pool.wait_ge(s_exp, (q * STEPS + g) * 2 + 2 + BANKS)
                        pool.wait_ge(s_accp, (q + 1) * NPOOL + i - 1)
                        acc = probs[on_pool[0] % PBUF] if i == 1 else run_pool
                        to = sum_pool if i == NPOOL else run_pool
                        pool.tensor_tensor(to[:], acc[:], probs[g % PBUF][:], ALU.add).then_inc(s_accp, 1)

                with pool.Fori(1, HEADS * NC + 1) as q:
                    slot(q)


def nth(c, lane):
    return c * B + lane + 1


def head_norm_and_layer1_inputs(nc, a, o_rows, t_rows, a_t, qk_hi, qk_lo, v_rows):
    MO = 2 * C // P
    MQK = 2 * C // P
    with ExitStack() as ctx:
        sb, ps, sem = tools(nc, ctx, "mid")
        L = range(B)
        wo = sb("wo", [P, MO, C])
        wqk = sb("wqk", [P, KC, 2 * C])
        wv = sb("wv", [P, KC, C])
        qk_bias = sb("qk_bias", [P, MQK])
        v_bias = sb("v_bias", [P, C])
        to_heads = sb("to_heads", [P, MO, H0])
        from_heads = sb("from_heads", [H0, MO, P])
        mean_mat = sb("mean_mat", [P, P])
        gain = sb("gain", [P, 1])
        eps = sb("eps", [P, 1])
        o_in = [sb(f"o_in{i}", [P, MO, T]) for i in L]
        x_in = [sb(f"x_in{i}", [P, KC, T]) for i in L]
        o_sq = [sb(f"o_sq{i}", [P, MO, T]) for i in L]
        h_std = [sb(f"h_std{i}", [H0, T]) for i in L]
        h_rstd = [sb(f"h_rstd{i}", [H0, T]) for i in L]
        o_norm = [sb(f"o_norm{i}", [P, MO, T]) for i in L]
        t = [sb(f"t{i}", [P, KC, T]) for i in L]
        dev = [sb(f"dev{i}", [P, KC, T]) for i in L]
        dev_sq = [sb(f"dev_sq{i}", [P, KC, T]) for i in L]
        std = [sb(f"std{i}", [P, T]) for i in L]
        rstd = [sb(f"rstd{i}", [P, T]) for i in L]
        ln = [sb(f"ln{i}", [P, KC, T]) for i in L]
        hi = [sb(f"hi{i}", [P, MQK, T], F32R) for i in L]
        lo = [sb(f"lo{i}", [P, MQK, T], F32R) for i in L]
        v_out = [sb(f"v_out{i}", [P, SUB, C]) for i in L]
        bank = [[ps(f"bank{i}{k}", [P, 512]) for k in range(4)] for i in L]
        s_w, s_eps, s_gain = sem("weights"), sem("eps"), sem("gain")
        s_ld = [sem(f"loaded{i}") for i in L]
        s_st_t = [sem(f"t_stored{i}") for i in L]
        s_st_q = [sem(f"qk_stored{i}") for i in L]
        s_st_v = [sem(f"v_stored{i}") for i in L]
        (s_osq, s_ms, s_hstd, s_hrstd, s_bc, s_onorm, s_y, s_t, s_mean, s_dev, s_dsq, s_var, s_std, s_rstd,
         s_ln, s_qk, s_hi, s_lo, s_v, s_vout) = (sem(n) for n in (
             "o_squared", "head_ms_mm", "head_std", "head_rstd", "head_rstd_mm", "o_normed", "y_mm", "t_ready",
             "mean_mm", "dev_ready", "dev_squared", "var_mm", "std_ready", "rstd_ready", "ln_ready", "qk_mm",
             "hi_done", "lo_done", "v_mm", "v_done"))

        with nc.Block() as block:
            @block.sync
            def _(sp):
                for i in L:
                    sp.sem_inc(s_st_t[i], 1)
                    sp.sem_inc(s_st_q[i], 1)
                    sp.sem_inc(s_st_v[i], 1)
                for dst, src in ((wo, a["out_w"]), (wqk, a["wqk1"]), (wv, a["wv1"]), (qk_bias, a["qk_bias1"]),
                                 (to_heads, a["to_heads"]), (from_heads, a["from_heads"]),
                                 (mean_mat, a["mean_mat"]), (gain, a["rms_scale"])):
                    sp.dma_start(dst[:], src).then_inc(s_w, 16)
                sp.dma_start(v_bias[:], a["v_bias1"].partition_broadcast(P)).then_inc(s_w, 16)
                with sp.Fori(0, NC) as c:
                    cols = bass.ds(c * T, T)
                    for i in L:
                        sp.wait_ge(s_t, nth(c, i))
                        for h in range(2):
                            sp.dma_start(o_in[i][h * VD:(h + 1) * VD, :, :],
                                         o_rows[:, bass.ds(1 + i * H0 + h, MO, step=2), cols]
                                         ).then_inc(s_ld[i], 16)
                        sp.dma_start(x_in[i][:], a["x"][i].rearrange("(k p) n -> p k n", p=P)[:, :, cols]
                                     ).then_inc(s_ld[i], 16)
                    for i in L:
                        sp.wait_ge(s_ln, nth(c, i))
                        sp.dma_start(t_rows[i].rearrange("(k p) n -> p k n", p=P)[:, :, cols], t[i][:]
                                     ).then_inc(s_st_t[i], 16)
                        sp.dma_start(a_t[i].rearrange("(k p) n -> p k n", p=P)[:, :, cols], ln[i][:]
                                     ).then_inc(s_st_t[i], 16)
                    for i in L:
                        sp.wait_ge(s_lo, nth(c, i) * MQK)
                        sp.dma_start(qk_hi[i].rearrange("(m p) n -> p m n", p=P)[:, :, cols],
                                     hi[i][:].bitcast(F32)).then_inc(s_st_q[i], 16)
                        sp.dma_start(qk_lo[i].rearrange("(m p) n -> p m n", p=P)[:, :, cols],
                                     lo[i][:].bitcast(F32)).then_inc(s_st_q[i], 16)
                    for i in L:
                        sp.wait_ge(s_vout, nth(c + 1, i))
                        sp.dma_start(v_rows[i].rearrange("(t p) c -> p t c", p=P)[:, bass.ds(c * SUB, SUB), :],
                                     v_out[i][:]).then_inc(s_st_v[i], 16)
                for i in L:
                    sp.wait_ge(s_st_t[i], NC * 32 + 1)
                    sp.wait_ge(s_st_q[i], NC * 32 + 1)
                    sp.wait_ge(s_st_v[i], NC * 16 + 1)

            @block.tensor
            def _(pe):
                pe.wait_ge(s_w, 16 * 9)
                with pe.Fori(0, NC) as c:
                    for i in L:
                        pe.wait_ge(s_osq, nth(c, i))
                        pe.wait_ge(s_vout, nth(c, i))
                        for m in range(MO):
                            mm = pe.matmul(bank[i][0][0:H0, 0:T], to_heads[:, m, :], o_sq[i][:, m, :],
                                           start=m == 0, stop=m == MO - 1)
                        mm.then_inc(s_ms, 1)
                    for i in L:
                        pe.wait_ge(s_hrstd, nth(c, i))
                        for m in range(MO):
                            mm = pe.matmul(bank[i][m][:, 0:T], from_heads[:, m, :], h_rstd[i][:],
                                           start=True, stop=True)
                        mm.then_inc(s_bc, 1)
                    for i in L:
                        pe.wait_ge(s_onorm, nth(c, i))
                        for h in range(KC):
                            for m in range(MO):
                                mm = pe.matmul(bank[i][h][:, 0:T], wo[:, m, h * P:(h + 1) * P],
                                               o_norm[i][:, m, :], start=m == 0, stop=m == MO - 1)
                        mm.then_inc(s_y, 1)
                    for i in L:
                        pe.wait_ge(s_t, nth(c + 1, i))
                        for k in range(KC):
                            mm = pe.matmul(bank[i][2][:, 0:T], mean_mat[:], t[i][:, k, :],
                                           start=k == 0, stop=k == KC - 1)
                        mm.then_inc(s_mean, 1)
                    for i in L:
                        pe.wait_ge(s_dsq, nth(c, i))
                        for k in range(KC):
                            mm = pe.matmul(bank[i][3][:, 0:T], mean_mat[:], dev_sq[i][:, k, :],
                                           start=k == 0, stop=k == KC - 1)
                        mm.then_inc(s_var, 1)
                    for i in L:
                        pe.wait_ge(s_ln, nth(c, i))
                        for m in range(MQK):
                            for k in range(KC):
                                mm = pe.matmul(bank[i][m][:, 0:T], wqk[:, k, m * P:(m + 1) * P], ln[i][:, k, :],
                                               start=k == 0, stop=k == KC - 1)
                            mm.then_inc(s_qk, 1)
                    for i in L:
                        pe.wait_ge(s_lo, nth(c, i) * MQK)
                        for s in range(SUB):
                            for k in range(KC):
                                mm = pe.matmul(bank[i][s][:, 0:C], ln[i][:, k, s * P:(s + 1) * P], wv[:, k, :],
                                               start=k == 0, stop=k == KC - 1)
                        mm.then_inc(s_v, 1)

            @block.scalar
            def _(act):
                act.wait_ge(s_eps, 1)
                act.wait_ge(s_w, 16 * 9)
                with act.Fori(0, NC) as c:
                    for i in L:
                        act.wait_ge(s_ld[i], (c + 1) * 48)
                        act.activation(o_sq[i][:], o_in[i][:], ACT.Square).then_inc(s_osq, 1)
                    for i in L:
                        act.wait_ge(s_ms, nth(c, i))
                        act.activation(h_std[i][:], bank[i][0][0:H0, 0:T], ACT.Sqrt,
                                       bias=eps[0:H0, 0:1]).then_inc(s_hstd, 1)
                    for i in L:
                        act.wait_ge(s_dev, nth(c, i))
                        act.activation(dev_sq[i][:], dev[i][:], ACT.Square).then_inc(s_dsq, 1)
                    for i in L:
                        act.wait_ge(s_var, nth(c, i))
                        act.activation(std[i][:], bank[i][3][:, 0:T], ACT.Sqrt, bias=eps[:, 0:1]).then_inc(s_std, 1)
                    for i in L:
                        act.wait_ge(s_st_q[i], c * 32 + 1)
                        for m in range(MQK):
                            act.wait_ge(s_qk, nth(c, i) * MQK - (MQK - 1) + m)
                            act.activation(hi[i][:, m, :], bank[i][m][:, 0:T], ACT.Identity,
                                           bias=qk_bias[:, m:m + 1]).then_inc(s_hi, 1)

            @block.vector
            def _(dve):
                dve.sem_inc(s_t, B)
                dve.sem_inc(s_vout, B)
                dve.memset(eps[:], LN_EPS).then_inc(s_eps, 1)
                dve.wait_ge(s_w, 16 * 9)
                dve.tensor_scalar(gain[:], gain[:], 1.0 - LAMBDA_INIT, None, ALU.mult).then_inc(s_gain, 1)
                dve.wait_ge(s_gain, 1)
                with dve.Fori(0, NC) as c:
                    for i in L:
                        dve.wait_ge(s_hstd, nth(c, i))
                        dve.reciprocal(h_rstd[i][:], h_std[i][:]).then_inc(s_hrstd, 1)
                    for i in L:
                        dve.wait_ge(s_bc, nth(c, i))
                        for m in range(MO):
                            ins = dve.scalar_tensor_tensor(out=o_norm[i][:, m, :], in0=o_in[i][:, m, :],
                                                           scalar=gain[:, 0:1], in1=bank[i][m][:, 0:T],
                                                           op0=ALU.mult, op1=ALU.mult)
                        ins.then_inc(s_onorm, 1)
                    for i in L:
                        dve.wait_ge(s_y, nth(c, i))
                        dve.wait_ge(s_st_t[i], c * 32 + 1)
                        for k in range(KC):
                            ins = dve.tensor_tensor(t[i][:, k, :], x_in[i][:, k, :], bank[i][k][:, 0:T], ALU.add)
                        ins.then_inc(s_t, 1)
                    for i in L:
                        dve.wait_ge(s_mean, nth(c, i))
                        for k in range(KC):
                            ins = dve.tensor_tensor(dev[i][:, k, :], t[i][:, k, :], bank[i][2][:, 0:T], ALU.subtract)
                        ins.then_inc(s_dev, 1)
                    for i in L:
                        dve.wait_ge(s_std, nth(c, i))
                        dve.reciprocal(rstd[i][:], std[i][:]).then_inc(s_rstd, 1)
                        dve.wait_ge(s_rstd, nth(c, i))
                        for k in range(KC):
                            ins = dve.tensor_tensor(ln[i][:, k, :], dev[i][:, k, :], rstd[i][:], ALU.mult)
                        ins.then_inc(s_ln, 1)
                    for i in L:
                        for m in range(MQK):
                            dve.wait_ge(s_hi, nth(c, i) * MQK - (MQK - 1) + m)
                            dve.scalar_tensor_tensor(out=lo[i][:, m, :], in0=bank[i][m][:, 0:T],
                                                     scalar=qk_bias[:, m:m + 1], in1=hi[i][:, m, :].bitcast(F32),
                                                     op0=ALU.add, op1=ALU.subtract).then_inc(s_lo, 1)
                    for i in L:
                        dve.wait_ge(s_v, nth(c, i))
                        dve.wait_ge(s_st_v[i], c * 16 + 1)
                        for s in range(SUB):
                            ins = dve.tensor_tensor(v_out[i][:, s, :], bank[i][s][:, 0:C], v_bias[:], ALU.add)
                        ins.then_inc(s_vout, 1)


def causal_attention(nc, qk_hi, qk_lo, v_rows, ident, o_t):
    HN, DH = 4, C // 4
    PAIRS = HN // 2
    BANKS = 3
    PBUF = 6
    KV_LOADS, Q_LOADS = 7, 6
    SCALE = DH ** -0.5
    MASKED = -3e38
    assert B == 2 and PAIRS == 2
    SLOTS = PAIRS * NC
    steps = [SUB * (z % NC + 1) for z in range(SLOTS)]
    first = [sum(steps[:z]) for z in range(SLOTS + 1)]
    at_step = [(z, g) for z in range(SLOTS) for g in range(steps[z])]
    LAP = first[SLOTS]
    units = [[(j, s, k) for j in range(2) for s in range(SUB) for k in range(z % NC + 1)] for z in range(SLOTS)]
    ufirst = [sum(len(u) for u in units[:z]) for z in range(SLOTS + 1)]
    ULAP = ufirst[SLOTS]
    afirst = [sum(n - 1 for n in steps[:z]) for z in range(SLOTS + 1)]
    ALAP = afirst[SLOTS]
    PIECES = (0, 2), (2, NC)

    plan = [([], [], []) for _ in range(LAP)]
    pair_steps, ahead = first[NC], len(units[0]) + len(units[1])
    for z in range(SLOTS):
        par, c = divmod(z, NC)
        n = ufirst[NC] - ahead
        for u in range(len(units[z])):
            k = ufirst[z] - par * ufirst[NC] + u
            if c < 2:
                at = (par - 1) * pair_steps + first[NC - 1] + k * (steps[NC - 1] - 2) // ahead
            else:
                at = par * pair_steps + (k - ahead) * (first[NC - 1] - 1) // n
            lap = 1 if at < 0 else 0
            plan[at % LAP][0].append((lap, z, u))
        plan[at % LAP][1].append((lap, z))
        plan[(at + 1) % LAP][2].append((lap, z))
        assert at + 1 < first[z]

    def sums_step(z):
        return 0 if z % NC < 2 else 2

    def thirds_at(z, g):
        s = g - sums_step(z) - 1
        last = steps[z] - sums_step(z) - 2
        return [k for k in range(SUB) if min(k, last) == s]

    sums_at = [first[z] + sums_step(z) for z in range(1, SLOTS)] + [LAP]

    def rows_before(z):
        return sum(len(plan[at][2]) for at in range(min(sums_at[z] + 1, LAP)))

    def sums_before(at):
        return sum(1 for x in sums_at if x < at)

    with ExitStack() as ctx:
        sb, ps, sem = tools(nc, ctx, "causal")
        ka = [[sb(f"ka{i}{j}", [P, N], F32R) for j in range(2)] for i in range(2)]
        kb = [[sb(f"kb{i}{j}", [DH + 1, N], F32R) for j in range(2)] for i in range(2)]
        qa = [sb(f"qa{j}", [P, N], F32R) for j in range(2)]
        qb = [sb(f"qb{j}", [DH + 1, N], F32R) for j in range(2)]
        vs = [sb(f"vs{i}", [P, NT, 2, DH]) for i in range(2)]
        probs = [sb(f"probs{i}", [P, 2 * T]) for i in range(PBUF)]
        run_sum = sb("run_sum", [P, 2 * T])
        row_sum = sb("row_sum", [P, 2 * T])
        maxes = [sb(f"maxes{i}", [P, 2 * SUB, NC]) for i in range(2)]
        neg_max = sb("neg_max", [P, 2 * SUB])
        out_sb = sb("out", [P, T])
        recip = sb("recip", [P, T])
        normed = [sb(f"normed{i}", [P, T]) for i in range(2)]
        ones = sb("ones", [P, DH])
        ident_sb = sb("ident", [P, P])
        ident_bf = sb("ident_bf", [P, P], BF16)
        mask_q = sb("mask_q", [P, SUB, T], BF16)
        mask_k = sb("mask_k", [P, SUB, T], BF16)
        scores = [ps(f"scores{i}", [P, 512]) for i in range(BANKS)]
        max_ps = [ps(f"max{i}", [P, 512]) for i in range(BANKS)]
        out_ps = ps("out_ps", [P, 512])
        misc = ps("misc", [P, 512])
        s_const, s_ones, s_zero, s_mask = sem("const"), sem("ones"), sem("mask_zeroed"), sem("masks_ready")
        s_kv = [[sem(f"keys_loaded{i}{k}") for k in range(2)] for i in range(2)]
        s_q = [sem(f"queries_loaded{c}") for c in range(NC)]
        s_st, s_exp, s_pv, s_acc = (sem(n) for n in ("scores_mm", "exp_done", "pv_mm", "row_sum_done"))
        s_mx, s_red, s_neg, s_rows, s_row = (sem(n) for n in (
            "max_mm", "max_taken", "neg_max_ready", "rows_mm", "rows_placed"))
        s_oev, s_l, s_rec, s_norm = (sem(n) for n in ("out_taken", "sums_mm", "recip_done", "normed_ready"))
        s_store = [sem(f"stored{i}") for i in range(2)]

        with nc.Block() as block:
            @block.sync
            def _(sp):
                for i in range(2):
                    sp.sem_inc(s_store[i], 1)
                sp.dma_start(ident_sb[:], ident).then_inc(s_const, 16)
                hi, lo = (x.rearrange("b (x h j d) n -> (b x h) j d n", x=2, h=PAIRS, j=2)
                          for x in (qk_hi, qk_lo))

                def load_queries(b, par, c):
                    cols = slice(c * T, (c + 1) * T)
                    for j in range(2):
                        for dst, row, src in ((qa, 0, hi), (qa, DH, hi), (qb, 0, lo)):
                            sp.dma_start(dst[j][row:row + DH, cols].bitcast(F32),
                                         src[b * 2 * PAIRS + par, j, :, cols]).then_inc(s_q[c], 16)

                def load_keys(b, par, piece):
                    start, end = PIECES[piece]
                    cols = slice(start * T, end * T)
                    for j in range(2):
                        for dst, row, src in ((ka, 0, hi), (ka, DH, lo), (kb, 0, hi)):
                            sp.dma_start(dst[par][j][row:row + DH, cols].bitcast(F32),
                                         src[b * 2 * PAIRS + PAIRS + par, j, :, cols]).then_inc(s_kv[par][piece], 16)
                    sp.dma_start(vs[par][:, start * SUB:end * SUB, :, :].rearrange("p t j d -> p t (j d)"),
                                 v_rows.rearrange("b (t p) c -> p (b t) c", p=P)[
                                     :, b * NT + start * SUB:b * NT + end * SUB,
                                     par * 2 * DH:(par + 1) * 2 * DH]).then_inc(s_kv[par][piece], 16)

                def store(b, z):
                    par, c = divmod(z, NC)
                    sp.wait_ge(s_norm, b * SLOTS + z + 2)
                    sp.dma_start(o_t[b][par * P:(par + 1) * P, c * T:(c + 1) * T],
                                 normed[z % 2][:]).then_inc(s_store[z % 2], 16)

                for c in range(2):
                    load_queries(0, 0, c)
                load_keys(0, 0, 0)
                load_keys(0, 0, 1)
                for c in range(2, NC):
                    load_queries(0, 0, c)
                for b in range(B):
                    for par in range(PAIRS):
                        nb, npar = (b, 1) if par == 0 else ((b + 1) % B, 0)
                        sp.wait_ge(s_pv, b * LAP + first[par * NC] + PBUF)
                        for piece in range(2):
                            load_keys(nb, npar, piece)
                        for c in range(NC):
                            z = par * NC + c
                            sp.wait_ge(s_pv, b * LAP + first[z + 1] + PBUF)
                            load_queries(nb, npar, c)
                            if c > 0:
                                store(b, z - 1)
                        store(b, par * NC + NC - 1)
                for i in range(2):
                    sp.wait_ge(s_store[i], B * SLOTS // 2 * 16 + 1)
                for piece in range(2):
                    sp.wait_ge(s_kv[0][piece], (B + 1) * KV_LOADS * 16)
                    sp.wait_ge(s_kv[1][piece], B * KV_LOADS * 16)
                for c in range(NC):
                    sp.wait_ge(s_q[c], (B * PAIRS + 1) * Q_LOADS * 16)

            @block.tensor
            def _(pe):
                pe.sem_inc(s_pv, PBUF)
                pe.sem_inc(s_rows, 1)
                pe.wait_ge(s_const, 16)
                pe.wait_ge(s_ones, 2)
                pe.wait_ge(s_mask, 3)

                def score_step(b, z, g):
                    par, c = divmod(z, NC)
                    if g == 0:
                        pe.wait_ge(s_row, (b * SLOTS + z + 1) * 2 + 1)
                    cols, keys = slice(c * T, (c + 1) * T), slice(g * P, (g + 1) * P)
                    diagonal = g - SUB * c
                    for j in range(2):
                        at = (first[z] + g) * 2 + j
                        pe.wait_ge(s_exp, b * 2 * LAP + at + 1)
                        to = scores[at % BANKS][:, 0:T]
                        pe.matmul(to, ka[par][j][:, keys], qa[j][:, cols], start=True, stop=False)
                        mm = pe.matmul(to, kb[par][j][:, keys], qb[j][:, cols], start=False, stop=diagonal < 0)
                        if diagonal >= 0:
                            mm = pe.matmul(to, ident_bf[:], mask_k[:, diagonal, :], start=False, stop=True)
                        mm.then_inc(s_st, 1)

                def max_unit(b, z, u):
                    par, c = divmod(z, NC)
                    if u == 0:
                        pe.wait_ge(s_q[c], (b * PAIRS + par + 1) * Q_LOADS * 16)
                        pe.wait_ge(s_kv[par][0 if c < PIECES[0][1] else 1], (b + 1) * KV_LOADS * 16)
                    j, s, k = units[z][u]
                    at = ufirst[z] + u
                    pe.wait_ge(s_red, b * ULAP + at + 1)
                    queries = slice(c * T + s * P, c * T + (s + 1) * P)
                    to, keys = max_ps[at % BANKS][:, 0:T], slice(k * T, (k + 1) * T)
                    pe.matmul(to, qa[j][:, queries], ka[par][j][:, keys], start=True, stop=False)
                    mm = pe.matmul(to, qb[j][0:DH, queries], kb[par][j][0:DH, keys], start=False, stop=k < c)
                    if k == c:
                        mm = pe.matmul(to, ident_bf[:], mask_q[:, s, :], start=False, stop=True)
                    mm.then_inc(s_mx, 1)

                def pv_step(b, z, g):
                    if g == 0:
                        pe.wait_ge(s_oev, b * SLOTS + z + 1)
                    pe.wait_ge(s_exp, (b * LAP + first[z] + g) * 2 + 2 + BANKS)
                    for j in range(2):
                        mm = pe.matmul(out_ps[DH * j:DH * (j + 1), 0:T], vs[z // NC][:, g, j, :],
                                       probs[(first[z] + g) % PBUF][:, j * T:(j + 1) * T],
                                       start=g == 0, stop=g == steps[z] - 1, tile_position=(0, DH * j))
                    mm.then_inc(s_pv, 1)

                def rows(b, z, sums_done):
                    pe.wait_ge(s_rec, sums_done * SUB + SUB)
                    pe.wait_ge(s_row, (b * SLOTS + z) * 2 + 1)
                    pe.wait_ge(s_neg, b * SLOTS + z + 1)
                    for j in range(2):
                        for s in range(SUB):
                            mm = pe.matmul(misc[32 * j:32 * j + 1, s * P:(s + 1) * P],
                                           neg_max[:, j * SUB + s:j * SUB + s + 1], ident_sb[:],
                                           start=True, stop=True, tile_position=(0, 32 * j))
                    mm.then_inc(s_rows, 1)

                def sums(b, z):
                    pe.wait_ge(s_row, (b * SLOTS + 2 + rows_before(z)) * 2 + 1)
                    pe.wait_ge(s_rec, (b * SLOTS + z) * SUB + SUB)
                    pe.wait_ge(s_acc, (b + 1) * ALAP + afirst[z + 1])
                    for j in range(2):
                        mm = pe.matmul(misc[DH * j:DH * (j + 1), 0:T], ones[:], row_sum[:, j * T:(j + 1) * T],
                                       start=True, stop=True, tile_position=(0, DH * j))
                    mm.then_inc(s_l, 1)

                for z in range(2):
                    for u in range(len(units[z])):
                        max_unit(0, z, u)
                    rows(0, z, 0)
                with pe.Fori(0, B) as b:
                    for at, (z, g) in enumerate(at_step):
                        todo, _, made = plan[at]
                        n = 1 if len(todo) > 2 else 0
                        for lap, uz, u in todo[:n]:
                            max_unit(b + lap, uz, u)
                        score_step(b, z, g)
                        for lap, uz, u in todo[n:n + 1]:
                            max_unit(b + lap, uz, u)
                        if g > 0:
                            pv_step(b, z, g - 1)
                        for lap, uz, u in todo[n + 1:]:
                            max_unit(b + lap, uz, u)
                        for lap, rz in made:
                            rows(b + lap, rz, b * SLOTS + sums_before(at))
                        if z > 0 and g == sums_step(z):
                            sums(b, z - 1)
                        if g == steps[z] - 1:
                            pv_step(b, z, g)
                    sums(b, SLOTS - 1)

            @block.scalar
            def _(act):
                act.sem_inc(s_exp, BANKS)
                act.sem_inc(s_oev, 1)
                act.sem_inc(s_row, 1)

                def place_row(b, z):
                    c = z % NC
                    act.wait_ge(s_rows, b * SLOTS + z + 2)
                    act.activation(qb[1][DH:DH + 1, c * T:(c + 1) * T], misc[32:33, 0:T], ACT.Copy).then_inc(s_row, 1)

                def take_out(b, z):
                    act.wait_ge(s_norm, b * SLOTS + z + 1)
                    act.wait_ge(s_pv, b * LAP + first[z + 1] + PBUF)
                    act.activation(out_sb[:], out_ps[:, 0:T], ACT.Copy).then_inc(s_oev, 1)

                for z in range(2):
                    place_row(0, z)
                with act.Fori(0, B) as b:
                    for at, (z, g) in enumerate(at_step):
                        act.wait_ge(s_pv, b * LAP + at + 1)
                        bz, bg = at_step[at - PBUF]
                        act.wait_ge(s_acc, (b + (1 if at >= PBUF else 0)) * ALAP + afirst[bz] + max(bg, 1))
                        for j in range(2):
                            act.wait_ge(s_st, (b * LAP + at) * 2 + j + 1)
                            act.activation(probs[at % PBUF][:, j * T:(j + 1) * T],
                                           scores[(2 * at + j) % BANKS][:, 0:T], ACT.Exp, scale=SCALE
                                           ).then_inc(s_exp, 1)
                        if g == 0 and z > 0:
                            take_out(b, z - 1)
                        for lap, rz in plan[at][2]:
                            place_row(b + lap, rz)
                    take_out(b, SLOTS - 1)

            @block.vector
            def _(dve):
                dve.sem_inc(s_red, BANKS)
                dve.sem_inc(s_rec, SUB)
                dve.sem_inc(s_norm, 1)
                for par in range(2):
                    for j in range(2):
                        ins = dve.memset(kb[par][j][DH:DH + 1, :].bitcast(F32), 1.0)
                ins.then_inc(s_ones, 1)
                dve.memset(ones[:], 1.0).then_inc(s_ones, 1)
                dve.wait_ge(s_const, 16)
                dve.tensor_copy(ident_bf[:], ident_sb[:]).then_inc(s_mask, 1)

                def max_unit(b, z, u):
                    j, s, k = units[z][u]
                    at = ufirst[z] + u
                    dve.wait_ge(s_mx, b * ULAP + at + 1)
                    dve.tensor_reduce(maxes[z % 2][:, j * SUB + s:j * SUB + s + 1, k], max_ps[at % BANKS][:, 0:T],
                                      AX.X, ALU.max).then_inc(s_red, 1)

                def negate(b, z):
                    dve.wait_ge(s_rows, b * SLOTS + z + 1)
                    dve.wait_ge(s_red, b * ULAP + ufirst[z + 1] + BANKS)
                    dve.tensor_reduce(neg_max[:], maxes[z % 2][:, :, 0:z % NC + 1], AX.X, ALU.max,
                                      negate=True).then_inc(s_neg, 1)

                def place_row(b, z):
                    c = z % NC
                    dve.wait_ge(s_rows, b * SLOTS + z + 2)
                    dve.tensor_copy(qb[0][DH:DH + 1, c * T:(c + 1) * T], misc[0:1, 0:T]).then_inc(s_row, 1)

                def invert(b, z, s):
                    if s == 0:
                        dve.wait_ge(s_l, b * SLOTS + z + 1)
                        dve.wait_ge(s_norm, b * SLOTS + z + 1)
                    dve.reciprocal(recip[:, s * P:(s + 1) * P], misc[:, s * P:(s + 1) * P]).then_inc(s_rec, 1)

                def normalise(b, z):
                    dve.wait_ge(s_oev, b * SLOTS + z + 2)
                    dve.wait_ge(s_store[z % 2], (b * (SLOTS // 2) + z // 2) * 16 + 1)
                    dve.wait_ge(s_rec, (b * SLOTS + z + 1) * SUB + SUB)
                    dve.tensor_tensor(normed[z % 2][:], out_sb[:], recip[:], ALU.mult).then_inc(s_norm, 1)

                for z in range(2):
                    for u in range(len(units[z])):
                        max_unit(0, z, u)
                    negate(0, z)
                    place_row(0, z)
                with dve.Fori(0, B) as b:
                    for at, (z, g) in enumerate(at_step):
                        todo, complete, made = plan[at]
                        for lap, uz, u in todo:
                            max_unit(b + lap, uz, u)
                        for lap, cz in complete:
                            negate(b + lap, cz)
                        if z > 0:
                            for s in thirds_at(z, g):
                                invert(b, z - 1, s)
                            if SUB - 1 in thirds_at(z, g):
                                normalise(b, z - 1)
                        for lap, rz in made:
                            place_row(b + lap, rz)
                    for s in range(SUB):
                        invert(b, SLOTS - 1, s)
                    normalise(b, SLOTS - 1)

            @block.gpsimd
            def _(pool):
                pool.sem_inc(s_acc, ALAP)
                pool.memset(mask_q[:], 0.0).then_inc(s_zero, 1)
                pool.memset(mask_k[:], 0.0).then_inc(s_zero, 1)
                pool.wait_ge(s_zero, 2)
                for s in range(SUB):
                    ins = pool.affine_select(out=mask_q[:, s, :], in_=mask_q[:, s, :], compare_op=ALU.is_ge,
                                             fill=MASKED, base=s * P, pattern=[[-1, T]], channel_multiplier=1)
                ins.then_inc(s_mask, 1)
                for s in range(SUB):
                    ins = pool.affine_select(out=mask_k[:, s, :], in_=mask_k[:, s, :], compare_op=ALU.is_ge,
                                             fill=MASKED, base=-s * P, pattern=[[1, T]], channel_multiplier=-1)
                ins.then_inc(s_mask, 1)
                with pool.Fori(0, B) as b:
                    for at, (z, g) in enumerate(at_step):
                        if g == 0:
                            continue
                        pool.wait_ge(s_exp, (b * LAP + at) * 2 + 2 + BANKS)
                        pool.wait_ge(s_acc, (b + 1) * ALAP + afirst[z] + g - 1)
                        acc = probs[(at - 1) % PBUF] if g == 1 else run_sum
                        to = row_sum if g == steps[z] - 1 else run_sum
                        pool.tensor_tensor(to[:], acc[:], probs[at % PBUF][:], ALU.add).then_inc(s_acc, 1)


def recurrence_gate_and_ffn(nc, a, o_t, a_t, t_t, t2_t):
    HN, DH = 4, C // 4
    FF = 4 * C // P
    LNS = 3
    WEIGHTS = 24
    with ExitStack() as ctx:
        sb, ps, sem = tools(nc, ctx, "rec")
        L = range(B)
        w = {n: sb(n, [P, KC, C]) for n in ("o_w", "rq_w", "rk_w", "rv_w", "ro_w")}
        w["cg_w"] = sb("cg_w", [P, 2 * KC, C])
        w["ffn_w1"] = sb("ffn_w1", [P, KC, 4 * C])
        w["ffn_w2"] = sb("ffn_w2", [P, FF, C])
        cols = {n: sb(n, [P, KC]) for n in ("o_b", "rq_b", "rk_b", "ro_b", "cg_b", "ffn_b2", "ln1_g", "ln1_b",
                                            "ln2_g", "ln2_b", "ln3_g", "ln3_b")}
        cols["ffn_b1"] = sb("ffn_b1", [P, FF])
        rv_bias = sb("rv_bias", [P, C])
        mean_mat = sb("mean_mat", [P, P])
        ident = sb("ident", [P, P])
        half_cg_b = sb("half_cg_b", [P, KC])
        eps = sb("eps", [P, 1])
        tri = sb("tri", [P, 2 * T])
        gain = [cols["ln1_g"], cols["ln2_g"], cols["ln3_g"]]
        bias = [cols["ln1_b"], cols["ln2_b"], cols["ln3_b"]]

        def per_lane(name, shape, dt=F32):
            return [sb(f"{name}{i}", shape, dt) for i in L]
        t, x, o = (per_lane(n, [P, KC, T]) for n in ("t", "x", "o"))
        res, par, dev, sq, nm, dn, seq, mrg, t2 = (per_lane(n, [P, KC, T]) for n in (
            "res", "par", "dev", "sq", "nm", "dn", "seq", "mrg", "t2"))
        std, rstd = per_lane("std", [P, T]), per_lane("rstd", [P, T])
        hid = per_lane("hid", [P, FF, T])
        fm = per_lane("fm", [P, 2 * KC, T])
        vx = per_lane("vx", [P, SUB, HN, P])
        kt = per_lane("kt", [P, SUB, C])
        at = [[sb(f"at{i}{k}", [P, 2 * T]) for k in range(2)] for i in L]
        state = per_lane("state", [P, KC, P])
        bank = [[ps(f"bank{i}{k}", [P, 512]) for k in range(4)] for i in L]
        s_w, s_set = sem("weights"), sem("set_up")
        s_ld = [sem(f"loaded{i}") for i in L]
        s_st = [sem(f"stored{i}") for i in L]
        (s_att, s_res, s_mean, s_dev, s_sq, s_var, s_std, s_rstd, s_scaled, s_ln, s_z, s_zmin, s_zout, s_zexp,
         s_fm, s_v, s_vx, s_kt, s_ktout) = (sem(n) for n in (
             "att_mm", "res_ready", "mean_mm", "dev_ready", "dev_squared", "var_mm", "std_ready", "rstd_ready",
             "scaled", "ln_ready", "features_mm", "z_min", "z_taken", "z_exp", "features_ready", "v_mm",
             "values_ready", "keys_turned", "keys_ready"))
        (s_a, s_at, s_oe, s_upd, s_num, s_den, s_state, s_rden, s_rec, s_ro, s_gate, s_th, s_diff, s_gated, s_mrg,
         s_h, s_gelu, s_f, s_t2, s_cgb) = (sem(n) for n in (
             "a_mm", "a_masked", "out_mm", "update_mm", "num_taken", "den_taken", "state_ready", "den_inverted",
             "rec_ready", "ro_mm", "gate_mm", "gate_tanh", "par_less_seq", "gated", "merged_ready", "hidden_mm",
             "hidden_ready", "ffn_mm", "t2_ready", "cgb_halved"))
        s_tri = sem("tri_set")

        def ln(c, r, i):
            return (c * LNS + r) * B + i + 1

        def head(c, h, i):
            return (c * HN + h) * B + i + 1

        def project(pe, to, weight, src, tiles, m):
            for k in range(tiles):
                mm = pe.matmul(to[:, 0:T], weight[:, k, m * P:(m + 1) * P], src(k), start=k == 0, stop=k == tiles - 1)
            return mm

        with nc.Block() as block:
            @block.sync
            def _(sp):
                for i in L:
                    sp.sem_inc(s_st[i], 1)
                loads = [(w[n], a[n]) for n in w] + [(cols[n], a[n]) for n in cols] + [
                    (mean_mat, a["mean_mat"]), (ident, a["ident"])]
                assert len(loads) + 1 == WEIGHTS
                for dst, src in loads:
                    sp.dma_start(dst[:], src).then_inc(s_w, 16)
                sp.dma_start(rv_bias[:], a["rv_b"].partition_broadcast(P)).then_inc(s_w, 16)
                with sp.Fori(0, NC) as c:
                    at_c = bass.ds(c * T, T)
                    for i in L:
                        sp.wait_ge(s_t2, nth(c, i))
                        for dst, src in ((o, o_t), (x, a_t), (t, t_t)):
                            sp.dma_start(dst[i][:], src[i].rearrange("(k p) n -> p k n", p=P)[:, :, at_c]
                                         ).then_inc(s_ld[i], 16)
                    for i in L:
                        sp.wait_ge(s_t2, nth(c + 1, i))
                        sp.dma_start(t2_t[i].rearrange("(k p) n -> p k n", p=P)[:, :, at_c], t2[i][:]
                                     ).then_inc(s_st[i], 16)
                for i in L:
                    sp.wait_ge(s_st[i], NC * 16 + 1)

            @block.tensor
            def _(pe):
                pe.wait_ge(s_w, 16 * WEIGHTS)
                pe.wait_ge(s_set, 6)

                def mean(c, r):
                    for i in L:
                        pe.wait_ge(s_res, ln(c, r, i))
                        for k in range(KC):
                            mm = pe.matmul(bank[i][2][:, 0:T], mean_mat[:], res[i][:, k, :],
                                           start=k == 0, stop=k == KC - 1)
                        mm.then_inc(s_mean, 1)

                def var(c, r):
                    for i in L:
                        pe.wait_ge(s_sq, ln(c, r, i))
                        for k in range(KC):
                            mm = pe.matmul(bank[i][3][:, 0:T], mean_mat[:], sq[i][:, k, :],
                                           start=k == 0, stop=k == KC - 1)
                        mm.then_inc(s_var, 1)

                with pe.Fori(0, NC) as c:
                    for i in L:
                        pe.wait_ge(s_ld[i], (c + 1) * 48)
                        pe.wait_ge(s_t2, nth(c, i))
                        for m in range(KC):
                            mm = project(pe, bank[i][m], w["o_w"], lambda k: o[i][:, k, :], KC, m)
                        mm.then_inc(s_att, 1)
                    mean(c, 0)
                    var(c, 0)
                    for i in L:
                        pe.wait_ge(s_ln, ln(c, 0, i))
                        for m in range(2 * KC):
                            mm = project(pe, bank[i][m], w["rq_w" if m < KC else "rk_w"],
                                         lambda k: par[i][:, k, :], KC, m % KC)
                        mm.then_inc(s_z, 1)
                    for i in L:
                        pe.wait_ge(s_zout, nth(c, i))
                        for s in range(SUB):
                            for k in range(KC):
                                mm = pe.matmul(bank[i][s][:, 0:C], par[i][:, k, s * P:(s + 1) * P],
                                               w["rv_w"][:, k, :], start=k == 0, stop=k == KC - 1)
                        mm.then_inc(s_v, 1)
                    for i in L:
                        pe.wait_ge(s_fm, nth(c, i))
                        pe.wait_ge(s_vx, nth(c, i))
                        for k in range(KC):
                            for s in range(SUB):
                                mm = pe.transpose(bank[i][3 if k == 0 else 0][:, s * P:(s + 1) * P],
                                                  fm[i][:, KC + k, s * P:(s + 1) * P], ident[:])
                        mm.then_inc(s_kt, 1)
                    for h in range(HN):
                        half, base = h // 2, DH * (h % 2)
                        rows = slice(base, base + DH)
                        for i in L:
                            if h == 0:
                                pe.wait_ge(s_ktout, nth(c, i))
                            else:
                                pe.wait_ge(s_at, head(c, h - 1, i))
                            for s, (b, col) in enumerate(((0, 0), (1, 0), (0, T))):
                                mm = pe.matmul(bank[i][b][:, col:col + T - s * P],
                                               fm[i][rows, KC + half, s * P:(s + 1) * P],
                                               fm[i][rows, half, s * P:T], start=True, stop=True)
                            mm.then_inc(s_a, 1)
                        for i in L:
                            pe.wait_ge(s_at, head(c, h, i))
                            pe.wait_ge(s_num, head(c, h, i))
                            pe.wait_ge(s_den, head(c, h, i))
                            if h == 0:
                                pe.wait_ge(s_state, nth(c, i))
                            pe.matmul(bank[i][2][:, 0:T], state[i][rows, half, :], fm[i][rows, half, :],
                                      start=True, stop=False)
                            for s, col in enumerate((0, T + P, T)):
                                mm = pe.matmul(bank[i][2][:, s * P:T], vx[i][:, s, h, :],
                                               at[i][h % 2][:, col:col + T - s * P], start=False, stop=s == SUB - 1)
                            mm.then_inc(s_oe, 1)
                            for s in range(SUB):
                                mm = pe.matmul(bank[i][3][rows, half * P:(half + 1) * P],
                                               kt[i][:, s, h * DH:(h + 1) * DH], vx[i][:, s, h, :],
                                               start=s == 0, stop=s == SUB - 1, tile_position=(0, base))
                            if h == HN - 1:
                                mm.then_inc(s_upd, 1)
                    for i in L:
                        pe.wait_ge(s_rec, nth(c, i))
                        for m in range(KC):
                            mm = project(pe, bank[i][m], w["ro_w"], lambda k: nm[i][:, k, :], KC, m)
                        mm.then_inc(s_ro, 1)
                    mean(c, 1)
                    var(c, 1)
                    for i in L:
                        pe.wait_ge(s_ln, ln(c, 1, i))
                        for m in range(KC):
                            mm = project(pe, bank[i][m], w["cg_w"],
                                         lambda k: (par if k < KC else seq)[i][:, k % KC, :], 2 * KC, m)
                        mm.then_inc(s_gate, 1)
                    for i in L:
                        pe.wait_ge(s_mrg, nth(c, i))
                        for m in range(FF):
                            if m >= 4:
                                pe.wait_ge(s_gelu, nth(c, i) * FF - (FF - 1) + m - 4)
                            project(pe, bank[i][m % 4], w["ffn_w1"], lambda k: mrg[i][:, k, :], KC, m
                                    ).then_inc(s_h, 1)
                    for i in L:
                        pe.wait_ge(s_gelu, nth(c, i) * FF)
                        for m in range(KC):
                            mm = project(pe, bank[i][m], w["ffn_w2"], lambda k: hid[i][:, k, :], FF, m)
                        mm.then_inc(s_f, 1)
                    mean(c, 2)
                    var(c, 2)

            @block.scalar
            def _(act):
                act.wait_ge(s_w, 16 * WEIGHTS)
                act.wait_ge(s_set, 6)
                act.sem_inc(s_num, B)
                act.activation(half_cg_b[:], cols["cg_b"][:], ACT.Copy, scale=0.5).then_inc(s_cgb, 1)
                act.wait_ge(s_cgb, 1)

                def layer_norm(c, r, out):
                    for i in L:
                        act.wait_ge(s_dev, ln(c, r, i))
                        act.activation(sq[i][:], dev[i][:], ACT.Square).then_inc(s_sq, 1)
                    for i in L:
                        act.wait_ge(s_var, ln(c, r, i))
                        act.activation(std[i][:], bank[i][3][:, 0:T], ACT.Sqrt, bias=eps[:, 0:1]).then_inc(s_std, 1)
                    for i in L:
                        act.wait_ge(s_scaled, ln(c, r, i))
                        for k in range(KC):
                            ins = act.activation(out[i][:, k, :], dev[i][:, k, :], ACT.Identity,
                                                 bias=bias[r][:, k:k + 1])
                        ins.then_inc(s_ln, 1)

                with act.Fori(0, NC) as c:
                    layer_norm(c, 0, par)
                    for i in L:
                        act.wait_ge(s_z, nth(c, i))
                        for m in range(2 * KC):
                            ins = act.activation(hid[i][:, m, :], bank[i][m][:, 0:T], ACT.Identity,
                                                 bias=cols["rq_b" if m < KC else "rk_b"][:, m % KC:m % KC + 1])
                        ins.then_inc(s_zout, 1)
                    for i in L:
                        act.wait_ge(s_zmin, nth(c, i))
                        act.activation(fm[i][:], hid[i][:, 4:8, :], ACT.Exp).then_inc(s_zexp, 1)
                    for i in L:
                        act.wait_ge(s_kt, nth(c, i))
                        for k in range(KC):
                            ins = act.activation(kt[i][:, :, k * P:(k + 1) * P],
                                                 bank[i][3 if k == 0 else 0][:, 0:T].rearrange(
                                                     "p (s c) -> p s c", s=SUB), ACT.Copy)
                        ins.then_inc(s_ktout, 1)
                    for h in range(HN):
                        half, base = h // 2, DH * (h % 2)
                        for i in L:
                            act.wait_ge(s_oe, head(c, h, i))
                            act.activation(nm[i][base:base + DH, half, :], bank[i][2][0:DH, 0:T], ACT.Copy
                                           ).then_inc(s_num, 1)
                    layer_norm(c, 1, seq)
                    for i in L:
                        act.wait_ge(s_gate, nth(c, i))
                        for m in range(KC):
                            ins = act.activation(nm[i][:, m, :], bank[i][m][:, 0:T], ACT.Tanh, scale=0.5,
                                                 bias=half_cg_b[:, m:m + 1])
                        ins.then_inc(s_th, 1)
                    for i in L:
                        for m in range(FF):
                            act.wait_ge(s_h, nth(c, i) * FF - (FF - 1) + m)
                            act.activation(hid[i][:, m, :], bank[i][m % 4][:, 0:T], ACT.Gelu,
                                           bias=cols["ffn_b1"][:, m:m + 1]).then_inc(s_gelu, 1)
                    layer_norm(c, 2, seq)

            @block.vector
            def _(dve):
                dve.sem_inc(s_den, B)
                dve.sem_inc(s_t2, B)
                dve.memset(eps[:], LN_EPS).then_inc(s_set, 1)
                for i in L:
                    dve.memset(vx[i][:], 1.0).then_inc(s_set, 1)
                    dve.memset(state[i][:], 0.0).then_inc(s_state, 1)
                dve.wait_ge(s_w, 16 * WEIGHTS)
                dve.wait_ge(s_set, 6)

                def residual(c, r, counter, bias_cols, other):
                    for i in L:
                        dve.wait_ge(counter, nth(c, i))
                        for m in range(KC):
                            ins = dve.scalar_tensor_tensor(out=res[i][:, m, :], in0=bank[i][m][:, 0:T],
                                                           scalar=bias_cols[:, m:m + 1], in1=other[i][:, m, :],
                                                           op0=ALU.add, op1=ALU.add)
                        ins.then_inc(s_res, 1)

                def layer_norm(c, r):
                    for i in L:
                        dve.wait_ge(s_mean, ln(c, r, i))
                        for k in range(KC):
                            ins = dve.tensor_tensor(dev[i][:, k, :], res[i][:, k, :], bank[i][2][:, 0:T], ALU.subtract)
                        ins.then_inc(s_dev, 1)
                    for i in L:
                        dve.wait_ge(s_std, ln(c, r, i))
                        dve.reciprocal(rstd[i][:], std[i][:]).then_inc(s_rstd, 1)
                    for i in L:
                        dve.wait_ge(s_rstd, ln(c, r, i))
                        for k in range(KC):
                            ins = dve.scalar_tensor_tensor(out=dev[i][:, k, :], in0=dev[i][:, k, :],
                                                           scalar=gain[r][:, k:k + 1], in1=rstd[i][:],
                                                           op0=ALU.mult, op1=ALU.mult)
                        ins.then_inc(s_scaled, 1)

                with dve.Fori(0, NC) as c:
                    residual(c, 0, s_att, cols["o_b"], x)
                    layer_norm(c, 0)
                    for i in L:
                        dve.wait_ge(s_zout, nth(c, i))
                        dve.tensor_scalar(hid[i][:, 4:8, :], hid[i][:, 0:4, :], 0.0, None, ALU.min
                                          ).then_inc(s_zmin, 1)
                    for i in L:
                        dve.wait_ge(s_zexp, nth(c, i))
                        dve.scalar_tensor_tensor(out=fm[i][:], in0=hid[i][:, 0:4, :], scalar=0.0, in1=fm[i][:],
                                                 op0=ALU.max, op1=ALU.add).then_inc(s_fm, 1)
                    for i in L:
                        dve.wait_ge(s_v, nth(c, i))
                        for s in range(SUB):
                            ins = dve.tensor_tensor(vx[i][:, s, :, 0:DH],
                                                    bank[i][s][:, 0:C].rearrange("p (h d) -> p h d", h=HN),
                                                    rv_bias[:].rearrange("p (h d) -> p h d", h=HN), ALU.add)
                        ins.then_inc(s_vx, 1)
                    for h in range(HN):
                        half, base = h // 2, DH * (h % 2)
                        for i in L:
                            dve.wait_ge(s_a, head(c, h, i))
                            if h >= 2:
                                dve.wait_ge(s_oe, head(c, h - 2, i))
                            dve.tensor_tensor(at[i][h % 2][:, 0:512], bank[i][0][:, 0:512], tri[:, 0:512], ALU.mult)
                            dve.tensor_tensor(at[i][h % 2][:, 512:768], bank[i][1][:, 0:256], tri[:, 512:768],
                                              ALU.mult).then_inc(s_at, 1)
                        for i in L:
                            dve.wait_ge(s_oe, head(c, h, i))
                            dve.tensor_scalar(dn[i][base:base + DH, half, :], bank[i][2][DH:P, 0:T], EPS_REC, None,
                                              ALU.add).then_inc(s_den, 1)
                    for i in L:
                        dve.wait_ge(s_upd, nth(c, i))
                        dve.tensor_tensor(state[i][:].rearrange("p k m -> p (k m)"),
                                          state[i][:].rearrange("p k m -> p (k m)"), bank[i][3][:, 0:2 * P],
                                          ALU.add).then_inc(s_state, 1)
                    for i in L:
                        dve.wait_ge(s_den, head(c + 1, 0, i))
                        dve.reciprocal(dn[i][:], dn[i][:]).then_inc(s_rden, 1)
                        dve.wait_ge(s_rden, nth(c, i))
                        dve.wait_ge(s_num, head(c + 1, 0, i))
                        dve.tensor_tensor(nm[i][:], nm[i][:], dn[i][:], ALU.mult).then_inc(s_rec, 1)
                    residual(c, 1, s_ro, cols["ro_b"], par)
                    layer_norm(c, 1)
                    for i in L:
                        dve.wait_ge(s_ln, ln(c, 1, i))
                        dve.tensor_tensor(dn[i][:], par[i][:], seq[i][:], ALU.subtract).then_inc(s_diff, 1)
                    for i in L:
                        dve.wait_ge(s_th, nth(c, i))
                        dve.wait_ge(s_diff, nth(c, i))
                        dve.scalar_tensor_tensor(out=mrg[i][:], in0=nm[i][:], scalar=1.0, in1=dn[i][:],
                                                 op0=ALU.add, op1=ALU.mult).then_inc(s_gated, 1)
                        dve.wait_ge(s_gated, nth(c, i))
                        dve.scalar_tensor_tensor(out=mrg[i][:], in0=mrg[i][:], scalar=0.5, in1=seq[i][:],
                                                 op0=ALU.mult, op1=ALU.add).then_inc(s_mrg, 1)
                    residual(c, 2, s_f, cols["ffn_b2"], mrg)
                    layer_norm(c, 2)
                    for i in L:
                        dve.wait_ge(s_ln, ln(c, 2, i))
                        dve.wait_ge(s_st[i], c * 16 + 1)
                        dve.tensor_tensor(t2[i][:], t[i][:], seq[i][:], ALU.add).then_inc(s_t2, 1)

            @block.gpsimd
            def _(pool):
                pool.memset(tri[:], 1.0).then_inc(s_tri, 1)
                pool.wait_ge(s_tri, 1)
                for col in (0, T, T + P):
                    pool.affine_select(out=tri[:, col:col + P], in_=tri[:, col:col + P], compare_op=ALU.is_ge,
                                       fill=0.0, base=0, pattern=[[1, P]], channel_multiplier=-1).then_inc(s_set, 1)


def routed_ffn(nc, a, t_t, logits, base_t, delta_t):
    FF = 4 * C // P
    WEIGHTS = 7
    with ExitStack() as ctx:
        sb, ps, sem = tools(nc, ctx, "ffn")
        L = range(B)
        w1 = sb("w1", [P, KC, 4 * C])
        w2 = sb("w2", [P, FF, C])
        wr = sb("wr", [P, KC])
        br = sb("br", [1, 1])
        b1 = sb("b1", [P, FF])
        b2 = sb("b2", [P, KC])
        mean_mat = sb("mean_mat", [P, P])
        eps = sb("eps", [P, 1])
        t, dev, sq, x, base, delta = ([sb(f"{n}{i}", [P, KC, T]) for i in L] for n in (
            "t", "dev", "sq", "x", "base", "delta"))
        std, rstd = ([sb(f"{n}{i}", [P, T]) for i in L] for n in ("std", "rstd"))
        hid = [sb(f"hid{i}", [P, FF, T]) for i in L]
        row = [sb(f"row{i}", [1, T]) for i in L]
        bank = [[ps(f"bank{i}{k}", [P, 512]) for k in range(4)] for i in L]
        s_w, s_set = sem("weights"), sem("set_up")
        s_ld = [sem(f"loaded{i}") for i in L]
        s_st = [sem(f"stored{i}") for i in L]
        (s_mean, s_dev, s_sq, s_var, s_std, s_rstd, s_x, s_logit, s_row, s_base, s_h, s_gelu, s_f, s_delta) = (
            sem(n) for n in ("mean_mm", "dev_ready", "dev_squared", "var_mm", "std_ready", "rstd_ready", "x_ready",
                             "logit_mm", "row_ready", "base_ready", "hidden_mm", "hidden_ready", "ffn_mm",
                             "delta_ready"))

        with nc.Block() as block:
            @block.sync
            def _(sp):
                for i in L:
                    sp.sem_inc(s_st[i], 1)
                for dst, src in ((w1, a["w1"]), (w2, a["w2"]), (wr, a["wr"]), (br, a["br"]), (b1, a["b1"]),
                                 (b2, a["b2"]), (mean_mat, a["mean_mat"])):
                    sp.dma_start(dst[:], src).then_inc(s_w, 16)
                with sp.Fori(0, NC) as c:
                    at_c = bass.ds(c * T, T)
                    for i in L:
                        sp.wait_ge(s_base, nth(c, i))
                        sp.dma_start(t[i][:], t_t[i].rearrange("(k p) n -> p k n", p=P)[:, :, at_c]
                                     ).then_inc(s_ld[i], 16)
                    for i in L:
                        sp.wait_ge(s_row, nth(c, i))
                        sp.dma_start(logits[i:i + 1, at_c], row[i][:]).then_inc(s_st[i], 16)
                        sp.wait_ge(s_base, nth(c + 1, i))
                        sp.dma_start(base_t[i].rearrange("(k p) n -> p k n", p=P)[:, :, at_c], base[i][:]
                                     ).then_inc(s_st[i], 16)
                    for i in L:
                        sp.wait_ge(s_delta, nth(c + 1, i))
                        sp.dma_start(delta_t[i].rearrange("(k p) n -> p k n", p=P)[:, :, at_c], delta[i][:]
                                     ).then_inc(s_st[i], 16)
                for i in L:
                    sp.wait_ge(s_st[i], NC * 48 + 1)

            @block.tensor
            def _(pe):
                pe.wait_ge(s_w, 16 * WEIGHTS)
                with pe.Fori(0, NC) as c:
                    for i in L:
                        pe.wait_ge(s_ld[i], (c + 1) * 16)
                        pe.wait_ge(s_delta, nth(c, i))
                        for k in range(KC):
                            mm = pe.matmul(bank[i][2][:, 0:T], mean_mat[:], t[i][:, k, :],
                                           start=k == 0, stop=k == KC - 1)
                        mm.then_inc(s_mean, 1)
                    for i in L:
                        pe.wait_ge(s_sq, nth(c, i))
                        for k in range(KC):
                            mm = pe.matmul(bank[i][3][:, 0:T], mean_mat[:], sq[i][:, k, :],
                                           start=k == 0, stop=k == KC - 1)
                        mm.then_inc(s_var, 1)
                    for i in L:
                        pe.wait_ge(s_x, nth(c, i))
                        for k in range(KC):
                            mm = pe.matmul(bank[i][2][0:1, 0:T], wr[:, k:k + 1], x[i][:, k, :],
                                           start=k == 0, stop=k == KC - 1)
                        mm.then_inc(s_logit, 1)
                    for i in L:
                        for m in range(FF):
                            if m == 2:
                                pe.wait_ge(s_row, nth(c, i))
                            if m >= 4:
                                pe.wait_ge(s_gelu, nth(c, i) * FF - (FF - 1) + m - 4)
                            for k in range(KC):
                                mm = pe.matmul(bank[i][m % 4][:, 0:T], w1[:, k, m * P:(m + 1) * P], x[i][:, k, :],
                                               start=k == 0, stop=k == KC - 1)
                            mm.then_inc(s_h, 1)
                    for i in L:
                        pe.wait_ge(s_gelu, nth(c, i) * FF)
                        for m in range(KC):
                            for k in range(FF):
                                mm = pe.matmul(bank[i][m][:, 0:T], w2[:, k, m * P:(m + 1) * P], hid[i][:, k, :],
                                               start=k == 0, stop=k == FF - 1)
                        mm.then_inc(s_f, 1)

            @block.scalar
            def _(act):
                act.wait_ge(s_w, 16 * WEIGHTS)
                act.wait_ge(s_set, 1)
                act.sem_inc(s_delta, B)
                with act.Fori(0, NC) as c:
                    for i in L:
                        act.wait_ge(s_dev, nth(c, i))
                        act.activation(sq[i][:], dev[i][:], ACT.Square).then_inc(s_sq, 1)
                    for i in L:
                        act.wait_ge(s_var, nth(c, i))
                        act.activation(std[i][:], bank[i][3][:, 0:T], ACT.Sqrt, bias=eps[:, 0:1]).then_inc(s_std, 1)
                    for i in L:
                        act.wait_ge(s_logit, nth(c, i))
                        act.wait_ge(s_st[i], c * 48 + 1)
                        act.activation(row[i][:], bank[i][2][0:1, 0:T], ACT.Identity, bias=br[:, 0:1]
                                       ).then_inc(s_row, 1)
                    for i in L:
                        for m in range(FF):
                            act.wait_ge(s_h, nth(c, i) * FF - (FF - 1) + m)
                            act.activation(hid[i][:, m, :], bank[i][m % 4][:, 0:T], ACT.Gelu_apprx_tanh,
                                           bias=b1[:, m:m + 1]).then_inc(s_gelu, 1)
                    for i in L:
                        act.wait_ge(s_f, nth(c, i))
                        for m in range(KC):
                            ins = act.activation(delta[i][:, m, :], bank[i][m][:, 0:T], ACT.Identity,
                                                 bias=b2[:, m:m + 1])
                        ins.then_inc(s_delta, 1)

            @block.vector
            def _(dve):
                dve.sem_inc(s_base, B)
                dve.memset(eps[:], LN_EPS).then_inc(s_set, 1)
                dve.wait_ge(s_set, 1)
                with dve.Fori(0, NC) as c:
                    for i in L:
                        dve.wait_ge(s_mean, nth(c, i))
                        for k in range(KC):
                            ins = dve.tensor_tensor(dev[i][:, k, :], t[i][:, k, :], bank[i][2][:, 0:T], ALU.subtract)
                        ins.then_inc(s_dev, 1)
                    for i in L:
                        dve.wait_ge(s_std, nth(c, i))
                        dve.reciprocal(rstd[i][:], std[i][:]).then_inc(s_rstd, 1)
                    for i in L:
                        dve.wait_ge(s_rstd, nth(c, i))
                        for k in range(KC):
                            ins = dve.tensor_tensor(x[i][:, k, :], dev[i][:, k, :], rstd[i][:], ALU.mult)
                        ins.then_inc(s_x, 1)
                    for i in L:
                        dve.wait_ge(s_x, nth(c, i))
                        dve.wait_ge(s_st[i], c * 48 + 1)
                        dve.tensor_tensor(base[i][:], t[i][:], x[i][:], ALU.add).then_inc(s_base, 1)


def select_and_merge(nc, logits, factors, ident, base_t, delta_t, out):
    KEPT = N // 2 - 1
    with ExitStack() as ctx:
        sb, ps, sem = tools(nc, ctx, "pick")
        L = range(B)
        row = [sb(f"row{i}", [P, N]) for i in L]
        by_tile = [sb(f"by_tile{i}", [NT, P]) for i in L]
        factor_row = [sb(f"factor_row{i}", [NT, P]) for i in L]
        ident_sb = sb("ident", [P, P])
        turn = [ps(f"turn{i}", [P, 512]) for i in L]
        s_const, s_turned, s_col, s_back, s_frow = (sem(n) for n in (
            "const", "logits_turned", "column_ready", "factors_turned", "factor_row_ready"))
        col = [sb(f"col{i}", [P, NT]) for i in L]
        before = sb("before", [P, P])
        scratch = sb("scratch", [P, N])
        tie = sb("tie", [P, P])
        counts = [sb(f"counts{i}", [P, NT, 3]) for i in L]
        rank = [sb(f"rank{i}", [P, NT]) for i in L]
        factor = [sb(f"factor{i}", [P, NT]) for i in L]
        spread = [sb(f"spread{i}", [P, N]) for i in L]
        base = [[sb(f"base{i}{k}", [P, N]) for k in range(KC)] for i in L]
        delta = [[sb(f"delta{i}{k}", [P, N]) for k in range(KC)] for i in L]
        s_tri, s_before, s_zero, s_step = sem("tri"), sem("before_ready"), sem("counts_zeroed"), sem("step")
        s_ld, s_in = [sem(f"loaded{i}") for i in L], [sem(f"tokens_loaded{i}") for i in L]
        s_rank, s_factor = sem("rank_ready"), sem("factor_ready")
        s_kept = [sem(f"factor_stored{i}") for i in L]
        s_spread = [sem(f"factor_spread{i}") for i in L]
        s_scaled, s_done, s_out = sem("scaled"), sem("merged"), sem("stored")

        with nc.Block() as block:
            @block.sync
            def _(sp):
                sp.dma_start(ident_sb[:], ident).then_inc(s_const, 16)
                for i in L:
                    sp.dma_start(row[i][:], logits[i].partition_broadcast(P)).then_inc(s_ld[i], 16)
                    sp.dma_start(by_tile[i][:], logits[i].rearrange("(t p) -> t p", p=P)).then_inc(s_ld[i], 16)
                for i in L:
                    for k in range(KC):
                        sp.dma_start(base[i][k][:], base_t[i, k * P:(k + 1) * P, :]).then_inc(s_in[i], 16)
                        sp.dma_start(delta[i][k][:], delta_t[i, k * P:(k + 1) * P, :]).then_inc(s_in[i], 16)
                for i in L:
                    sp.wait_ge(s_frow, i + 1)
                    sp.dma_start(factors[i].rearrange("(t p) -> t p", p=P), factor_row[i][:]).then_inc(s_kept[i], 16)
                    sp.wait_ge(s_kept[i], 16)
                    sp.dma_start(spread[i][:], factors[i].partition_broadcast(P)).then_inc(s_spread[i], 16)
                for i in L:
                    for k in range(KC):
                        sp.wait_ge(s_done, i * KC + k + 1)
                        sp.dma_start(out[i, k * P:(k + 1) * P, :], base[i][k][:]).then_inc(s_out, 16)
                sp.wait_ge(s_out, B * KC * 16)

            @block.tensor
            def _(pe):
                pe.wait_ge(s_const, 16)
                for i in L:
                    pe.wait_ge(s_ld[i], 32)
                    pe.transpose(turn[i][:, 0:NT], by_tile[i][:], ident_sb[0:NT, 0:NT]).then_inc(s_turned, 1)
                for i in L:
                    pe.wait_ge(s_factor, i + 1)
                    pe.transpose(turn[i][0:NT, 128:128 + P], factor[i][:], ident_sb[:]).then_inc(s_back, 1)

            @block.scalar
            def _(act):
                for i in L:
                    act.wait_ge(s_turned, i + 1)
                    act.activation(col[i][:], turn[i][:, 0:NT], ACT.Copy).then_inc(s_col, 1)
                for i in L:
                    act.wait_ge(s_back, i + 1)
                    act.activation(factor_row[i][:], turn[i][0:NT, 128:128 + P], ACT.Copy).then_inc(s_frow, 1)

            @block.gpsimd
            def _(pool):
                pool.memset(before[:], 1.0).then_inc(s_tri, 1)
                pool.wait_ge(s_tri, 1)
                pool.affine_select(out=before[:], in_=before[:], compare_op=ALU.is_gt, fill=0.0, base=0,
                                   pattern=[[-1, P]], channel_multiplier=1).then_inc(s_before, 1)

            @block.vector
            def _(dve):
                for i in L:
                    dve.memset(counts[i][:], 0.0).then_inc(s_zero, 1)
                dve.wait_ge(s_zero, B)
                dve.wait_ge(s_before, 1)
                step = Chain(dve, s_step)
                for i in L:
                    dve.wait_ge(s_ld[i], 32)
                    dve.wait_ge(s_col, i + 1)
                    for t in range(NT):
                        me = col[i][:, t:t + 1]
                        here = slice(t * P, (t + 1) * P)
                        if t > 0:
                            step.link(dve.tensor_scalar(scratch[:, 0:t * P], row[i][:, 0:t * P], me, 0.0,
                                                        ALU.is_ge, ALU.add, accum_out=counts[i][:, t, 0:1]))
                        if t < NT - 1:
                            step.link(dve.tensor_scalar(scratch[:, (t + 1) * P:N], row[i][:, (t + 1) * P:N], me, 0.0,
                                                        ALU.is_gt, ALU.add, accum_out=counts[i][:, t, 1:2]))
                        step.link(dve.scalar_tensor_tensor(out=tie[:], in0=row[i][:, here], scalar=me,
                                                           in1=before[:], op0=ALU.is_equal, op1=ALU.mult))
                        step.link(dve.scalar_tensor_tensor(out=scratch[:, here], in0=row[i][:, here], scalar=me,
                                                           in1=tie[:], op0=ALU.is_gt, op1=ALU.add,
                                                           accum_out=counts[i][:, t, 2:3]))
                    dve.tensor_reduce(rank[i][:], counts[i][:], AX.X, ALU.add).then_inc(s_rank, 1)
                    dve.wait_ge(s_rank, i + 1)
                    dve.scalar_tensor_tensor(out=factor[i][:], in0=rank[i][:], scalar=float(KEPT), in1=col[i][:],
                                             op0=ALU.is_lt, op1=ALU.mult).then_inc(s_factor, 1)
                for i in L:
                    dve.wait_ge(s_in[i], 2 * KC * 16)
                    dve.wait_ge(s_spread[i], 16)
                    for k in range(KC):
                        dve.tensor_tensor(delta[i][k][:], delta[i][k][:], spread[i][:], ALU.mult).then_inc(s_scaled, 1)
                        dve.wait_ge(s_scaled, i * KC + k + 1)
                        dve.tensor_tensor(base[i][k][:], base[i][k][:], delta[i][k][:], ALU.add).then_inc(s_done, 1)


def build(nc, a, out):
    qk_hi = nc.dram_tensor("qk_hi", (B, 4 * C, N), F32).ap()
    qk_lo = nc.dram_tensor("qk_lo", (B, 4 * C, N), F32).ap()
    v_rows = nc.dram_tensor("v_rows", (B * N, 2 * C), F32).ap()
    norm_and_project(nc, a["x"], a["wqk"], a["wv"], a["gmat"], qk_hi, qk_lo, v_rows)
    o_rows = nc.dram_tensor("o_rows", (VD, 1 + B * H0, N), F32).ap()
    differential_attention(nc, qk_hi, qk_lo, v_rows, [a[f"lambda_{n}"] for n in ("q1", "k1", "q2", "k2")],
                           a["ident"], a["fold"], o_rows)
    t_t = nc.dram_tensor("t_t", (B, C, N), F32).ap()
    a_t = nc.dram_tensor("a_t", (B, C, N), F32).ap()
    qk1_hi = nc.dram_tensor("qk1_hi", (B, 2 * C, N), F32).ap()
    qk1_lo = nc.dram_tensor("qk1_lo", (B, 2 * C, N), F32).ap()
    v1_rows = nc.dram_tensor("v1_rows", (B, N, C), F32).ap()
    head_norm_and_layer1_inputs(nc, a, o_rows, t_t, a_t, qk1_hi, qk1_lo, v1_rows)
    o1_t = nc.dram_tensor("o1_t", (B, C, N), F32).ap()
    causal_attention(nc, qk1_hi, qk1_lo, v1_rows, a["ident"], o1_t)
    t2_t = nc.dram_tensor("t2_t", (B, C, N), F32).ap()
    recurrence_gate_and_ffn(nc, a, o1_t, a_t, t_t, t2_t)
    logits = nc.dram_tensor("logits", (B, N), F32).ap()
    factors = nc.dram_tensor("factors", (B, N), F32).ap()
    base_t = nc.dram_tensor("base_t", (B, C, N), F32).ap()
    delta_t = nc.dram_tensor("delta_t", (B, C, N), F32).ap()
    routed_ffn(nc, a, t2_t, logits, base_t, delta_t)
    select_and_merge(nc, logits, factors, a["ident"], base_t, delta_t, out)


def layout(inputs):
    import numpy as np

    def tiles(w):
        w = np.asarray(w)
        return np.ascontiguousarray(w.reshape(-1, P, w.shape[1]).transpose(1, 0, 2))

    def columns(v):
        return np.ascontiguousarray(np.asarray(v).reshape(-1, P).T)

    a = {}
    a["x"] = np.ascontiguousarray(np.asarray(inputs["x"]).reshape(B, C, N))
    q_w, k_w, v_w = (np.asarray(inputs[f"L0_conv_{n}_w"]) for n in "qkv")
    a["wqk"] = tiles(np.concatenate([q_w, k_w]).T)
    a["wv"] = tiles(v_w.T)
    for n in ("q1", "k1", "q2", "k2"):
        a[f"lambda_{n}"] = np.ascontiguousarray(inputs[f"L0_conv_lambda_{n}"])
    a["ident"] = np.eye(P, dtype=np.float32)
    a["fold"] = np.concatenate([np.eye(VD, dtype=np.float32)] * 2)
    f = {k: np.asarray(v) for k, v in inputs.items()}
    a["out_w"] = tiles(f["L0_conv_out_w"].T)
    a["rms_scale"] = np.tile(f["L0_conv_rms_scale"].reshape(VD, 1), (2, 1))
    a["wqk1"] = tiles(f["L1_attn_qkv_w"][:, 0:2 * C])
    a["wv1"] = tiles(f["L1_attn_qkv_w"][:, 2 * C:])
    a["qk_bias1"] = np.ascontiguousarray(f["L1_attn_qkv_b"][0:2 * C].reshape(-1, P).T)
    a["v_bias1"] = np.ascontiguousarray(f["L1_attn_qkv_b"][2 * C:])
    of_head = (np.arange(2 * C)[:, None] // VD == np.arange(H0)[None, :]).astype(np.float32)
    a["to_heads"] = tiles(of_head / np.float32(VD))
    a["from_heads"] = np.ascontiguousarray(of_head.reshape(-1, P, H0).transpose(2, 0, 1))
    a["mean_mat"] = np.full((P, P), 1.0 / C, np.float32)
    for n in ("o_w", "rq_w", "rk_w", "rv_w", "ro_w", "cg_w", "ffn_w1", "ffn_w2"):
        a[n] = tiles(f[f"L1_attn_{n}"])
    for n in ("o_b", "rq_b", "rk_b", "ro_b", "cg_b", "ffn_b1", "ffn_b2", "ln1_g", "ln1_b", "ln2_g", "ln2_b",
              "ln3_g", "ln3_b"):
        a[n] = columns(f[f"L1_attn_{n}"])
    a["rv_b"] = f["L1_attn_rv_b"]
    for n in ("w1", "w2", "wr"):
        a[n] = tiles(f[f"L1_ffn_{n}"])
    a["wr"] = a["wr"].reshape(P, KC)
    a["br"] = f["L1_ffn_br"].reshape(1, 1)
    a["b1"], a["b2"] = columns(f["L1_ffn_b1"]), columns(f["L1_ffn_b2"])
    group = np.arange(P) // 8
    a["gmat"] = (group[:, None] == group[None, :]).astype(np.float32) / np.float32(8)
    return a


def kernel(**inputs):
    import numpy as np
    import concourse.bacc as bacc
    from concourse import mybir as mb
    from concourse.bass_utils import run_bass_kernel_spmd as run

    nc = bacc.Bacc("TRN2", target_bir_lowering=False, num_devices=1)
    arrays, a = {}, {}
    for name, value in layout(inputs).items():
        arrays[f"in_{name}"] = value
        a[name] = nc.dram_tensor(f"in_{name}", value.shape, mb.dt.from_np(value.dtype), kind="ExternalInput").ap()
    out = nc.dram_tensor("out", (B, C, N), F32, kind="ExternalOutput").ap()
    build(nc, a, out)
    r = run(nc, [arrays], core_ids=[0])
    return r.results[0]["out"].reshape(B, C, 48, 48)
```

```python
import math
from contextlib import ExitStack

import concourse.bass as bass
from concourse import mybir

F32 = mybir.dt.float32
F32R = mybir.dt.float32r
BF16 = mybir.dt.bfloat16
ALU = mybir.AluOpType
ACT = mybir.ActivationFunctionType
AX = mybir.AxisListType

P = 128
B = 2
C = 256
KC = C // P
N = 48 * 48
T = 384
NC = N // T
SUB = T // P
NT = N // P
H0 = 8
HD = 32
VD = 2 * HD
GN_EPS = 1e-5
LN_EPS = 1e-5
EPS_REC = 1e-6
GN_STEPS = 6
LAMBDA_INIT = 0.8 - 0.6 * math.exp(-0.3)


class Chain:

    def __init__(self, eng, sem, base=0):
        self.eng, self.sem, self.base, self.n = eng, sem, base, 0

    def link(self, ins, pad=None):
        self.n += 1
        ins.then_inc(self.sem, 1)
        self.eng.wait_ge(self.sem, self.base + self.n)
        if pad is not None:
            self.eng.memset(pad[:], 0.0)


def tools(nc, ctx, tag):
    def sb(name, shape, dt=F32):
        return ctx.enter_context(nc.sbuf_tensor(f"{tag}_{name}", shape, dt))

    def ps(name, shape):
        return ctx.enter_context(nc.psum_tensor(f"{tag}_{name}", shape, F32))

    used = []

    def sem(name):
        used.append(ctx.enter_context(nc.semaphore(f"{tag}_{name}")))
        return used[-1]

    def clear():
        with nc.Block() as block:
            @block.gpsimd
            def _(pool):
                for s in used:
                    pool.sem_clear(s)
    ctx.callback(clear)
    return sb, ps, sem


def norm_and_project(nc, x, wqk, wv, gmat, qk_hi, qk_lo, v_rows):
    MQK = 4 * C // P
    QB, VB = 4, 3
    with ExitStack() as ctx:
        sb, ps, sem = tools(nc, ctx, "proj")
        x_sb = sb("x", [P, B * KC, N])
        wqk_sb = sb("wqk", [P, KC, 4 * C])
        wv_sb = sb("wv", [P, KC, 2 * C])
        g_sb = sb("g", [P, P])
        stats = sb("stats", [P, KC, NC, 6])
        mv = sb("mv", [P, KC, 2])
        dev = sb("dev", [P, KC])
        dev2 = sb("dev2", [P, KC])
        spread = sb("spread", [P, KC])
        gmean = sb("gmean", [P, KC])
        std = sb("std", [P, KC])
        rstd = sb("rstd", [P, KC])
        shift = sb("shift", [P, KC])
        eps = sb("eps", [P, 1])
        pad = sb("pad", [P, 1])
        xn = [sb(f"xn{i}", [P, KC, T]) for i in range(2)]
        hi = [sb(f"hi{i}", [P, MQK, T], F32R) for i in range(2)]
        lo = [sb(f"lo{i}", [P, MQK, T], F32R) for i in range(2)]
        vst = [sb(f"vst{i}", [P, SUB, 2 * C]) for i in range(2)]
        qk_ps = [ps(f"qk{i}", [P, 512]) for i in range(QB)]
        v_ps = [ps(f"v{i}", [P, 512]) for i in range(VB)]
        gn_ps = ps("gn", [P, 512])
        s_w, s_x = sem("w"), sem("x_loaded")
        s_gn, s_mean, s_spread, s_gmean, s_gvar, s_std = (sem(n) for n in (
            "gn_step", "mean_ready", "spread_ready", "gmean_mm", "gvar_mm", "std_ready"))
        s_xn, s_qk, s_v = sem("xn_ready"), sem("qk_mm"), sem("v_mm")
        s_hi, s_lo, s_vst = sem("hi_done"), sem("lo_done"), sem("v_staged")
        s_out = [sem(f"stored{i}") for i in range(2)]
        s_eps = sem("eps")
        OUTS = 48

        with nc.Block() as block:
            @block.sync
            def _(sp):
                for i in range(2):
                    sp.sem_inc(s_out[i], 1)
                sp.dma_start(x_sb[:, 0:KC, :], x[0].rearrange("(k p) n -> p k n", p=P)).then_inc(s_x, 16)
                sp.dma_start(g_sb[:], gmat).then_inc(s_w, 16)
                sp.dma_start(wqk_sb[:], wqk).then_inc(s_w, 16)
                sp.dma_start(wv_sb[:], wv).then_inc(s_w, 16)
                for b in range(1, B):
                    sp.wait_ge(s_x, b * 16)
                    sp.dma_start(x_sb[:, b * KC:(b + 1) * KC, :], x[b].rearrange("(k p) n -> p k n", p=P)
                                 ).then_inc(s_x, 16)
                with sp.Fori(0, B) as b:
                    with sp.Fori(0, NC // 2) as i:
                        for par in range(2):
                            g = b * NC + i * 2 + par
                            cols = bass.ds((i * 2 + par) * T, T)
                            sp.wait_ge(s_lo, g * MQK + MQK + QB)
                            sp.dma_start(qk_hi.rearrange("b (m p) n -> p (b m) n", p=P)[
                                :, bass.ds(b * MQK, MQK), cols], hi[par][:].bitcast(F32)).then_inc(s_out[par], 16)
                            sp.dma_start(qk_lo.rearrange("b (m p) n -> p (b m) n", p=P)[
                                :, bass.ds(b * MQK, MQK), cols], lo[par][:].bitcast(F32)).then_inc(s_out[par], 16)
                            sp.wait_ge(s_vst, g * SUB + SUB + VB)
                            sp.dma_start(v_rows.rearrange("(t p) c -> p t c", p=P)[
                                :, bass.ds(g * SUB, SUB), :], vst[par][:]).then_inc(s_out[par], 16)
                for i in range(2):
                    sp.wait_ge(s_out[i], B * NC // 2 * OUTS + 1)

            @block.tensor
            def _(pe):
                pe.sem_inc(s_v, 2 * SUB)
                pe.wait_ge(s_w, 48)
                with pe.Fori(0, B) as b:
                    pe.wait_ge(s_mean, b + 1)
                    pe.matmul(gn_ps[:, 0:KC], g_sb[:], mv[:, :, 0], start=True, stop=True).then_inc(s_gmean, 1)
                    pe.wait_ge(s_spread, b + 1)
                    pe.matmul(gn_ps[:, KC:2 * KC], g_sb[:], spread[:], start=True, stop=True).then_inc(s_gvar, 1)
                    with pe.Fori(0, NC // 2) as i:
                        for par in range(2):
                            g = b * NC + i * 2 + par
                            pe.wait_ge(s_xn, (g + 1) * KC + 1)
                            for m in range(MQK):
                                pe.wait_ge(s_lo, g * MQK + m + 1)
                                for k in range(KC):
                                    mm = pe.matmul(qk_ps[m % QB][:, 0:T], wqk_sb[:, k, m * P:(m + 1) * P],
                                                   xn[par][:, k, :], start=k == 0, stop=k == KC - 1)
                                mm.then_inc(s_qk, 1)
                            for s in range(SUB):
                                pe.wait_ge(s_vst, g * SUB + s + 1)
                                for k in range(KC):
                                    mm = pe.matmul(v_ps[s][:, :], xn[par][:, k, s * P:(s + 1) * P],
                                                   wv_sb[:, k, :], start=k == 0, stop=k == KC - 1)
                                mm.then_inc(s_v, 1)

            @block.scalar
            def _(act):
                act.sem_inc(s_vst, VB)
                with act.Fori(0, B) as b:
                    act.wait_ge(s_gvar, b + 1)
                    act.wait_ge(s_eps, 1)
                    act.activation(std[:], gn_ps[:, KC:2 * KC], ACT.Sqrt, bias=eps[:, 0:1]).then_inc(s_std, 1)
                    with act.Fori(0, NC // 2) as i:
                        for par in range(2):
                            g = b * NC + i * 2 + par
                            act.wait_ge(s_out[par], (b * (NC // 2) + i) * OUTS + 1)
                            for m in range(MQK):
                                act.wait_ge(s_qk, g * MQK + m + 1)
                                act.activation(hi[par][:, m, :], qk_ps[m % QB][:, 0:T], ACT.Copy).then_inc(s_hi, 1)
                            for s in range(SUB):
                                act.wait_ge(s_v, g * SUB + s + 1 + 2 * SUB)
                                act.activation(vst[par][:, s, :], v_ps[s][:, :], ACT.Copy).then_inc(s_vst, 1)

            @block.vector
            def _(dve):
                dve.sem_inc(s_lo, QB)
                dve.sem_inc(s_xn, 1)
                dve.memset(eps[:], GN_EPS).then_inc(s_eps, 1)
                with dve.Fori(0, B) as b:
                    step = Chain(dve, s_gn, b * GN_STEPS)
                    dve.wait_ge(s_x, (b + 1) * 16)
                    for k in range(KC):
                        for c in range(NC):
                            ins = dve.bn_stats(stats[:, k, c, :], x_sb[
                                :, bass.ds(b * KC + k, 1), c * T:(c + 1) * T].rearrange("p a n -> p (a n)"))
                    step.link(ins, pad=pad)
                    for k in range(KC):
                        ins = dve.bn_aggr(mv[:, k, :], stats[:, k, :, :])
                    ins.then_inc(s_mean, 1)
                    dve.wait_ge(s_mean, b + 1)
                    dve.wait_ge(s_gmean, b + 1)
                    step.link(dve.tensor_copy(gmean[:], gn_ps[:, 0:KC]))
                    step.link(dve.tensor_tensor(dev[:], mv[:, :, 0], gmean[:], ALU.subtract))
                    step.link(dve.tensor_tensor(dev2[:], dev[:], dev[:], ALU.mult))
                    dve.tensor_tensor(spread[:], dev2[:], mv[:, :, 1], ALU.add).then_inc(s_spread, 1)
                    dve.wait_ge(s_std, b + 1)
                    step.link(dve.reciprocal(rstd[:], std[:]))
                    step.link(dve.scalar_tensor_tensor(out=shift[:], in0=gmean[:], scalar=-1.0, in1=rstd[:],
                                                       op0=ALU.mult, op1=ALU.mult), pad=pad)
                    assert step.n == GN_STEPS
                    with dve.Fori(0, NC // 2) as i:
                        for par in range(2):
                            c = i * 2 + par
                            g = b * NC + c
                            dve.wait_ge(s_v, g * SUB + SUB)
                            for k in range(KC):
                                dve.tensor_scalar(xn[par][:, k, :], x_sb[
                                                      :, bass.ds(b * KC + k, 1), bass.ds(c * T, T)].rearrange(
                                                          "p a n -> p (a n)"),
                                                  rstd[:, k:k + 1], shift[:, k:k + 1],
                                                  ALU.mult, ALU.add).then_inc(s_xn, 1)
                            for m in range(MQK):
                                dve.wait_ge(s_qk, g * MQK + m + 1)
                                dve.wait_ge(s_hi, g * MQK + m + 1)
                                dve.tensor_tensor(lo[par][:, m, :], qk_ps[m % QB][:, 0:T],
                                                  hi[par][:, m, :].bitcast(F32), ALU.subtract).then_inc(s_lo, 1)


def differential_attention(nc, qk_hi, qk_lo, v_rows, lambdas, ident, fold, o_rows):
    PARTS = 3
    ROWS = PARTS * HD
    HEADS = B * H0
    STEPS = NT
    BANKS = 3
    PBUF = 6
    LOADS = 2 * 2 * PARTS + 1
    UNITS = 2 * SUB * NC
    ROWS_STEP = STEPS - 2
    SUMS_STEP, COMBINE_STEP = 3, 9
    SCALE = HD ** -0.5
    on_dve = [g for g in range(STEPS) if g % 4 == 3]
    on_pool = [g for g in range(STEPS) if g not in on_dve]
    ND, NPOOL = len(on_dve) - 1, len(on_pool) - 1
    with ExitStack() as ctx:
        sb, ps, sem = tools(nc, ctx, "diff")
        ks = [[sb(f"ks{i}{j}", [ROWS + 1, N], F32R) for j in range(2)] for i in range(2)]
        qs = [[sb(f"qs{i}{j}", [ROWS + 1, N], F32R) for j in range(2)] for i in range(2)]
        vs = [sb(f"vs{i}", [P, NT, 2, VD]) for i in range(2)]
        q_now = sb("q_now", [ROWS, 2, T], F32R)
        probs = [sb(f"probs{i}", [P, 2 * T]) for i in range(PBUF)]
        run_pool = sb("run_pool", [P, 2 * T])
        sum_pool = sb("sum_pool", [P, 2 * T])
        run_dve = sb("run_dve", [P, 2 * T])
        sum_dve = sb("sum_dve", [P, 2 * T])
        maxes = sb("maxes", [P, 2 * SUB, NC])
        neg_max = sb("neg_max", [P, 2 * SUB])
        out_sb = sb("out", [P, T])
        recip = sb("recip", [P, T])
        normed = sb("normed", [P, T])
        combined = sb("combined", [VD, T])
        ones = sb("ones", [P, VD])
        ident_sb = sb("ident", [P, P])
        fold_sb = sb("fold", [P, VD])
        lam_in = sb("lam_in", [P, 4, C])
        lam_prod = sb("lam_prod", [P, 2, C])
        lam_sum = sb("lam_sum", [P, 2, H0])
        lam_exp = sb("lam_exp", [P, 2, H0])
        lam_diff = sb("lam_diff", [P, H0])
        neg_lam = sb("neg_lam", [P, HEADS])
        scores = [ps(f"scores{i}", [P, 512]) for i in range(BANKS)]
        max_ps = [ps(f"max{i}", [P, 512]) for i in range(BANKS)]
        out_ps = ps("out_ps", [P, 512])
        misc = ps("misc", [P, 512])
        s_const, s_ones, s_lam, s_lamexp, s_lamready = (sem(n) for n in (
            "const", "ones", "lam_step", "lam_exp", "lam_ready"))
        s_ld = [sem(f"loaded{i}") for i in range(2)]
        s_vs, s_qnow = sem("values_ready"), sem("q_now_ready")
        s_st, s_exp, s_pv, s_accp, s_accd = (sem(n) for n in (
            "scores_mm", "exp_done", "pv_mm", "sum_pool_done", "sum_dve_done"))
        s_mx, s_red, s_neg, s_rows, s_row = (sem(n) for n in (
            "max_mm", "max_taken", "neg_max_ready", "rows_mm", "rows_placed"))
        s_oev, s_l, s_rec, s_norm, s_comb, s_cout, s_st_o = (sem(n) for n in (
            "out_taken", "sums_mm", "recip_done", "normed_ready", "combined_mm", "combined_taken", "stored"))

        busy = [SUMS_STEP + 1 + s for s in range(SUB)] + [g + 1 for g in on_dve[1:]]
        per_step = [1 if g in busy else 3 for g in range(ROWS_STEP)]
        per_step[0] = per_step[COMBINE_STEP - 2] = 2
        assert sum(per_step) == UNITS

        def units_at(g):
            return list(range(sum(per_step[:g]), sum(per_step[:g + 1])))

        with nc.Block() as block:
            @block.sync
            def _(sp):
                sp.dma_start(ident_sb[:], ident).then_inc(s_const, 16)
                sp.dma_start(fold_sb[:], fold).then_inc(s_const, 16)
                for i, l in enumerate(lambdas):
                    sp.dma_start(lam_in[:, i, :], l.rearrange("h d -> (h d)").partition_broadcast(P)).then_inc(s_const, 16)

                qh = qk_hi.rearrange("b (h j d) n -> (b h) j d n", j=2, d=HD)
                ql = qk_lo.rearrange("b (h j d) n -> (b h) j d n", j=2, d=HD)

                def load(par, b, h):
                    for j in range(2):
                        for dst, kind, parts in ((qs, 0, (qh, qh, ql)), (ks, 1, (qh, ql, qh))):
                            for r, src in enumerate(parts):
                                sp.dma_start(dst[par][j][r * HD:(r + 1) * HD, :].bitcast(F32),
                                             src[bass.ds(b * 2 * H0 + kind * H0 + h, 1), j, :, :].rearrange(
                                                 "a d n -> (a d) n")).then_inc(s_ld[par], 16)
                    sp.dma_start(vs[par][:, :, 0, :], v_rows.rearrange("(t p) c -> p t c", p=P)[
                        :, bass.ds(b * NT, NT), bass.ds(h * VD, VD)]).then_inc(s_ld[par], 16)

                with sp.Fori(0, B) as b:
                    with sp.Fori(0, H0 // 2) as i:
                        for par in range(2):
                            sp.wait_ge(s_comb, (b * H0 + i * 2 + par) * NC + NC + 1)
                            load(par, b, i * 2 + par)
                sp.wait_ge(s_comb, HEADS * NC + NC + 1)
                load(0, 0, 0)
                sp.wait_ge(s_ld[0], (HEADS // 2 + 1) * LOADS * 16)
                sp.wait_ge(s_ld[1], HEADS // 2 * LOADS * 16)

            @block.tensor
            def _(pe):
                pe.sem_inc(s_comb, 2 * NC)
                pe.sem_inc(s_mx, 2 * UNITS)
                pe.sem_inc(s_st, 2 * STEPS)
                pe.sem_inc(s_pv, PBUF + STEPS)
                pe.sem_inc(s_rows, 1)
                pe.wait_ge(s_const, 16 * 6)
                pe.wait_ge(s_ones, 5)

                def score_step(par, q, c, g):
                    if g == 0:
                        pe.wait_ge(s_row, q * 2 + 2)
                    for j in range(2):
                        pe.wait_ge(s_exp, (q * STEPS + g) * 2 + j + 1)
                        pe.matmul(scores[(2 * g + j) % BANKS][:, 0:T], ks[par][j][:, g * P:(g + 1) * P],
                                  qs[par][j][:, bass.ds(c * T, T)], start=True, stop=True).then_inc(s_st, 1)

                def max_unit(par, q1, u):
                    j, s, k = u // (SUB * NC), u // NC % SUB, u % NC
                    if u % (SUB * NC) == 0:
                        pe.wait_ge(s_qnow, q1 * 2 + j + 1)
                    pe.wait_ge(s_red, q1 * UNITS + u + 1)
                    pe.matmul(max_ps[u % BANKS][:, 0:T], q_now[:, j, s * P:(s + 1) * P],
                              ks[par][j][0:ROWS, k * T:(k + 1) * T], start=True, stop=True).then_inc(s_mx, 1)

                def pv_step(par, q, g, n=None):
                    if g == 0 and n is not None:
                        pe.wait_ge(s_vs, n + 1)
                    if g == 0:
                        pe.wait_ge(s_oev, q)
                    pe.wait_ge(s_exp, (q * STEPS + g) * 2 + 2 + BANKS)
                    for j in range(2):
                        mm = pe.matmul(out_ps[64 * j:64 * j + VD, 0:T], vs[par][:, g, j, :],
                                       probs[g % PBUF][:, j * T:(j + 1) * T], start=g == 0, stop=g == STEPS - 1,
                                       tile_position=(0, 64 * j))
                    mm.then_inc(s_pv, 1)

                def rows(q1, first=False):
                    if not first:
                        pe.wait_ge(s_cout, q1 - 1)
                    pe.wait_ge(s_neg, q1 + 1)
                    for j in range(2):
                        for s in range(SUB):
                            mm = pe.matmul(misc[32 * j:32 * j + 1, s * P:(s + 1) * P],
                                           neg_max[:, j * SUB + s:j * SUB + s + 1], ident_sb[:],
                                           start=True, stop=True, tile_position=(0, 32 * j))
                    mm.then_inc(s_rows, 1)

                def sums(q):
                    pe.wait_ge(s_row, q * 2 + 4)
                    pe.wait_ge(s_accp, (q + 2) * NPOOL)
                    pe.wait_ge(s_accd, (q + 2) * ND)
                    for j in range(2):
                        for k, part in enumerate((sum_pool, sum_dve)):
                            mm = pe.matmul(misc[64 * j:64 * j + VD, 0:T], ones[:],
                                           part[:, j * T:(j + 1) * T], start=k == 0, stop=k == 1,
                                           tile_position=(0, 64 * j))
                    mm.then_inc(s_l, 1)

                def combine(q):
                    pe.wait_ge(s_norm, q + 2)
                    pe.matmul(misc[0:VD, 0:T], fold_sb[:], normed[:], start=True, stop=True).then_inc(s_comb, 1)

                def slot(par, q, c, next_par, n=None):
                    for g in range(STEPS):
                        units = units_at(g)
                        before, between = (units[:1], units[1:2]) if len(units) == 3 else ([], units[:1])
                        for u in before:
                            max_unit(next_par, q + 1, u)
                        score_step(par, q, c, g)
                        for u in between:
                            max_unit(next_par, q + 1, u)
                        if g > 0:
                            pv_step(par, q, g - 1, n)
                        for u in units[len(before + between):]:
                            max_unit(next_par, q + 1, u)
                        if g == SUMS_STEP:
                            sums(q - 1)
                        if g == COMBINE_STEP:
                            combine(q - 1)
                        if g == ROWS_STEP:
                            rows(q + 1)
                    pv_step(par, q, STEPS - 1)

                pe.wait_ge(s_ld[0], LOADS * 16)
                for u in range(UNITS):
                    max_unit(0, 1, u)
                rows(1, first=True)
                with pe.Fori(0, HEADS // 2) as i:
                    for par in range(2):
                        n = i * 2 + par
                        slot(par, n * NC + 1, 0, par, n)
                        with pe.Fori(1, NC - 1) as c:
                            slot(par, n * NC + c + 1, c, par)
                        pe.wait_ge(s_ld[1 - par], (i + 1 + par) * LOADS * 16)
                        slot(par, n * NC + NC, NC - 1, 1 - par)
                sums(HEADS * NC)
                combine(HEADS * NC)

            @block.scalar
            def _(act):
                act.sem_inc(s_exp, BANKS + 2 * STEPS)
                act.sem_inc(s_row, 2)
                act.sem_inc(s_qnow, 2)
                act.sem_inc(s_st_o, 1)

                def stage_queries(par, q1, c1, j):
                    act.wait_ge(s_mx, q1 * UNITS + (j + 1) * (UNITS // 2))
                    act.activation(q_now[:, j, :], qs[par][j][0:ROWS, bass.ds(c1 * T, T)].bitcast(F32),
                                   ACT.Copy).then_inc(s_qnow, 1)

                def place_rows(par, q1, c1):
                    act.wait_ge(s_rows, q1 + 1)
                    act.activation(qs[par][0][ROWS:ROWS + 1, bass.ds(c1 * T, T)], misc[0:1, 0:T],
                                   ACT.Copy).then_inc(s_row, 1)

                def take_out(q):
                    act.wait_ge(s_norm, q + 1)
                    act.wait_ge(s_pv, (q + 1) * STEPS + PBUF)
                    act.activation(out_sb[:], out_ps[:, 0:T], ACT.Copy).then_inc(s_oev, 1)

                def take_combined(q):
                    act.wait_ge(s_comb, q + 1 + 2 * NC)
                    act.wait_ge(s_st_o, q * 16 + 1)
                    act.activation(combined[:], misc[0:VD, 0:T], ACT.Copy).then_inc(s_cout, 1)

                def store_combined(q, n, c):
                    act.wait_ge(s_cout, q + 1)
                    act.dma_start(o_rows[:, bass.ds(n + 1, 1), bass.ds(c * T, T)], combined[:]).then_inc(s_st_o, 16)

                def slot(par, q, next_par, c1, n_prev, c_prev):
                    for g in range(STEPS):
                        if g == 0:
                            stage_queries(next_par, q + 1, c1, 0)
                        if UNITS // 2 - 1 in units_at(g):
                            stage_queries(next_par, q + 1, c1, 1)
                        act.wait_ge(s_pv, q * STEPS + g + 1)
                        back = (g - PBUF) % STEPS
                        lap = 1 if g >= PBUF else 0
                        if back in on_pool:
                            act.wait_ge(s_accp, (q + lap) * NPOOL + max(on_pool.index(back), 1))
                        else:
                            act.wait_ge(s_accd, (q + lap) * ND + max(on_dve.index(back), 1))
                        for j in range(2):
                            act.wait_ge(s_st, (q * STEPS + g) * 2 + j + 1)
                            act.activation(probs[g % PBUF][:, j * T:(j + 1) * T],
                                           scores[(2 * g + j) % BANKS][:, 0:T], ACT.Exp, scale=SCALE
                                           ).then_inc(s_exp, 1)
                        if g == 0:
                            take_out(q - 1)
                        if g == COMBINE_STEP + 1:
                            take_combined(q - 1)
                        if g == COMBINE_STEP + 2:
                            store_combined(q - 1, n_prev, c_prev)
                        if g == ROWS_STEP:
                            place_rows(next_par, q + 1, c1)

                act.wait_ge(s_lam, 2)
                act.activation(lam_exp[:], lam_sum[:], ACT.Exp).then_inc(s_lamexp, 1)
                act.wait_ge(s_ld[0], LOADS * 16)
                for j in range(2):
                    act.activation(q_now[:, j, :], qs[0][j][0:ROWS, 0:T].bitcast(F32), ACT.Copy).then_inc(s_qnow, 1)
                place_rows(0, 1, 0)
                with act.Fori(0, HEADS // 2) as i:
                    for par in range(2):
                        n = i * 2 + par
                        slot(par, n * NC + 1, par, 1, n - 1, NC - 1)
                        with act.Fori(1, NC - 1) as c:
                            slot(par, n * NC + c + 1, par, c + 1, n, c - 1)
                        act.wait_ge(s_ld[1 - par], (i + 1 + par) * LOADS * 16)
                        slot(par, n * NC + NC, 1 - par, 0, n, NC - 2)
                take_out(HEADS * NC)
                take_combined(HEADS * NC)
                store_combined(HEADS * NC, HEADS - 1, NC - 1)
                act.wait_ge(s_st_o, (HEADS * NC + 1) * 16 + 1)

            @block.vector
            def _(dve):
                dve.sem_inc(s_red, BANKS + UNITS)
                dve.sem_inc(s_neg, 1)
                dve.sem_inc(s_accd, 2 * ND)
                dve.sem_inc(s_norm, 1)
                for par in range(2):
                    for j in range(2):
                        ins = dve.memset(ks[par][j][ROWS:ROWS + 1, :].bitcast(F32), 1.0)
                ins.then_inc(s_ones, 1)
                dve.memset(ones[:], 1.0).then_inc(s_ones, 1)
                dve.memset(sum_dve[:], 1.0).then_inc(s_ones, 1)
                dve.memset(out_ps[:, 0:T], 0.0).then_inc(s_ones, 1)
                dve.wait_ge(s_const, 16 * 6)
                step = Chain(dve, s_lam)
                for i in range(2):
                    ins = dve.tensor_tensor(lam_prod[:, i, :], lam_in[:, 2 * i, :], lam_in[:, 2 * i + 1, :], ALU.mult)
                step.link(ins)
                step.link(dve.tensor_reduce(lam_sum[:], lam_prod[:].rearrange("p i (h d) -> p i h d", d=HD),
                                            AX.X, ALU.add))
                dve.wait_ge(s_lamexp, 1)
                step.link(dve.tensor_tensor(lam_diff[:], lam_exp[:, 1, :], lam_exp[:, 0, :], ALU.subtract))
                for b in range(B):
                    ins = dve.tensor_scalar(neg_lam[:, b * H0:(b + 1) * H0], lam_diff[:], -LAMBDA_INIT, None, ALU.add)
                step.link(ins)

                def max_unit(q1, u):
                    dve.wait_ge(s_mx, (q1 + 1) * UNITS + u + 1)
                    dve.tensor_reduce(maxes[:, u // NC:u // NC + 1, u % NC], max_ps[u % BANKS][:, 0:T], AX.X,
                                      ALU.max).then_inc(s_red, 1)

                def negate(q1):
                    dve.wait_ge(s_rows, q1)
                    dve.wait_ge(s_red, q1 * UNITS + UNITS + BANKS)
                    dve.tensor_reduce(neg_max[:], maxes[:], AX.X, ALU.max, negate=True).then_inc(s_neg, 1)

                def add_up(q, g):
                    i = on_dve.index(g)
                    if i == 0:
                        return
                    dve.wait_ge(s_exp, (q * STEPS + g) * 2 + 2 + BANKS)
                    dve.wait_ge(s_accd, (q + 1) * ND + i - 1)
                    acc = probs[on_dve[0] % PBUF] if i == 1 else run_dve
                    to = sum_dve if i == ND else run_dve
                    dve.tensor_tensor(to[:], acc[:], probs[g % PBUF][:], ALU.add).then_inc(s_accd, 1)

                def invert(q, s):
                    if s == 0:
                        dve.wait_ge(s_l, q + 1)
                        dve.wait_ge(s_norm, q + 1)
                    dve.reciprocal(recip[:, s * P:(s + 1) * P], misc[:, s * P:(s + 1) * P]).then_inc(s_rec, 1)

                def normalise(q):
                    dve.wait_ge(s_oev, q + 1)
                    dve.wait_ge(s_rec, (q + 1) * SUB)
                    dve.tensor_tensor(normed[:], out_sb[:], recip[:], ALU.mult).then_inc(s_norm, 1)

                def place_rows(par, q1, c1):
                    dve.wait_ge(s_rows, q1 + 1)
                    dve.tensor_copy(qs[par][1][ROWS:ROWS + 1, bass.ds(c1 * T, T)], misc[32:33, 0:T]
                                    ).then_inc(s_row, 1)

                def slot(q, next_par, c1):
                    for g in range(STEPS):
                        for u in units_at(g):
                            max_unit(q + 1, u)
                        if g - 1 in on_dve:
                            add_up(q, g - 1)
                        if 0 < g - SUMS_STEP <= SUB:
                            invert(q - 1, g - SUMS_STEP - 1)
                        if g == COMBINE_STEP - 2:
                            normalise(q - 1)
                        if g == ROWS_STEP - 1:
                            negate(q + 1)
                        if g == ROWS_STEP:
                            place_rows(next_par, q + 1, c1)

                for u in range(UNITS):
                    max_unit(1, u)
                negate(1)
                place_rows(0, 1, 0)
                with dve.Fori(0, HEADS // 2) as i:
                    for par in range(2):
                        n = i * 2 + par
                        dve.wait_ge(s_lam, 4)
                        dve.wait_ge(s_ld[par], (i + 1) * LOADS * 16)
                        dve.tensor_scalar(vs[par][:, :, 1, :], vs[par][:, :, 0, :], neg_lam[:, bass.ds(n, 1)],
                                          None, ALU.mult).then_inc(s_vs, 1)
                        with dve.Fori(1, NC) as c:
                            slot(n * NC + c, par, c)
                        slot(n * NC + NC, 1 - par, 0)
                for s in range(SUB):
                    invert(HEADS * NC, s)
                normalise(HEADS * NC)

            @block.gpsimd
            def _(pool):
                pool.sem_inc(s_accp, 2 * NPOOL)
                pool.memset(sum_pool[:], 1.0).then_inc(s_ones, 1)

                def slot(q):
                    for i, g in enumerate(on_pool):
                        if i == 0:
                            continue
                        pool.wait_ge(s_exp, (q * STEPS + g) * 2 + 2 + BANKS)
                        pool.wait_ge(s_accp, (q + 1) * NPOOL + i - 1)
                        acc = probs[on_pool[0] % PBUF] if i == 1 else run_pool
                        to = sum_pool if i == NPOOL else run_pool
                        pool.tensor_tensor(to[:], acc[:], probs[g % PBUF][:], ALU.add).then_inc(s_accp, 1)

                with pool.Fori(1, HEADS * NC + 1) as q:
                    slot(q)


def run_stages(eng, order, stage):
    for name, i, behind in order:
        if not behind:
            stage(name, 0, i)
    with eng.Fori(1, NC) as c:
        for name, i, behind in order:
            stage(name, c - behind, i)
    for name, i, behind in order:
        if behind:
            stage(name, NC - 1, i)


def run_stages(eng, order, stage):
    for name, i, behind in order:
        if not behind:
            stage(name, 0, i)
    with eng.Fori(1, NC) as c:
        for name, i, behind in order:
            stage(name, c - behind, i)
    for name, i, behind in order:
        if behind:
            stage(name, NC - 1, i)


def nth(c, lane):
    return c * B + lane + 1


def head_norm_and_layer1_inputs(nc, a, o_rows, t_rows, a_t, qk_hi, qk_lo, v_rows):
    MO = 2 * C // P
    MQK = 2 * C // P
    ORDER = (
        ("square", 0, 0), ("head_std", 0, 0), ("mean", 1, 1), ("v", 0, 1), ("var", 1, 1), ("factors", 0, 0),
        ("qk", 1, 1), ("y", 0, 0), ("square", 1, 0), ("head_std", 1, 0), ("mean", 0, 0), ("v", 1, 1),
        ("var", 0, 0), ("factors", 1, 0), ("qk", 0, 0), ("y", 1, 0))
    with ExitStack() as ctx:
        sb, ps, sem = tools(nc, ctx, "mid")
        L = range(B)
        wo = sb("wo", [P, MO, C])
        wqk = sb("wqk", [P, KC, 2 * C])
        wv = sb("wv", [P, KC, C])
        qk_bias = sb("qk_bias", [P, MQK])
        v_bias = sb("v_bias", [P, C])
        to_heads = sb("to_heads", [P, MO, H0])
        from_heads = sb("from_heads", [H0, MO, P])
        mean_mat = sb("mean_mat", [P, P])
        gain = sb("gain", [P, 1])
        eps = sb("eps", [P, 1])
        o_in = [sb(f"o_in{i}", [P, MO, T]) for i in L]
        x_in = [sb(f"x_in{i}", [P, KC, T]) for i in L]
        o_sq = [sb(f"o_sq{i}", [P, MO, T]) for i in L]
        h_std = [sb(f"h_std{i}", [H0, T]) for i in L]
        h_rstd = [sb(f"h_rstd{i}", [H0, T]) for i in L]
        o_norm = [sb(f"o_norm{i}", [P, MO, T]) for i in L]
        t = [sb(f"t{i}", [P, KC, T]) for i in L]
        dev = [sb(f"dev{i}", [P, KC, T]) for i in L]
        dev_sq = [sb(f"dev_sq{i}", [P, KC, T]) for i in L]
        std = [sb(f"std{i}", [P, T]) for i in L]
        rstd = [sb(f"rstd{i}", [P, T]) for i in L]
        ln = [sb(f"ln{i}", [P, KC, T]) for i in L]
        hi = [sb(f"hi{i}", [P, MQK, T], F32R) for i in L]
        lo = [sb(f"lo{i}", [P, MQK, T], F32R) for i in L]
        v_out = [sb(f"v_out{i}", [P, SUB, C]) for i in L]
        bank = [[ps(f"bank{i}{k}", [P, 512]) for k in range(4)] for i in L]
        s_first, s_w, s_eps, s_gain = sem("first_weights"), sem("weights"), sem("eps"), sem("gain")
        s_ld = [sem(f"loaded{i}") for i in L]
        s_st_t = [sem(f"t_stored{i}") for i in L]
        s_st_q = [sem(f"qk_stored{i}") for i in L]
        s_st_v = [sem(f"v_stored{i}") for i in L]
        (s_osq, s_ms, s_hstd, s_hrstd, s_bc, s_onorm, s_y, s_t, s_mean, s_dev, s_dsq, s_var, s_std, s_rstd,
         s_ln, s_qk, s_hi, s_lo, s_v, s_vout) = ([sem(f"{n}{i}") for i in L] for n in (
             "o_squared", "head_ms_mm", "head_std", "head_rstd", "head_rstd_mm", "o_normed", "y_mm", "t_ready",
             "mean_mm", "dev_ready", "dev_squared", "var_mm", "std_ready", "rstd_ready", "ln_ready", "qk_mm",
             "hi_done", "lo_done", "v_mm", "v_done"))

        with nc.Block() as block:
            @block.sync
            def _(sp):
                for i in L:
                    sp.sem_inc(s_st_t[i], 1)
                    sp.sem_inc(s_st_q[i], 1)
                    sp.sem_inc(s_st_v[i], 1)

                def load(c, i):
                    cols = bass.ds(c * T, T)
                    for h in range(2):
                        sp.dma_start(o_in[i][h * VD:(h + 1) * VD, :, :],
                                     o_rows[:, bass.ds(1 + i * H0 + h, MO, step=2), cols]).then_inc(s_ld[i], 16)
                    sp.dma_start(x_in[i][:], a["x"][i].rearrange("(k p) n -> p k n", p=P)[:, :, cols]
                                 ).then_inc(s_ld[i], 16)

                def load_next(c, i):
                    sp.wait_ge(s_t[i], c + 1)
                    load(c + 1, i)

                def store_t(c, i):
                    cols = bass.ds(c * T, T)
                    sp.wait_ge(s_ln[i], c + 1)
                    sp.dma_start(t_rows[i].rearrange("(k p) n -> p k n", p=P)[:, :, cols], t[i][:]
                                 ).then_inc(s_st_t[i], 16)
                    sp.dma_start(a_t[i].rearrange("(k p) n -> p k n", p=P)[:, :, cols], ln[i][:]
                                 ).then_inc(s_st_t[i], 16)

                def store_qk(c, i):
                    cols = bass.ds(c * T, T)
                    sp.wait_ge(s_lo[i], (c + 2) * MQK)
                    sp.dma_start(qk_hi[i].rearrange("(m p) n -> p m n", p=P)[:, :, cols],
                                 hi[i][:].bitcast(F32)).then_inc(s_st_q[i], 16)
                    sp.dma_start(qk_lo[i].rearrange("(m p) n -> p m n", p=P)[:, :, cols],
                                 lo[i][:].bitcast(F32)).then_inc(s_st_q[i], 16)

                def store_v(c, i):
                    sp.wait_ge(s_vout[i], c + 2)
                    sp.dma_start(v_rows[i].rearrange("(t p) c -> p t c", p=P)[:, bass.ds(c * SUB, SUB), :],
                                 v_out[i][:]).then_inc(s_st_v[i], 16)

                for i in L:
                    load(0, i)
                for dst, src in ((to_heads, a["to_heads"]), (from_heads, a["from_heads"]),
                                 (gain, a["rms_scale"])):
                    sp.dma_start(dst[:], src).then_inc(s_first, 16)
                for dst, src in ((wo, a["out_w"]), (mean_mat, a["mean_mat"]), (wqk, a["wqk1"]),
                                 (wv, a["wv1"]), (qk_bias, a["qk_bias1"])):
                    sp.dma_start(dst[:], src).then_inc(s_w, 16)
                sp.dma_start(v_bias[:], a["v_bias1"].partition_broadcast(P)).then_inc(s_w, 16)
                with sp.Fori(0, NC - 1) as c:
                    load_next(c, 0)
                    store_t(c, 0)
                    store_qk(c, 0)
                    load_next(c, 1)
                    store_v(c, 0)
                    store_t(c, 1)
                    store_qk(c, 1)
                    store_v(c, 1)
                for i in L:
                    store_t(NC - 1, i)
                    store_qk(NC - 1, i)
                    store_v(NC - 1, i)
                for i in L:
                    sp.wait_ge(s_st_t[i], NC * 32 + 1)
                    sp.wait_ge(s_st_q[i], NC * 32 + 1)
                    sp.wait_ge(s_st_v[i], NC * 16 + 1)

            @block.tensor
            def _(pe):
                pe.wait_ge(s_first, 16 * 3)

                def stage(name, c, i):
                    if name == "square":
                        pe.wait_ge(s_osq[i], c + 1)
                        pe.wait_ge(s_lo[i], (c + 1) * MQK)
                        for m in range(MO):
                            mm = pe.matmul(bank[i][3][0:H0, 0:T], to_heads[:, m, :], o_sq[i][:, m, :],
                                           start=m == 0, stop=m == MO - 1)
                        mm.then_inc(s_ms[i], 1)
                    elif name == "factors":
                        pe.wait_ge(s_hrstd[i], c + 1)
                        pe.wait_ge(s_vout[i], c + 1)
                        for m in range(MO):
                            mm = pe.matmul(bank[i][m][:, 0:T], from_heads[:, m, :], h_rstd[i][:],
                                           start=True, stop=True)
                        mm.then_inc(s_bc[i], 1)
                    elif name == "y":
                        pe.wait_ge(s_w, 16 * 6)
                        pe.wait_ge(s_onorm[i], c + 1)
                        for h in range(KC):
                            for m in range(MO):
                                mm = pe.matmul(bank[i][h][:, 0:T], wo[:, m, h * P:(h + 1) * P],
                                               o_norm[i][:, m, :], start=m == 0, stop=m == MO - 1)
                        mm.then_inc(s_y[i], 1)
                    elif name == "mean":
                        pe.wait_ge(s_t[i], c + 1)
                        for k in range(KC):
                            mm = pe.matmul(bank[i][2][:, 0:T], mean_mat[:], t[i][:, k, :],
                                           start=k == 0, stop=k == KC - 1)
                        mm.then_inc(s_mean[i], 1)
                    elif name == "var":
                        pe.wait_ge(s_dsq[i], c + 1)
                        for k in range(KC):
                            mm = pe.matmul(bank[i][3][:, 0:T], mean_mat[:], dev_sq[i][:, k, :],
                                           start=k == 0, stop=k == KC - 1)
                        mm.then_inc(s_var[i], 1)
                    elif name == "qk":
                        pe.wait_ge(s_ln[i], c + 1)
                        for m in range(MQK):
                            for k in range(KC):
                                mm = pe.matmul(bank[i][m][:, 0:T], wqk[:, k, m * P:(m + 1) * P], ln[i][:, k, :],
                                               start=k == 0, stop=k == KC - 1)
                            mm.then_inc(s_qk[i], 1)
                    elif name == "v":
                        pe.wait_ge(s_lo[i], (c + 2) * MQK)
                        for s in range(SUB):
                            for k in range(KC):
                                mm = pe.matmul(bank[i][s][:, 0:C], ln[i][:, k, s * P:(s + 1) * P], wv[:, k, :],
                                               start=k == 0, stop=k == KC - 1)
                        mm.then_inc(s_v[i], 1)

                run_stages(pe, ORDER, stage)

            @block.scalar
            def _(act):
                act.wait_ge(s_eps, 1)

                def stage(name, c, i):
                    if name == "square":
                        act.wait_ge(s_ld[i], (c + 1) * 48)
                        act.activation(o_sq[i][:], o_in[i][:], ACT.Square).then_inc(s_osq[i], 1)
                    elif name == "head_std":
                        act.wait_ge(s_ms[i], c + 1)
                        act.activation(h_std[i][:], bank[i][3][0:H0, 0:T], ACT.Sqrt,
                                       bias=eps[0:H0, 0:1]).then_inc(s_hstd[i], 1)
                    elif name == "mean":
                        act.wait_ge(s_dev[i], c + 1)
                        act.activation(dev_sq[i][:], dev[i][:], ACT.Square).then_inc(s_dsq[i], 1)
                    elif name == "var":
                        act.wait_ge(s_var[i], c + 1)
                        act.activation(std[i][:], bank[i][3][:, 0:T], ACT.Sqrt, bias=eps[:, 0:1]
                                       ).then_inc(s_std[i], 1)
                    elif name == "qk":
                        act.wait_ge(s_st_q[i], c * 32 + 1)
                        act.wait_ge(s_w, 16 * 6)
                        for m in range(MQK):
                            act.wait_ge(s_qk[i], c * MQK + m + 1)
                            act.activation(hi[i][:, m, :], bank[i][m][:, 0:T], ACT.Identity,
                                           bias=qk_bias[:, m:m + 1]).then_inc(s_hi[i], 1)

                run_stages(act, ORDER, stage)

            @block.vector
            def _(dve):
                for i in L:
                    dve.sem_inc(s_vout[i], 1)
                    dve.sem_inc(s_lo[i], MQK)
                dve.memset(eps[:], LN_EPS).then_inc(s_eps, 1)
                dve.wait_ge(s_first, 16 * 3)
                dve.tensor_scalar(gain[:], gain[:], 1.0 - LAMBDA_INIT, None, ALU.mult).then_inc(s_gain, 1)
                dve.wait_ge(s_gain, 1)

                def stage(name, c, i):
                    if name == "head_std":
                        dve.wait_ge(s_hstd[i], c + 1)
                        dve.reciprocal(h_rstd[i][:], h_std[i][:]).then_inc(s_hrstd[i], 1)
                    elif name == "factors":
                        dve.wait_ge(s_bc[i], c + 1)
                        for m in range(MO):
                            ins = dve.scalar_tensor_tensor(out=o_norm[i][:, m, :], in0=o_in[i][:, m, :],
                                                           scalar=gain[:, 0:1], in1=bank[i][m][:, 0:T],
                                                           op0=ALU.mult, op1=ALU.mult)
                        ins.then_inc(s_onorm[i], 1)
                    elif name == "y":
                        dve.wait_ge(s_w, 16 * 6)
                        dve.wait_ge(s_y[i], c + 1)
                        dve.wait_ge(s_st_t[i], c * 32 + 1)
                        for k in range(KC):
                            ins = dve.tensor_tensor(t[i][:, k, :], x_in[i][:, k, :], bank[i][k][:, 0:T], ALU.add)
                        ins.then_inc(s_t[i], 1)
                    elif name == "mean":
                        dve.wait_ge(s_mean[i], c + 1)
                        for k in range(KC):
                            ins = dve.tensor_tensor(dev[i][:, k, :], t[i][:, k, :], bank[i][2][:, 0:T], ALU.subtract)
                        ins.then_inc(s_dev[i], 1)
                    elif name == "var":
                        dve.wait_ge(s_std[i], c + 1)
                        dve.reciprocal(rstd[i][:], std[i][:]).then_inc(s_rstd[i], 1)
                        dve.wait_ge(s_rstd[i], c + 1)
                        for k in range(KC):
                            ins = dve.tensor_tensor(ln[i][:, k, :], dev[i][:, k, :], rstd[i][:], ALU.mult)
                        ins.then_inc(s_ln[i], 1)
                    elif name == "qk":
                        for m in range(MQK):
                            dve.wait_ge(s_hi[i], c * MQK + m + 1)
                            dve.scalar_tensor_tensor(out=lo[i][:, m, :], in0=bank[i][m][:, 0:T],
                                                     scalar=qk_bias[:, m:m + 1], in1=hi[i][:, m, :].bitcast(F32),
                                                     op0=ALU.add, op1=ALU.subtract).then_inc(s_lo[i], 1)
                    elif name == "v":
                        dve.wait_ge(s_v[i], c + 1)
                        dve.wait_ge(s_st_v[i], c * 16 + 1)
                        for s in range(SUB):
                            ins = dve.tensor_tensor(v_out[i][:, s, :], bank[i][s][:, 0:C], v_bias[:], ALU.add)
                        ins.then_inc(s_vout[i], 1)

                run_stages(dve, ORDER, stage)


def causal_attention(nc, qk_hi, qk_lo, v_rows, ident, o_t):
    HN, DH = 4, C // 4
    PAIRS = HN // 2
    BANKS = 3
    PBUF = 6
    KV_LOADS, Q_LOADS = 7, 6
    SCALE = DH ** -0.5
    MASKED = -3e38
    assert B == 2 and PAIRS == 2
    SLOTS = PAIRS * NC
    steps = [SUB * (z % NC + 1) for z in range(SLOTS)]
    first = [sum(steps[:z]) for z in range(SLOTS + 1)]
    at_step = [(z, g) for z in range(SLOTS) for g in range(steps[z])]
    LAP = first[SLOTS]
    units = [[(j, s, k) for j in range(2) for s in range(SUB) for k in range(z % NC + 1)] for z in range(SLOTS)]
    ufirst = [sum(len(u) for u in units[:z]) for z in range(SLOTS + 1)]
    ULAP = ufirst[SLOTS]
    afirst = [sum(n - 1 for n in steps[:z]) for z in range(SLOTS + 1)]
    ALAP = afirst[SLOTS]
    PIECES = (0, 2), (2, NC)

    plan = [([], [], []) for _ in range(LAP)]
    pair_steps, ahead = first[NC], len(units[0]) + len(units[1])
    for z in range(SLOTS):
        par, c = divmod(z, NC)
        n = ufirst[NC] - ahead
        for u in range(len(units[z])):
            k = ufirst[z] - par * ufirst[NC] + u
            if c < 2:
                at = (par - 1) * pair_steps + first[NC - 1] + k * (steps[NC - 1] - 2) // ahead
            else:
                at = par * pair_steps + (k - ahead) * (first[NC - 1] - 1) // n
            lap = 1 if at < 0 else 0
            plan[at % LAP][0].append((lap, z, u))
        plan[at % LAP][1].append((lap, z))
        plan[(at + 1) % LAP][2].append((lap, z))
        assert at + 1 < first[z]

    def sums_step(z):
        return 0 if z % NC < 2 else 2

    def thirds_at(z, g):
        s = g - sums_step(z) - 1
        last = steps[z] - sums_step(z) - 2
        return [k for k in range(SUB) if min(k, last) == s]

    sums_at = [first[z] + sums_step(z) for z in range(1, SLOTS)] + [LAP]

    def rows_before(z):
        return sum(len(plan[at][2]) for at in range(min(sums_at[z] + 1, LAP)))

    def sums_before(at):
        return sum(1 for x in sums_at if x < at)

    with ExitStack() as ctx:
        sb, ps, sem = tools(nc, ctx, "causal")
        ka = [[sb(f"ka{i}{j}", [P, N], F32R) for j in range(2)] for i in range(2)]
        kb = [[sb(f"kb{i}{j}", [DH + 1, N], F32R) for j in range(2)] for i in range(2)]
        qa = [sb(f"qa{j}", [P, N], F32R) for j in range(2)]
        qb = [sb(f"qb{j}", [DH + 1, N], F32R) for j in range(2)]
        vs = [sb(f"vs{i}", [P, NT, 2, DH]) for i in range(2)]
        probs = [sb(f"probs{i}", [P, 2 * T]) for i in range(PBUF)]
        run_sum = sb("run_sum", [P, 2 * T])
        row_sum = sb("row_sum", [P, 2 * T])
        maxes = [sb(f"maxes{i}", [P, 2 * SUB, NC]) for i in range(2)]
        neg_max = sb("neg_max", [P, 2 * SUB])
        out_sb = sb("out", [P, T])
        recip = sb("recip", [P, T])
        normed = [sb(f"normed{i}", [P, T]) for i in range(2)]
        ones = sb("ones", [P, DH])
        ident_sb = sb("ident", [P, P])
        ident_bf = sb("ident_bf", [P, P], BF16)
        mask_q = sb("mask_q", [P, SUB, T], BF16)
        mask_k = sb("mask_k", [P, SUB, T], BF16)
        scores = [ps(f"scores{i}", [P, 512]) for i in range(BANKS)]
        max_ps = [ps(f"max{i}", [P, 512]) for i in range(BANKS)]
        out_ps = ps("out_ps", [P, 512])
        misc = ps("misc", [P, 512])
        s_const, s_ones, s_zero, s_mask = sem("const"), sem("ones"), sem("mask_zeroed"), sem("masks_ready")
        s_kv = [[sem(f"keys_loaded{i}{k}") for k in range(2)] for i in range(2)]
        s_q = [sem(f"queries_loaded{c}") for c in range(NC)]
        s_st, s_exp, s_pv, s_acc = (sem(n) for n in ("scores_mm", "exp_done", "pv_mm", "row_sum_done"))
        s_mx, s_red, s_neg, s_rows, s_row = (sem(n) for n in (
            "max_mm", "max_taken", "neg_max_ready", "rows_mm", "rows_placed"))
        s_oev, s_l, s_rec, s_norm = (sem(n) for n in ("out_taken", "sums_mm", "recip_done", "normed_ready"))
        s_store = [sem(f"stored{i}") for i in range(2)]

        with nc.Block() as block:
            @block.sync
            def _(sp):
                for i in range(2):
                    sp.sem_inc(s_store[i], 1)
                sp.dma_start(ident_sb[:], ident).then_inc(s_const, 16)
                hi, lo = (x.rearrange("b (x h j d) n -> (b x h) j d n", x=2, h=PAIRS, j=2)
                          for x in (qk_hi, qk_lo))

                def load_queries(b, par, c):
                    cols = slice(c * T, (c + 1) * T)
                    for j in range(2):
                        for dst, row, src in ((qa, 0, hi), (qa, DH, hi), (qb, 0, lo)):
                            sp.dma_start(dst[j][row:row + DH, cols].bitcast(F32),
                                         src[b * 2 * PAIRS + par, j, :, cols]).then_inc(s_q[c], 16)

                def load_keys(b, par, piece):
                    start, end = PIECES[piece]
                    cols = slice(start * T, end * T)
                    for j in range(2):
                        for dst, row, src in ((ka, 0, hi), (ka, DH, lo), (kb, 0, hi)):
                            sp.dma_start(dst[par][j][row:row + DH, cols].bitcast(F32),
                                         src[b * 2 * PAIRS + PAIRS + par, j, :, cols]).then_inc(s_kv[par][piece], 16)
                    sp.dma_start(vs[par][:, start * SUB:end * SUB, :, :].rearrange("p t j d -> p t (j d)"),
                                 v_rows.rearrange("b (t p) c -> p (b t) c", p=P)[
                                     :, b * NT + start * SUB:b * NT + end * SUB,
                                     par * 2 * DH:(par + 1) * 2 * DH]).then_inc(s_kv[par][piece], 16)

                def store(b, z):
                    par, c = divmod(z, NC)
                    sp.wait_ge(s_norm, b * SLOTS + z + 2)
                    sp.dma_start(o_t[b][par * P:(par + 1) * P, c * T:(c + 1) * T],
                                 normed[z % 2][:]).then_inc(s_store[z % 2], 16)

                for c in range(2):
                    load_queries(0, 0, c)
                load_keys(0, 0, 0)
                load_keys(0, 0, 1)
                for c in range(2, NC):
                    load_queries(0, 0, c)
                for b in range(B):
                    for par in range(PAIRS):
                        nb, npar = (b, 1) if par == 0 else ((b + 1) % B, 0)
                        sp.wait_ge(s_pv, b * LAP + first[par * NC] + PBUF)
                        for piece in range(2):
                            load_keys(nb, npar, piece)
                        for c in range(NC):
                            z = par * NC + c
                            sp.wait_ge(s_pv, b * LAP + first[z + 1] + PBUF)
                            load_queries(nb, npar, c)
                            if c > 0:
                                store(b, z - 1)
                        store(b, par * NC + NC - 1)
                for i in range(2):
                    sp.wait_ge(s_store[i], B * SLOTS // 2 * 16 + 1)
                for piece in range(2):
                    sp.wait_ge(s_kv[0][piece], (B + 1) * KV_LOADS * 16)
                    sp.wait_ge(s_kv[1][piece], B * KV_LOADS * 16)
                for c in range(NC):
                    sp.wait_ge(s_q[c], (B * PAIRS + 1) * Q_LOADS * 16)

            @block.tensor
            def _(pe):
                pe.sem_inc(s_pv, PBUF)
                pe.sem_inc(s_rows, 1)
                pe.wait_ge(s_const, 16)
                pe.wait_ge(s_ones, 2)
                pe.wait_ge(s_mask, 3)

                def score_step(b, z, g):
                    par, c = divmod(z, NC)
                    if g == 0:
                        pe.wait_ge(s_row, (b * SLOTS + z + 1) * 2 + 1)
                    cols, keys = slice(c * T, (c + 1) * T), slice(g * P, (g + 1) * P)
                    diagonal = g - SUB * c
                    for j in range(2):
                        at = (first[z] + g) * 2 + j
                        pe.wait_ge(s_exp, b * 2 * LAP + at + 1)
                        to = scores[at % BANKS][:, 0:T]
                        pe.matmul(to, ka[par][j][:, keys], qa[j][:, cols], start=True, stop=False)
                        mm = pe.matmul(to, kb[par][j][:, keys], qb[j][:, cols], start=False, stop=diagonal < 0)
                        if diagonal >= 0:
                            mm = pe.matmul(to, ident_bf[:], mask_k[:, diagonal, :], start=False, stop=True)
                        mm.then_inc(s_st, 1)

                def max_unit(b, z, u):
                    par, c = divmod(z, NC)
                    if u == 0:
                        pe.wait_ge(s_q[c], (b * PAIRS + par + 1) * Q_LOADS * 16)
                        pe.wait_ge(s_kv[par][0 if c < PIECES[0][1] else 1], (b + 1) * KV_LOADS * 16)
                    j, s, k = units[z][u]
                    at = ufirst[z] + u
                    pe.wait_ge(s_red, b * ULAP + at + 1)
                    queries = slice(c * T + s * P, c * T + (s + 1) * P)
                    to, keys = max_ps[at % BANKS][:, 0:T], slice(k * T, (k + 1) * T)
                    pe.matmul(to, qa[j][:, queries], ka[par][j][:, keys], start=True, stop=False)
                    mm = pe.matmul(to, qb[j][0:DH, queries], kb[par][j][0:DH, keys], start=False, stop=k < c)
                    if k == c:
                        mm = pe.matmul(to, ident_bf[:], mask_q[:, s, :], start=False, stop=True)
                    mm.then_inc(s_mx, 1)

                def pv_step(b, z, g):
                    if g == 0:
                        pe.wait_ge(s_oev, b * SLOTS + z + 1)
                    pe.wait_ge(s_exp, (b * LAP + first[z] + g) * 2 + 2 + BANKS)
                    for j in range(2):
                        mm = pe.matmul(out_ps[DH * j:DH * (j + 1), 0:T], vs[z // NC][:, g, j, :],
                                       probs[(first[z] + g) % PBUF][:, j * T:(j + 1) * T],
                                       start=g == 0, stop=g == steps[z] - 1, tile_position=(0, DH * j))
                    mm.then_inc(s_pv, 1)

                def rows(b, z, sums_done):
                    pe.wait_ge(s_rec, sums_done * SUB + SUB)
                    pe.wait_ge(s_row, (b * SLOTS + z) * 2 + 1)
                    pe.wait_ge(s_neg, b * SLOTS + z + 1)
                    for j in range(2):
                        for s in range(SUB):
                            mm = pe.matmul(misc[32 * j:32 * j + 1, s * P:(s + 1) * P],
                                           neg_max[:, j * SUB + s:j * SUB + s + 1], ident_sb[:],
                                           start=True, stop=True, tile_position=(0, 32 * j))
                    mm.then_inc(s_rows, 1)

                def sums(b, z):
                    pe.wait_ge(s_row, (b * SLOTS + 2 + rows_before(z)) * 2 + 1)
                    pe.wait_ge(s_rec, (b * SLOTS + z) * SUB + SUB)
                    pe.wait_ge(s_acc, (b + 1) * ALAP + afirst[z + 1])
                    for j in range(2):
                        mm = pe.matmul(misc[DH * j:DH * (j + 1), 0:T], ones[:], row_sum[:, j * T:(j + 1) * T],
                                       start=True, stop=True, tile_position=(0, DH * j))
                    mm.then_inc(s_l, 1)

                for z in range(2):
                    for u in range(len(units[z])):
                        max_unit(0, z, u)
                    rows(0, z, 0)
                with pe.Fori(0, B) as b:
                    for at, (z, g) in enumerate(at_step):
                        todo, _, made = plan[at]
                        n = 1 if len(todo) > 2 else 0
                        for lap, uz, u in todo[:n]:
                            max_unit(b + lap, uz, u)
                        score_step(b, z, g)
                        for lap, uz, u in todo[n:n + 1]:
                            max_unit(b + lap, uz, u)
                        if g > 0:
                            pv_step(b, z, g - 1)
                        for lap, uz, u in todo[n + 1:]:
                            max_unit(b + lap, uz, u)
                        for lap, rz in made:
                            rows(b + lap, rz, b * SLOTS + sums_before(at))
                        if z > 0 and g == sums_step(z):
                            sums(b, z - 1)
                        if g == steps[z] - 1:
                            pv_step(b, z, g)
                    sums(b, SLOTS - 1)

            @block.scalar
            def _(act):
                act.sem_inc(s_exp, BANKS)
                act.sem_inc(s_oev, 1)
                act.sem_inc(s_row, 1)

                def place_row(b, z):
                    c = z % NC
                    act.wait_ge(s_rows, b * SLOTS + z + 2)
                    act.activation(qb[1][DH:DH + 1, c * T:(c + 1) * T], misc[32:33, 0:T], ACT.Copy).then_inc(s_row, 1)

                def take_out(b, z):
                    act.wait_ge(s_norm, b * SLOTS + z + 1)
                    act.wait_ge(s_pv, b * LAP + first[z + 1] + PBUF)
                    act.activation(out_sb[:], out_ps[:, 0:T], ACT.Copy).then_inc(s_oev, 1)

                for z in range(2):
                    place_row(0, z)
                with act.Fori(0, B) as b:
                    for at, (z, g) in enumerate(at_step):
                        act.wait_ge(s_pv, b * LAP + at + 1)
                        bz, bg = at_step[at - PBUF]
                        act.wait_ge(s_acc, (b + (1 if at >= PBUF else 0)) * ALAP + afirst[bz] + max(bg, 1))
                        for j in range(2):
                            act.wait_ge(s_st, (b * LAP + at) * 2 + j + 1)
                            act.activation(probs[at % PBUF][:, j * T:(j + 1) * T],
                                           scores[(2 * at + j) % BANKS][:, 0:T], ACT.Exp, scale=SCALE
                                           ).then_inc(s_exp, 1)
                        if g == 0 and z > 0:
                            take_out(b, z - 1)
                        for lap, rz in plan[at][2]:
                            place_row(b + lap, rz)
                    take_out(b, SLOTS - 1)

            @block.vector
            def _(dve):
                dve.sem_inc(s_red, BANKS)
                dve.sem_inc(s_rec, SUB)
                dve.sem_inc(s_norm, 1)
                for par in range(2):
                    for j in range(2):
                        ins = dve.memset(kb[par][j][DH:DH + 1, :].bitcast(F32), 1.0)
                ins.then_inc(s_ones, 1)
                dve.memset(ones[:], 1.0).then_inc(s_ones, 1)
                dve.wait_ge(s_const, 16)
                dve.tensor_copy(ident_bf[:], ident_sb[:]).then_inc(s_mask, 1)

                def max_unit(b, z, u):
                    j, s, k = units[z][u]
                    at = ufirst[z] + u
                    dve.wait_ge(s_mx, b * ULAP + at + 1)
                    dve.tensor_reduce(maxes[z % 2][:, j * SUB + s:j * SUB + s + 1, k], max_ps[at % BANKS][:, 0:T],
                                      AX.X, ALU.max).then_inc(s_red, 1)

                def negate(b, z):
                    dve.wait_ge(s_rows, b * SLOTS + z + 1)
                    dve.wait_ge(s_red, b * ULAP + ufirst[z + 1] + BANKS)
                    dve.tensor_reduce(neg_max[:], maxes[z % 2][:, :, 0:z % NC + 1], AX.X, ALU.max,
                                      negate=True).then_inc(s_neg, 1)

                def place_row(b, z):
                    c = z % NC
                    dve.wait_ge(s_rows, b * SLOTS + z + 2)
                    dve.tensor_copy(qb[0][DH:DH + 1, c * T:(c + 1) * T], misc[0:1, 0:T]).then_inc(s_row, 1)

                def invert(b, z, s):
                    if s == 0:
                        dve.wait_ge(s_l, b * SLOTS + z + 1)
                        dve.wait_ge(s_norm, b * SLOTS + z + 1)
                    dve.reciprocal(recip[:, s * P:(s + 1) * P], misc[:, s * P:(s + 1) * P]).then_inc(s_rec, 1)

                def normalise(b, z):
                    dve.wait_ge(s_oev, b * SLOTS + z + 2)
                    dve.wait_ge(s_store[z % 2], (b * (SLOTS // 2) + z // 2) * 16 + 1)
                    dve.wait_ge(s_rec, (b * SLOTS + z + 1) * SUB + SUB)
                    dve.tensor_tensor(normed[z % 2][:], out_sb[:], recip[:], ALU.mult).then_inc(s_norm, 1)

                for z in range(2):
                    for u in range(len(units[z])):
                        max_unit(0, z, u)
                    negate(0, z)
                    place_row(0, z)
                with dve.Fori(0, B) as b:
                    for at, (z, g) in enumerate(at_step):
                        todo, complete, made = plan[at]
                        for lap, uz, u in todo:
                            max_unit(b + lap, uz, u)
                        for lap, cz in complete:
                            negate(b + lap, cz)
                        if z > 0:
                            for s in thirds_at(z, g):
                                invert(b, z - 1, s)
                            if SUB - 1 in thirds_at(z, g):
                                normalise(b, z - 1)
                        for lap, rz in made:
                            place_row(b + lap, rz)
                    for s in range(SUB):
                        invert(b, SLOTS - 1, s)
                    normalise(b, SLOTS - 1)

            @block.gpsimd
            def _(pool):
                pool.sem_inc(s_acc, ALAP)
                pool.memset(mask_q[:], 0.0).then_inc(s_zero, 1)
                pool.memset(mask_k[:], 0.0).then_inc(s_zero, 1)
                pool.wait_ge(s_zero, 2)
                for s in range(SUB):
                    ins = pool.affine_select(out=mask_q[:, s, :], in_=mask_q[:, s, :], compare_op=ALU.is_ge,
                                             fill=MASKED, base=s * P, pattern=[[-1, T]], channel_multiplier=1)
                ins.then_inc(s_mask, 1)
                for s in range(SUB):
                    ins = pool.affine_select(out=mask_k[:, s, :], in_=mask_k[:, s, :], compare_op=ALU.is_ge,
                                             fill=MASKED, base=-s * P, pattern=[[1, T]], channel_multiplier=-1)
                ins.then_inc(s_mask, 1)
                with pool.Fori(0, B) as b:
                    for at, (z, g) in enumerate(at_step):
                        if g == 0:
                            continue
                        pool.wait_ge(s_exp, (b * LAP + at) * 2 + 2 + BANKS)
                        pool.wait_ge(s_acc, (b + 1) * ALAP + afirst[z] + g - 1)
                        acc = probs[(at - 1) % PBUF] if g == 1 else run_sum
                        to = row_sum if g == steps[z] - 1 else run_sum
                        pool.tensor_tensor(to[:], acc[:], probs[at % PBUF][:], ALU.add).then_inc(s_acc, 1)


def recurrence_gate_and_ffn(nc, a, o_t, a_t, t_t, t2_t):
    HN, DH = 4, C // 4
    FF = 4 * C // P
    LNS = 3
    FIRST, WEIGHTS = 6, 18
    ORDER = (
        ("att", 0, 0), ("hidden0", 1, 1), ("mean0", 0, 0), ("hidden1", 1, 1), ("var0", 0, 0), ("ffn0", 1, 1),
        ("affine0", 0, 0), ("features", 0, 0), ("ffn1", 1, 1), ("values", 0, 0), ("elu", 0, 0), ("mean2", 1, 1),
        ("turn", 0, 0), ("var2", 1, 1), ("own0", 0, 0), ("affine2", 1, 1), ("merge", 1, 1), ("att", 1, 0),
        ("own1", 0, 0), ("mean0", 1, 0), ("head0", 0, 0), ("own2", 0, 0), ("var0", 1, 0), ("head1", 0, 0),
        ("divide0", 0, 0), ("own3", 0, 0), ("head2", 0, 0), ("affine0", 1, 0), ("features", 1, 0),
        ("head3", 0, 0), ("divide1", 0, 0), ("values", 1, 0), ("elu", 1, 0), ("ro", 0, 0), ("turn", 1, 0),
        ("mean1", 0, 0), ("own0", 1, 0), ("var1", 0, 0), ("own1", 1, 0), ("head0", 1, 0), ("affine1", 0, 0),
        ("own2", 1, 0), ("gate", 0, 0), ("head1", 1, 0), ("gated", 0, 0), ("divide0", 1, 0), ("own3", 1, 0),
        ("head2", 1, 0), ("head3", 1, 0), ("divide1", 1, 0), ("hidden0", 0, 0), ("ro", 1, 0), ("hidden1", 0, 0),
        ("mean1", 1, 0), ("ffn0", 0, 0), ("var1", 1, 0), ("ffn1", 0, 0), ("affine1", 1, 0), ("gate", 1, 0),
        ("mean2", 0, 0), ("gated", 1, 0), ("var2", 0, 0), ("affine2", 0, 0), ("merge", 0, 0))
    with ExitStack() as ctx:
        sb, ps, sem = tools(nc, ctx, "rec")
        L = range(B)
        w = {n: sb(n, [P, KC, C]) for n in ("o_w", "rq_w", "rk_w", "rv_w", "ro_w")}
        w["cg_w"] = sb("cg_w", [P, 2 * KC, C])
        w["ffn_w1"] = sb("ffn_w1", [P, KC, 4 * C])
        w["ffn_w2"] = sb("ffn_w2", [P, FF, C])
        cols = {n: sb(n, [P, KC]) for n in ("o_b", "rq_b", "rk_b", "ro_b", "cg_b", "ffn_b2", "ln1_g", "ln1_b",
                                            "ln2_g", "ln2_b", "ln3_g", "ln3_b")}
        cols["ffn_b1"] = sb("ffn_b1", [P, FF])
        rv_bias = sb("rv_bias", [P, C])
        mean_mat = sb("mean_mat", [P, P])
        ident = sb("ident", [P, P])
        half_cg_b = sb("half_cg_b", [P, KC])
        eps = sb("eps", [P, 1])
        tri = sb("tri", [P, 2 * T])
        gain = [cols["ln1_g"], cols["ln2_g"], cols["ln3_g"]]
        bias = [cols["ln1_b"], cols["ln2_b"], cols["ln3_b"]]

        def per_lane(name, shape, dt=F32):
            return [sb(f"{name}{i}", shape, dt) for i in L]
        t, x, o = (per_lane(n, [P, KC, T]) for n in ("t", "x", "o"))
        res, par, dev, sq, nm, dn, seq, mrg, t2 = (per_lane(n, [P, KC, T]) for n in (
            "res", "par", "dev", "sq", "nm", "dn", "seq", "mrg", "t2"))
        std, rstd = per_lane("std", [P, T]), per_lane("rstd", [P, T])
        hid = per_lane("hid", [P, FF, T])
        fm = per_lane("fm", [P, 2 * KC, T])
        vx = per_lane("vx", [P, SUB, HN, P])
        kt = per_lane("kt", [P, SUB, C])
        at = [[sb(f"at{i}{k}", [P, 2 * T]) for k in range(2)] for i in L]
        state = per_lane("state", [P, KC, P])
        bank = [[ps(f"bank{i}{k}", [P, 512]) for k in range(4)] for i in L]
        s_first, s_w, s_set = sem("first_weights"), sem("weights"), sem("set_up")
        s_ld = [sem(f"loaded{i}") for i in L]
        s_ldt = [sem(f"t_loaded{i}") for i in L]
        s_st = [sem(f"stored{i}") for i in L]
        (s_att, s_res, s_mean, s_dev, s_sq, s_var, s_std, s_rstd, s_scaled, s_ln, s_z, s_zmin, s_zout, s_zexp,
         s_fm, s_v, s_vx, s_kt, s_ktout) = ([sem(f"{n}{i}") for i in L] for n in (
             "att_mm", "res_ready", "mean_mm", "dev_ready", "dev_squared", "var_mm", "std_ready", "rstd_ready",
             "scaled", "ln_ready", "features_mm", "z_min", "z_taken", "z_exp", "features_ready", "v_mm",
             "values_ready", "keys_turned", "keys_ready"))
        (s_a, s_at, s_oe, s_upd, s_num, s_den, s_state, s_rden, s_rec, s_ro, s_gate, s_th, s_diff, s_gated, s_mrg,
         s_h, s_gelu, s_f, s_t2) = ([sem(f"{n}{i}") for i in L] for n in (
             "a_mm", "a_masked", "out_mm", "update_mm", "num_taken", "den_taken", "state_ready", "den_inverted",
             "rec_ready", "ro_mm", "gate_mm", "gate_tanh", "par_less_seq", "gated", "merged_ready", "hidden_mm",
             "hidden_ready", "ffn_mm", "t2_ready"))
        s_tri, s_cgb = sem("tri_set"), sem("cgb_halved")

        def ln(c, r):
            return c * LNS + r + 1

        def head(c, h):
            return c * HN + h + 1

        def project(pe, to, weight, src, tiles, m):
            for k in range(tiles):
                mm = pe.matmul(to[:, 0:T], weight[:, k, m * P:(m + 1) * P], src(k), start=k == 0, stop=k == tiles - 1)
            return mm

        with nc.Block() as block:
            @block.sync
            def _(sp):
                for i in L:
                    sp.sem_inc(s_st[i], 1)
                for i in L:
                    for dst, src, count in ((o, o_t, s_ld), (x, a_t, s_ld), (t, t_t, s_ldt)):
                        sp.dma_start(dst[i][:], src[i].rearrange("(k p) n -> p k n", p=P)[:, :, 0:T]
                                     ).then_inc(count[i], 16)
                early = "o_w", "o_b", "ln1_g", "ln1_b", "cg_b"
                loads = {**w, **cols}
                for n in early:
                    sp.dma_start(loads[n][:], a[n]).then_inc(s_first, 16)
                sp.dma_start(mean_mat[:], a["mean_mat"]).then_inc(s_first, 16)
                late = [(loads[n], a[n]) for n in loads if n not in early] + [(ident, a["ident"])]
                assert len(early) + 1 == FIRST and len(late) + 1 == WEIGHTS
                for dst, src in late:
                    sp.dma_start(dst[:], src).then_inc(s_w, 16)
                sp.dma_start(rv_bias[:], a["rv_b"].partition_broadcast(P)).then_inc(s_w, 16)

                def load(c, i):
                    for dst, src in ((o, o_t), (x, a_t)):
                        sp.dma_start(dst[i][:], src[i].rearrange("(k p) n -> p k n", p=P)[:, :, bass.ds(c * T, T)]
                                     ).then_inc(s_ld[i], 16)

                def load_t(c, i):
                    sp.dma_start(t[i][:], t_t[i].rearrange("(k p) n -> p k n", p=P)[:, :, bass.ds(c * T, T)]
                                 ).then_inc(s_ldt[i], 16)

                def store(c, i):
                    sp.wait_ge(s_t2[i], c + 1)
                    sp.dma_start(t2_t[i].rearrange("(k p) n -> p k n", p=P)[:, :, bass.ds(c * T, T)], t2[i][:]
                                 ).then_inc(s_st[i], 16)

                with sp.Fori(0, NC - 1) as c:
                    for i in L:
                        sp.wait_ge(s_res[i], ln(c, 0))
                        load(c + 1, i)
                    for i in L:
                        store(c, i)
                        load_t(c + 1, i)
                for i in L:
                    store(NC - 1, i)
                for i in L:
                    sp.wait_ge(s_st[i], NC * 16 + 1)

            @block.tensor
            def _(pe):
                pe.wait_ge(s_first, 16 * FIRST)
                pe.wait_ge(s_set, 6)

                def average(c, i, ready, count, src, to, done):
                    pe.wait_ge(ready[i], count)
                    for k in range(KC):
                        mm = pe.matmul(bank[i][to][:, 0:T], mean_mat[:], src[i][:, k, :],
                                       start=k == 0, stop=k == KC - 1)
                    mm.then_inc(done[i], 1)

                def own(c, h, i):
                    half, base = h // 2, DH * (h % 2)
                    rows = slice(base, base + DH)
                    if h == 0:
                        pe.wait_ge(s_ktout[i], c + 1)
                    else:
                        pe.wait_ge(s_at[i], head(c, h - 1))
                    for s, (b, col) in enumerate(((0, 0), (1, 0), (0, T))):
                        mm = pe.matmul(bank[i][b][:, col:col + T - s * P],
                                       fm[i][rows, KC + half, s * P:(s + 1) * P],
                                       fm[i][rows, half, s * P:T], start=True, stop=True)
                    mm.then_inc(s_a[i], 1)

                def heads_out(c, h, i):
                    half, base = h // 2, DH * (h % 2)
                    rows = slice(base, base + DH)
                    pe.wait_ge(s_at[i], head(c, h))
                    pe.wait_ge(s_num[i], head(c, h))
                    pe.wait_ge(s_den[i], head(c, h))
                    if h == 0:
                        pe.wait_ge(s_state[i], c + 1)
                    pe.matmul(bank[i][2][:, 0:T], state[i][rows, half, :], fm[i][rows, half, :],
                              start=True, stop=False)
                    for s, col in enumerate((0, T + P, T)):
                        mm = pe.matmul(bank[i][2][:, s * P:T], vx[i][:, s, h, :],
                                       at[i][h % 2][:, col:col + T - s * P], start=False, stop=s == SUB - 1)
                    mm.then_inc(s_oe[i], 1)
                    for s in range(SUB):
                        mm = pe.matmul(bank[i][3][rows, half * P:(half + 1) * P],
                                       kt[i][:, s, h * DH:(h + 1) * DH], vx[i][:, s, h, :],
                                       start=s == 0, stop=s == SUB - 1, tile_position=(0, base))
                    if h == HN - 1:
                        mm.then_inc(s_upd[i], 1)

                def stage(name, c, i):
                    if name == "att":
                        pe.wait_ge(s_ld[i], (c + 1) * 32)
                        for m in range(KC):
                            mm = project(pe, bank[i][m], w["o_w"], lambda k: o[i][:, k, :], KC, m)
                        mm.then_inc(s_att[i], 1)
                    elif name[:4] == "mean":
                        average(c, i, s_res, ln(c, int(name[4])), res, 2, s_mean)
                    elif name[:3] == "var":
                        average(c, i, s_sq, ln(c, int(name[3])), sq, 3, s_var)
                    elif name == "features":
                        pe.wait_ge(s_w, 16 * WEIGHTS)
                        pe.wait_ge(s_ln[i], ln(c, 0))
                        for m in range(2 * KC):
                            mm = project(pe, bank[i][m], w["rq_w" if m < KC else "rk_w"],
                                         lambda k: par[i][:, k, :], KC, m % KC)
                        mm.then_inc(s_z[i], 1)
                    elif name == "values":
                        pe.wait_ge(s_zout[i], c + 1)
                        for s in range(SUB):
                            for k in range(KC):
                                mm = pe.matmul(bank[i][s][:, 0:C], par[i][:, k, s * P:(s + 1) * P],
                                               w["rv_w"][:, k, :], start=k == 0, stop=k == KC - 1)
                        mm.then_inc(s_v[i], 1)
                    elif name == "turn":
                        pe.wait_ge(s_fm[i], c + 1)
                        pe.wait_ge(s_vx[i], c + 1)
                        for k in range(KC):
                            for s in range(SUB):
                                mm = pe.transpose(bank[i][3 if k == 0 else 0][:, s * P:(s + 1) * P],
                                                  fm[i][:, KC + k, s * P:(s + 1) * P], ident[:])
                        mm.then_inc(s_kt[i], 1)
                    elif name[:3] == "own":
                        own(c, int(name[3]), i)
                    elif name[:4] == "head":
                        heads_out(c, int(name[4]), i)
                    elif name == "ro":
                        pe.wait_ge(s_rec[i], (c + 1) * 2)
                        for m in range(KC):
                            mm = project(pe, bank[i][m], w["ro_w"], lambda k: nm[i][:, k, :], KC, m)
                        mm.then_inc(s_ro[i], 1)
                    elif name == "gate":
                        pe.wait_ge(s_ln[i], ln(c, 1))
                        for m in range(KC):
                            mm = project(pe, bank[i][m], w["cg_w"],
                                         lambda k: (par if k < KC else seq)[i][:, k % KC, :], 2 * KC, m)
                        mm.then_inc(s_gate[i], 1)
                    elif name[:6] == "hidden":
                        for m in range(4):
                            if name[6] == "0" and m == 0:
                                pe.wait_ge(s_mrg[i], c + 1)
                            if name[6] == "1":
                                pe.wait_ge(s_gelu[i], c * FF + m + 1)
                            project(pe, bank[i][m], w["ffn_w1"], lambda k: mrg[i][:, k, :], KC,
                                    m + 4 * int(name[6])).then_inc(s_h[i], 1)
                    elif name[:3] == "ffn":
                        m = int(name[3])
                        if m == 0:
                            pe.wait_ge(s_gelu[i], (c + 1) * FF)
                        mm = project(pe, bank[i][m], w["ffn_w2"], lambda k: hid[i][:, k, :], FF, m)
                        if m == KC - 1:
                            mm.then_inc(s_f[i], 1)

                run_stages(pe, ORDER, stage)

            @block.scalar
            def _(act):
                act.wait_ge(s_first, 16 * FIRST)
                act.wait_ge(s_set, 6)
                for i in L:
                    act.sem_inc(s_num[i], 1)
                act.activation(half_cg_b[:], cols["cg_b"][:], ACT.Copy, scale=0.5).then_inc(s_cgb, 1)
                act.wait_ge(s_cgb, 1)

                def stage(name, c, i):
                    if name[:4] == "mean":
                        act.wait_ge(s_dev[i], ln(c, int(name[4])))
                        act.activation(sq[i][:], dev[i][:], ACT.Square).then_inc(s_sq[i], 1)
                    elif name[:3] == "var":
                        act.wait_ge(s_var[i], ln(c, int(name[3])))
                        act.activation(std[i][:], bank[i][3][:, 0:T], ACT.Sqrt, bias=eps[:, 0:1]
                                       ).then_inc(s_std[i], 1)
                    elif name[:6] == "affine":
                        which = int(name[6])
                        act.wait_ge(s_scaled[i], ln(c, which))
                        for k in range(KC):
                            ins = act.activation((seq if which else par)[i][:, k, :], dev[i][:, k, :], ACT.Identity,
                                                 bias=bias[which][:, k:k + 1])
                        ins.then_inc(s_ln[i], 1)
                    elif name == "features":
                        act.wait_ge(s_w, 16 * WEIGHTS)
                        act.wait_ge(s_z[i], c + 1)
                        for m in range(2 * KC):
                            ins = act.activation(hid[i][:, m, :], bank[i][m][:, 0:T], ACT.Identity,
                                                 bias=cols["rq_b" if m < KC else "rk_b"][:, m % KC:m % KC + 1])
                        ins.then_inc(s_zout[i], 1)
                    elif name == "elu":
                        act.wait_ge(s_zmin[i], c + 1)
                        act.activation(fm[i][:], hid[i][:, 4:8, :], ACT.Exp).then_inc(s_zexp[i], 1)
                    elif name == "turn":
                        act.wait_ge(s_kt[i], c + 1)
                        for k in range(KC):
                            ins = act.activation(kt[i][:, :, k * P:(k + 1) * P],
                                                 bank[i][3 if k == 0 else 0][:, 0:T].rearrange(
                                                     "p (s c) -> p s c", s=SUB), ACT.Copy)
                        ins.then_inc(s_ktout[i], 1)
                    elif name[:4] == "head":
                        h = int(name[4])
                        half, base = h // 2, DH * (h % 2)
                        act.wait_ge(s_oe[i], head(c, h))
                        act.activation(nm[i][base:base + DH, half, :], bank[i][2][0:DH, 0:T], ACT.Copy
                                       ).then_inc(s_num[i], 1)
                    elif name == "gate":
                        act.wait_ge(s_gate[i], c + 1)
                        for m in range(KC):
                            ins = act.activation(nm[i][:, m, :], bank[i][m][:, 0:T], ACT.Tanh, scale=0.5,
                                                 bias=half_cg_b[:, m:m + 1])
                        ins.then_inc(s_th[i], 1)
                    elif name[:6] == "hidden":
                        for m in range(4):
                            at_m = m + 4 * int(name[6])
                            act.wait_ge(s_h[i], c * FF + at_m + 1)
                            act.activation(hid[i][:, at_m, :], bank[i][m][:, 0:T], ACT.Gelu,
                                           bias=cols["ffn_b1"][:, at_m:at_m + 1]).then_inc(s_gelu[i], 1)

                run_stages(act, ORDER, stage)

            @block.vector
            def _(dve):
                for i in L:
                    dve.sem_inc(s_den[i], 1)
                dve.memset(eps[:], LN_EPS).then_inc(s_set, 1)
                for i in L:
                    dve.memset(vx[i][:], 1.0).then_inc(s_set, 1)
                    dve.memset(state[i][:], 0.0).then_inc(s_state[i], 1)
                dve.wait_ge(s_first, 16 * FIRST)
                dve.wait_ge(s_set, 6)

                def residual(c, i, counter, bias_cols, other):
                    dve.wait_ge(counter[i], c + 1)
                    for m in range(KC):
                        ins = dve.scalar_tensor_tensor(out=res[i][:, m, :], in0=bank[i][m][:, 0:T],
                                                       scalar=bias_cols[:, m:m + 1], in1=other[i][:, m, :],
                                                       op0=ALU.add, op1=ALU.add)
                    ins.then_inc(s_res[i], 1)

                def stage(name, c, i):
                    if name == "att":
                        residual(c, i, s_att, cols["o_b"], x)
                    elif name[:4] == "mean":
                        dve.wait_ge(s_mean[i], ln(c, int(name[4])))
                        for k in range(KC):
                            ins = dve.tensor_tensor(dev[i][:, k, :], res[i][:, k, :], bank[i][2][:, 0:T], ALU.subtract)
                        ins.then_inc(s_dev[i], 1)
                    elif name[:3] == "var":
                        which = int(name[3])
                        dve.wait_ge(s_std[i], ln(c, which))
                        dve.reciprocal(rstd[i][:], std[i][:]).then_inc(s_rstd[i], 1)
                        dve.wait_ge(s_rstd[i], ln(c, which))
                        for k in range(KC):
                            ins = dve.scalar_tensor_tensor(out=dev[i][:, k, :], in0=dev[i][:, k, :],
                                                           scalar=gain[which][:, k:k + 1], in1=rstd[i][:],
                                                           op0=ALU.mult, op1=ALU.mult)
                        ins.then_inc(s_scaled[i], 1)
                    elif name == "features":
                        dve.wait_ge(s_w, 16 * WEIGHTS)
                        dve.wait_ge(s_zout[i], c + 1)
                        dve.tensor_scalar(hid[i][:, 4:8, :], hid[i][:, 0:4, :], 0.0, None, ALU.min
                                          ).then_inc(s_zmin[i], 1)
                    elif name == "elu":
                        dve.wait_ge(s_zexp[i], c + 1)
                        dve.scalar_tensor_tensor(out=fm[i][:], in0=hid[i][:, 0:4, :], scalar=0.0, in1=fm[i][:],
                                                 op0=ALU.max, op1=ALU.add).then_inc(s_fm[i], 1)
                    elif name == "values":
                        dve.wait_ge(s_v[i], c + 1)
                        for s in range(SUB):
                            ins = dve.tensor_tensor(vx[i][:, s, :, 0:DH],
                                                    bank[i][s][:, 0:C].rearrange("p (h d) -> p h d", h=HN),
                                                    rv_bias[:].rearrange("p (h d) -> p h d", h=HN), ALU.add)
                        ins.then_inc(s_vx[i], 1)
                    elif name[:3] == "own":
                        h = int(name[3])
                        dve.wait_ge(s_a[i], head(c, h))
                        if h >= 2:
                            dve.wait_ge(s_oe[i], head(c, h - 2))
                        dve.tensor_tensor(at[i][h % 2][:, 0:512], bank[i][0][:, 0:512], tri[:, 0:512], ALU.mult)
                        dve.tensor_tensor(at[i][h % 2][:, 512:768], bank[i][1][:, 0:256], tri[:, 512:768],
                                          ALU.mult).then_inc(s_at[i], 1)
                    elif name[:4] == "head":
                        h = int(name[4])
                        half, base = h // 2, DH * (h % 2)
                        dve.wait_ge(s_oe[i], head(c, h))
                        dve.tensor_scalar(dn[i][base:base + DH, half, :], bank[i][2][DH:P, 0:T], EPS_REC, None,
                                          ALU.add).then_inc(s_den[i], 1)
                    elif name[:6] == "divide":
                        half = int(name[6])
                        dve.wait_ge(s_den[i], head(c, 2 * half + 2))
                        dve.reciprocal(dn[i][:, half, :], dn[i][:, half, :]).then_inc(s_rden[i], 1)
                        dve.wait_ge(s_rden[i], c * 2 + half + 1)
                        dve.wait_ge(s_num[i], head(c, 2 * half + 2))
                        dve.tensor_tensor(nm[i][:, half, :], nm[i][:, half, :], dn[i][:, half, :], ALU.mult
                                          ).then_inc(s_rec[i], 1)
                        if half == 1:
                            dve.wait_ge(s_upd[i], c + 1)
                            dve.tensor_tensor(state[i][:].rearrange("p k m -> p (k m)"),
                                              state[i][:].rearrange("p k m -> p (k m)"), bank[i][3][:, 0:2 * P],
                                              ALU.add).then_inc(s_state[i], 1)
                    elif name == "ro":
                        residual(c, i, s_ro, cols["ro_b"], par)
                    elif name == "gate":
                        dve.wait_ge(s_ln[i], ln(c, 1))
                        dve.tensor_tensor(dn[i][:], par[i][:], seq[i][:], ALU.subtract).then_inc(s_diff[i], 1)
                    elif name == "gated":
                        dve.wait_ge(s_th[i], c + 1)
                        dve.wait_ge(s_diff[i], c + 1)
                        dve.scalar_tensor_tensor(out=mrg[i][:], in0=nm[i][:], scalar=1.0, in1=dn[i][:],
                                                 op0=ALU.add, op1=ALU.mult).then_inc(s_gated[i], 1)
                        dve.wait_ge(s_gated[i], c + 1)
                        dve.scalar_tensor_tensor(out=mrg[i][:], in0=mrg[i][:], scalar=0.5, in1=seq[i][:],
                                                 op0=ALU.mult, op1=ALU.add).then_inc(s_mrg[i], 1)
                    elif name == "ffn1":
                        residual(c, i, s_f, cols["ffn_b2"], mrg)
                    elif name == "merge":
                        dve.wait_ge(s_ln[i], ln(c, 2))
                        dve.wait_ge(s_ldt[i], (c + 1) * 16)
                        dve.wait_ge(s_st[i], c * 16 + 1)
                        dve.tensor_tensor(t2[i][:], t[i][:], seq[i][:], ALU.add).then_inc(s_t2[i], 1)

                run_stages(dve, ORDER, stage)

            @block.gpsimd
            def _(pool):
                pool.memset(tri[:], 1.0).then_inc(s_tri, 1)
                pool.wait_ge(s_tri, 1)
                for col in (0, T, T + P):
                    pool.affine_select(out=tri[:, col:col + P], in_=tri[:, col:col + P], compare_op=ALU.is_ge,
                                       fill=0.0, base=0, pattern=[[1, P]], channel_multiplier=-1).then_inc(s_set, 1)


def routed_ffn(nc, a, t_t, logits, base_t, delta_t):
    FF = 4 * C // P
    FIRST, WEIGHTS = 3, 4
    ORDER = (
        ("hidden0", 1, 1), ("mean", 0, 0), ("hidden1", 1, 1), ("var", 0, 0), ("ffn0", 1, 1), ("ffn1", 1, 1),
        ("logit", 0, 0), ("hidden0", 0, 0), ("mean", 1, 0), ("hidden1", 0, 0), ("var", 1, 0), ("ffn0", 0, 0),
        ("ffn1", 0, 0), ("logit", 1, 0))
    with ExitStack() as ctx:
        sb, ps, sem = tools(nc, ctx, "ffn")
        L = range(B)
        w1 = sb("w1", [P, KC, 4 * C])
        w2 = sb("w2", [P, FF, C])
        wr = sb("wr", [P, KC])
        br = sb("br", [1, 1])
        b1 = sb("b1", [P, FF])
        b2 = sb("b2", [P, KC])
        mean_mat = sb("mean_mat", [P, P])
        eps = sb("eps", [P, 1])
        t, dev, sq, x, base, delta = ([sb(f"{n}{i}", [P, KC, T]) for i in L] for n in (
            "t", "dev", "sq", "x", "base", "delta"))
        std, rstd = ([sb(f"{n}{i}", [P, T]) for i in L] for n in ("std", "rstd"))
        hid = [sb(f"hid{i}", [P, FF, T]) for i in L]
        row = [sb(f"row{i}", [1, T]) for i in L]
        bank = [[ps(f"bank{i}{k}", [P, 512]) for k in range(4)] for i in L]
        s_first, s_w, s_set = sem("first_weights"), sem("weights"), sem("set_up")
        s_ld = [sem(f"loaded{i}") for i in L]
        s_st = [sem(f"base_stored{i}") for i in L]
        s_stored_d = [sem(f"delta_stored{i}") for i in L]
        (s_mean, s_dev, s_sq, s_var, s_std, s_rstd, s_x, s_logit, s_row, s_base, s_h, s_gelu, s_f, s_delta) = (
            [sem(f"{n}{i}") for i in L] for n in ("mean_mm", "dev_ready", "dev_squared", "var_mm", "std_ready", "rstd_ready", "x_ready",
                             "logit_mm", "row_ready", "base_ready", "hidden_mm", "hidden_ready", "ffn_mm",
                             "delta_ready"))

        with nc.Block() as block:
            @block.sync
            def _(sp):
                for i in L:
                    sp.sem_inc(s_st[i], 1)
                    sp.sem_inc(s_stored_d[i], 1)

                def load(c, i):
                    sp.dma_start(t[i][:], t_t[i].rearrange("(k p) n -> p k n", p=P)[:, :, bass.ds(c * T, T)]
                                 ).then_inc(s_ld[i], 16)

                for i in L:
                    load(0, i)
                for dst, src in ((mean_mat, a["mean_mat"]), (wr, a["wr"]), (br, a["br"])):
                    sp.dma_start(dst[:], src).then_inc(s_first, 16)
                for dst, src in ((w1, a["w1"]), (b1, a["b1"]), (w2, a["w2"]), (b2, a["b2"])):
                    sp.dma_start(dst[:], src).then_inc(s_w, 16)

                def store_base(c, i):
                    sp.wait_ge(s_row[i], c + 1)
                    sp.dma_start(logits[i:i + 1, bass.ds(c * T, T)], row[i][:]).then_inc(s_st[i], 16)
                    sp.wait_ge(s_base[i], c + 1)
                    sp.dma_start(base_t[i].rearrange("(k p) n -> p k n", p=P)[:, :, bass.ds(c * T, T)], base[i][:]
                                 ).then_inc(s_st[i], 16)

                def store_delta(c, i):
                    sp.wait_ge(s_delta[i], c + 2)
                    sp.dma_start(delta_t[i].rearrange("(k p) n -> p k n", p=P)[:, :, bass.ds(c * T, T)], delta[i][:]
                                 ).then_inc(s_stored_d[i], 16)

                with sp.Fori(0, NC - 1) as c:
                    for i in L:
                        store_base(c, i)
                        load(c + 1, i)
                    for i in L:
                        store_delta(c, i)
                for i in L:
                    store_base(NC - 1, i)
                for i in L:
                    store_delta(NC - 1, i)
                for i in L:
                    sp.wait_ge(s_st[i], NC * 32 + 1)
                    sp.wait_ge(s_stored_d[i], NC * 16 + 1)

            @block.tensor
            def _(pe):
                pe.wait_ge(s_first, 16 * FIRST)

                def stage(name, c, i):
                    if name == "mean":
                        pe.wait_ge(s_ld[i], (c + 1) * 16)
                        for k in range(KC):
                            mm = pe.matmul(bank[i][2][:, 0:T], mean_mat[:], t[i][:, k, :],
                                           start=k == 0, stop=k == KC - 1)
                        mm.then_inc(s_mean[i], 1)
                    elif name == "var":
                        pe.wait_ge(s_sq[i], c + 1)
                        for k in range(KC):
                            mm = pe.matmul(bank[i][3][:, 0:T], mean_mat[:], sq[i][:, k, :],
                                           start=k == 0, stop=k == KC - 1)
                        mm.then_inc(s_var[i], 1)
                    elif name == "logit":
                        pe.wait_ge(s_x[i], c + 1)
                        for k in range(KC):
                            mm = pe.matmul(bank[i][2][0:1, 0:T], wr[:, k:k + 1], x[i][:, k, :],
                                           start=k == 0, stop=k == KC - 1)
                        mm.then_inc(s_logit[i], 1)
                    elif name[:6] == "hidden":
                        for m in range(4):
                            if name[6] == "0" and m == 0:
                                pe.wait_ge(s_w, 16 * WEIGHTS)
                                pe.wait_ge(s_delta[i], c + 1)
                            if name[6] == "0" and m == 2:
                                pe.wait_ge(s_row[i], c + 1)
                            if name[6] == "1":
                                pe.wait_ge(s_gelu[i], c * FF + m + 1)
                            at_m = m + 4 * int(name[6])
                            for k in range(KC):
                                mm = pe.matmul(bank[i][m][:, 0:T], w1[:, k, at_m * P:(at_m + 1) * P], x[i][:, k, :],
                                               start=k == 0, stop=k == KC - 1)
                            mm.then_inc(s_h[i], 1)
                    elif name[:3] == "ffn":
                        m = int(name[3])
                        if m == 0:
                            pe.wait_ge(s_gelu[i], (c + 1) * FF)
                        for k in range(FF):
                            mm = pe.matmul(bank[i][m][:, 0:T], w2[:, k, m * P:(m + 1) * P], hid[i][:, k, :],
                                           start=k == 0, stop=k == FF - 1)
                        mm.then_inc(s_f[i], 1)

                run_stages(pe, ORDER, stage)

            @block.scalar
            def _(act):
                act.wait_ge(s_first, 16 * FIRST)
                act.wait_ge(s_set, 1)
                for i in L:
                    act.sem_inc(s_delta[i], 1)

                def stage(name, c, i):
                    if name == "mean":
                        act.wait_ge(s_dev[i], c + 1)
                        act.activation(sq[i][:], dev[i][:], ACT.Square).then_inc(s_sq[i], 1)
                    elif name == "var":
                        act.wait_ge(s_var[i], c + 1)
                        act.activation(std[i][:], bank[i][3][:, 0:T], ACT.Sqrt, bias=eps[:, 0:1]
                                       ).then_inc(s_std[i], 1)
                    elif name == "logit":
                        act.wait_ge(s_logit[i], c + 1)
                        act.wait_ge(s_st[i], c * 32 + 1)
                        act.activation(row[i][:], bank[i][2][0:1, 0:T], ACT.Identity, bias=br[:, 0:1]
                                       ).then_inc(s_row[i], 1)
                    elif name[:6] == "hidden":
                        if name[6] == "0":
                            act.wait_ge(s_w, 16 * WEIGHTS)
                        for m in range(4):
                            at_m = m + 4 * int(name[6])
                            act.wait_ge(s_h[i], c * FF + at_m + 1)
                            act.activation(hid[i][:, at_m, :], bank[i][m][:, 0:T], ACT.Gelu_apprx_tanh,
                                           bias=b1[:, at_m:at_m + 1]).then_inc(s_gelu[i], 1)
                    elif name == "ffn1":
                        act.wait_ge(s_f[i], (c + 1) * KC)
                        act.wait_ge(s_stored_d[i], c * 16 + 1)
                        for m in range(KC):
                            ins = act.activation(delta[i][:, m, :], bank[i][m][:, 0:T], ACT.Identity,
                                                 bias=b2[:, m:m + 1])
                        ins.then_inc(s_delta[i], 1)

                run_stages(act, ORDER, stage)

            @block.vector
            def _(dve):
                dve.memset(eps[:], LN_EPS).then_inc(s_set, 1)
                dve.wait_ge(s_set, 1)

                def stage(name, c, i):
                    if name == "mean":
                        dve.wait_ge(s_mean[i], c + 1)
                        for k in range(KC):
                            ins = dve.tensor_tensor(dev[i][:, k, :], t[i][:, k, :], bank[i][2][:, 0:T], ALU.subtract)
                        ins.then_inc(s_dev[i], 1)
                    elif name == "var":
                        dve.wait_ge(s_std[i], c + 1)
                        dve.reciprocal(rstd[i][:], std[i][:]).then_inc(s_rstd[i], 1)
                        dve.wait_ge(s_rstd[i], c + 1)
                        for k in range(KC):
                            ins = dve.tensor_tensor(x[i][:, k, :], dev[i][:, k, :], rstd[i][:], ALU.mult)
                        ins.then_inc(s_x[i], 1)
                        dve.wait_ge(s_x[i], c + 1)
                        dve.wait_ge(s_st[i], c * 32 + 1)
                        dve.tensor_tensor(base[i][:], t[i][:], x[i][:], ALU.add).then_inc(s_base[i], 1)

                run_stages(dve, ORDER, stage)


def select_and_merge(nc, logits, factors, ident, base_t, delta_t, out):
    KEPT = N // 2 - 1
    with ExitStack() as ctx:
        sb, ps, sem = tools(nc, ctx, "pick")
        L = range(B)
        row = [sb(f"row{i}", [P, N]) for i in L]
        by_tile = [sb(f"by_tile{i}", [NT, P]) for i in L]
        factor_row = [sb(f"factor_row{i}", [NT, P]) for i in L]
        ident_sb = sb("ident", [P, P])
        turn = [ps(f"turn{i}", [P, 512]) for i in L]
        s_const, s_turned, s_col, s_back, s_frow = (sem(n) for n in (
            "const", "logits_turned", "column_ready", "factors_turned", "factor_row_ready"))
        col = [sb(f"col{i}", [P, NT]) for i in L]
        before = sb("before", [P, P])
        scratch = sb("scratch", [P, N])
        tie = sb("tie", [P, P])
        counts = [sb(f"counts{i}", [P, NT, 3]) for i in L]
        rank = [sb(f"rank{i}", [P, NT]) for i in L]
        factor = [sb(f"factor{i}", [P, NT]) for i in L]
        spread = [sb(f"spread{i}", [P, N]) for i in L]
        base = [[sb(f"base{i}{k}", [P, N]) for k in range(KC)] for i in L]
        delta = [[sb(f"delta{i}{k}", [P, N]) for k in range(KC)] for i in L]
        s_tri, s_before, s_zero, s_step = sem("tri"), sem("before_ready"), sem("counts_zeroed"), sem("step")
        s_ld, s_in = [sem(f"loaded{i}") for i in L], [sem(f"tokens_loaded{i}") for i in L]
        s_rank, s_factor = sem("rank_ready"), sem("factor_ready")
        s_kept = [sem(f"factor_stored{i}") for i in L]
        s_spread = [sem(f"factor_spread{i}") for i in L]
        s_scaled, s_done = ([sem(f"{n}{i}") for i in L] for n in ("scaled", "merged"))
        s_out = sem("stored")

        def merge(eng, i):
            eng.wait_ge(s_in[i], 2 * KC * 16)
            eng.wait_ge(s_spread[i], 16)
            for k in range(KC):
                eng.tensor_tensor(delta[i][k][:], delta[i][k][:], spread[i][:], ALU.mult).then_inc(s_scaled[i], 1)
                eng.wait_ge(s_scaled[i], k + 1)
                eng.tensor_tensor(base[i][k][:], base[i][k][:], delta[i][k][:], ALU.add).then_inc(s_done[i], 1)

        with nc.Block() as block:
            @block.sync
            def _(sp):
                sp.dma_start(ident_sb[:], ident).then_inc(s_const, 16)
                for i in L:
                    sp.dma_start(row[i][:], logits[i].partition_broadcast(P)).then_inc(s_ld[i], 16)
                    sp.dma_start(by_tile[i][:], logits[i].rearrange("(t p) -> t p", p=P)).then_inc(s_ld[i], 16)
                for i in L:
                    for k in range(KC):
                        sp.dma_start(base[i][k][:], base_t[i, k * P:(k + 1) * P, :]).then_inc(s_in[i], 16)
                        sp.dma_start(delta[i][k][:], delta_t[i, k * P:(k + 1) * P, :]).then_inc(s_in[i], 16)
                for i in L:
                    sp.wait_ge(s_frow, i + 1)
                    sp.dma_start(factors[i].rearrange("(t p) -> t p", p=P), factor_row[i][:]).then_inc(s_kept[i], 16)
                    sp.wait_ge(s_kept[i], 16)
                    sp.dma_start(spread[i][:], factors[i].partition_broadcast(P)).then_inc(s_spread[i], 16)
                    for k in range(KC):
                        sp.wait_ge(s_done[i], k + 1)
                        sp.dma_start(out[i, k * P:(k + 1) * P, :], base[i][k][:]).then_inc(s_out, 16)
                sp.wait_ge(s_out, B * KC * 16)

            @block.tensor
            def _(pe):
                pe.wait_ge(s_const, 16)
                for i in L:
                    pe.wait_ge(s_ld[i], 32)
                    pe.transpose(turn[i][:, 0:NT], by_tile[i][:], ident_sb[0:NT, 0:NT]).then_inc(s_turned, 1)
                for i in L:
                    pe.wait_ge(s_factor, i + 1)
                    pe.transpose(turn[i][0:NT, 128:128 + P], factor[i][:], ident_sb[:]).then_inc(s_back, 1)

            @block.scalar
            def _(act):
                for i in L:
                    act.wait_ge(s_turned, i + 1)
                    act.activation(col[i][:], turn[i][:, 0:NT], ACT.Copy).then_inc(s_col, 1)
                for i in L:
                    act.wait_ge(s_back, i + 1)
                    act.activation(factor_row[i][:], turn[i][0:NT, 128:128 + P], ACT.Copy).then_inc(s_frow, 1)

            @block.gpsimd
            def _(pool):
                pool.memset(before[:], 1.0).then_inc(s_tri, 1)
                pool.wait_ge(s_tri, 1)
                pool.affine_select(out=before[:], in_=before[:], compare_op=ALU.is_gt, fill=0.0, base=0,
                                   pattern=[[-1, P]], channel_multiplier=1).then_inc(s_before, 1)
                for i in range(B - 1):
                    merge(pool, i)

            @block.vector
            def _(dve):
                for i in L:
                    dve.memset(counts[i][:], 0.0).then_inc(s_zero, 1)
                dve.wait_ge(s_zero, B)
                dve.wait_ge(s_before, 1)
                step = Chain(dve, s_step)
                for i in L:
                    dve.wait_ge(s_ld[i], 32)
                    dve.wait_ge(s_col, i + 1)
                    for t in range(NT):
                        me = col[i][:, t:t + 1]
                        here = slice(t * P, (t + 1) * P)
                        if t > 0:
                            step.link(dve.tensor_scalar(scratch[:, 0:t * P], row[i][:, 0:t * P], me, 0.0,
                                                        ALU.is_ge, ALU.add, accum_out=counts[i][:, t, 0:1]))
                        if t < NT - 1:
                            step.link(dve.tensor_scalar(scratch[:, (t + 1) * P:N], row[i][:, (t + 1) * P:N], me, 0.0,
                                                        ALU.is_gt, ALU.add, accum_out=counts[i][:, t, 1:2]))
                        step.link(dve.scalar_tensor_tensor(out=tie[:], in0=row[i][:, here], scalar=me,
                                                           in1=before[:], op0=ALU.is_equal, op1=ALU.mult))
                        step.link(dve.scalar_tensor_tensor(out=scratch[:, here], in0=row[i][:, here], scalar=me,
                                                           in1=tie[:], op0=ALU.is_gt, op1=ALU.add,
                                                           accum_out=counts[i][:, t, 2:3]))
                    dve.tensor_reduce(rank[i][:], counts[i][:], AX.X, ALU.add).then_inc(s_rank, 1)
                    dve.wait_ge(s_rank, i + 1)
                    dve.scalar_tensor_tensor(out=factor[i][:], in0=rank[i][:], scalar=float(KEPT), in1=col[i][:],
                                             op0=ALU.is_lt, op1=ALU.mult).then_inc(s_factor, 1)
                merge(dve, B - 1)


def build(nc, a, out):
    qk_hi = nc.dram_tensor("qk_hi", (B, 4 * C, N), F32).ap()
    qk_lo = nc.dram_tensor("qk_lo", (B, 4 * C, N), F32).ap()
    v_rows = nc.dram_tensor("v_rows", (B * N, 2 * C), F32).ap()
    norm_and_project(nc, a["x"], a["wqk"], a["wv"], a["gmat"], qk_hi, qk_lo, v_rows)
    o_rows = nc.dram_tensor("o_rows", (VD, 1 + B * H0, N), F32).ap()
    differential_attention(nc, qk_hi, qk_lo, v_rows, [a[f"lambda_{n}"] for n in ("q1", "k1", "q2", "k2")],
                           a["ident"], a["fold"], o_rows)
    t_t = nc.dram_tensor("t_t", (B, C, N), F32).ap()
    a_t = nc.dram_tensor("a_t", (B, C, N), F32).ap()
    qk1_hi = nc.dram_tensor("qk1_hi", (B, 2 * C, N), F32).ap()
    qk1_lo = nc.dram_tensor("qk1_lo", (B, 2 * C, N), F32).ap()
    v1_rows = nc.dram_tensor("v1_rows", (B, N, C), F32).ap()
    head_norm_and_layer1_inputs(nc, a, o_rows, t_t, a_t, qk1_hi, qk1_lo, v1_rows)
    o1_t = nc.dram_tensor("o1_t", (B, C, N), F32).ap()
    causal_attention(nc, qk1_hi, qk1_lo, v1_rows, a["ident"], o1_t)
    t2_t = nc.dram_tensor("t2_t", (B, C, N), F32).ap()
    recurrence_gate_and_ffn(nc, a, o1_t, a_t, t_t, t2_t)
    logits = nc.dram_tensor("logits", (B, N), F32).ap()
    factors = nc.dram_tensor("factors", (B, N), F32).ap()
    base_t = nc.dram_tensor("base_t", (B, C, N), F32).ap()
    delta_t = nc.dram_tensor("delta_t", (B, C, N), F32).ap()
    routed_ffn(nc, a, t2_t, logits, base_t, delta_t)
    select_and_merge(nc, logits, factors, a["ident"], base_t, delta_t, out)


def layout(inputs):
    import numpy as np

    def tiles(w):
        w = np.asarray(w)
        return np.ascontiguousarray(w.reshape(-1, P, w.shape[1]).transpose(1, 0, 2))

    def columns(v):
        return np.ascontiguousarray(np.asarray(v).reshape(-1, P).T)

    a = {}
    a["x"] = np.ascontiguousarray(np.asarray(inputs["x"]).reshape(B, C, N))
    q_w, k_w, v_w = (np.asarray(inputs[f"L0_conv_{n}_w"]) for n in "qkv")
    a["wqk"] = tiles(np.concatenate([q_w, k_w]).T)
    a["wv"] = tiles(v_w.T)
    for n in ("q1", "k1", "q2", "k2"):
        a[f"lambda_{n}"] = np.ascontiguousarray(inputs[f"L0_conv_lambda_{n}"])
    a["ident"] = np.eye(P, dtype=np.float32)
    a["fold"] = np.concatenate([np.eye(VD, dtype=np.float32)] * 2)
    f = {k: np.asarray(v) for k, v in inputs.items()}
    a["out_w"] = tiles(f["L0_conv_out_w"].T)
    a["rms_scale"] = np.tile(f["L0_conv_rms_scale"].reshape(VD, 1), (2, 1))
    a["wqk1"] = tiles(f["L1_attn_qkv_w"][:, 0:2 * C])
    a["wv1"] = tiles(f["L1_attn_qkv_w"][:, 2 * C:])
    a["qk_bias1"] = np.ascontiguousarray(f["L1_attn_qkv_b"][0:2 * C].reshape(-1, P).T)
    a["v_bias1"] = np.ascontiguousarray(f["L1_attn_qkv_b"][2 * C:])
    of_head = (np.arange(2 * C)[:, None] // VD == np.arange(H0)[None, :]).astype(np.float32)
    a["to_heads"] = tiles(of_head / np.float32(VD))
    a["from_heads"] = np.ascontiguousarray(of_head.reshape(-1, P, H0).transpose(2, 0, 1))
    a["mean_mat"] = np.full((P, P), 1.0 / C, np.float32)
    for n in ("o_w", "rq_w", "rk_w", "rv_w", "ro_w", "cg_w", "ffn_w1", "ffn_w2"):
        a[n] = tiles(f[f"L1_attn_{n}"])
    for n in ("o_b", "rq_b", "rk_b", "ro_b", "cg_b", "ffn_b1", "ffn_b2", "ln1_g", "ln1_b", "ln2_g", "ln2_b",
              "ln3_g", "ln3_b"):
        a[n] = columns(f[f"L1_attn_{n}"])
    a["rv_b"] = f["L1_attn_rv_b"]
    for n in ("w1", "w2", "wr"):
        a[n] = tiles(f[f"L1_ffn_{n}"])
    a["wr"] = a["wr"].reshape(P, KC)
    a["br"] = f["L1_ffn_br"].reshape(1, 1)
    a["b1"], a["b2"] = columns(f["L1_ffn_b1"]), columns(f["L1_ffn_b2"])
    group = np.arange(P) // 8
    a["gmat"] = (group[:, None] == group[None, :]).astype(np.float32) / np.float32(8)
    return a


def kernel(**inputs):
    import numpy as np
    import concourse.bacc as bacc
    from concourse import mybir as mb
    from concourse.bass_utils import run_bass_kernel_spmd as run

    nc = bacc.Bacc("TRN2", target_bir_lowering=False, num_devices=1)
    arrays, a = {}, {}
    for name, value in layout(inputs).items():
        arrays[f"in_{name}"] = value
        a[name] = nc.dram_tensor(f"in_{name}", value.shape, mb.dt.from_np(value.dtype), kind="ExternalInput").ap()
    out = nc.dram_tensor("out", (B, C, N), F32, kind="ExternalOutput").ap()
    build(nc, a, out)
    r = run(nc, [arrays], core_ids=[0])
    return r.results[0]["out"].reshape(B, C, 48, 48)
```
